# Optimizing a Trainium2 kernel written in Bass

```python
import numpy as np
import jax
import jax.numpy as jnp

def _softmax(x, axis=-1):
    return jax.nn.softmax(x, axis=axis)

def _gelu(x):
    return jax.nn.gelu(x, approximate=True)

def _silu(x):
    return jax.nn.silu(x)

def _sigmoid(x):
    return jax.nn.sigmoid(x)

def _layernorm(x, axis=-1, eps=1e-05):
    m = jnp.mean(x, axis=axis, keepdims=True)
    v = jnp.var(x, axis=axis, keepdims=True)
    return (x - m) / jnp.sqrt(v + eps)

def _scatter_add(tgt, idx, src, axis=0):
    return tgt.at[idx].add(src)

def _segment_sum(src, seg, n):
    return jax.ops.segment_sum(src, seg, n)
kernel_name = 'mk_vit_tower_d2_tok_img768_r4_2e70a5'

def setup_inputs(seed: int=0):
    np.random.seed(seed)
    _w = jnp.asarray

    def _rec_inputs():
        import jax
        import jax.numpy as jnp
        _rk = jax.random.key(seed)
        x = -0.000125008 + 0.999885 * jax.random.normal(jax.random.fold_in(_rk, 1), (64, 1, 224, 224), jnp.float32)
        return x
    x = _rec_inputs()

    def _L0_tok_setup():
        import jax, jax.numpy as jnp
        import numpy as np
        PATCH = 16
        LATENT = 192

        def _extract_patches(x, p):
            B, C, H, W_ = x.shape
            nh, nw = (H // p, W_ // p)
            patches = x.reshape(B, C, nh, p, nw, p).transpose(0, 1, 2, 4, 3, 5)
            return patches.reshape(B, nh * nw, C * p * p)
        key = jax.random.key(seed)
        k1, k2 = jax.random.split(key)
        x = jax.random.normal(k1, (32, 1, 256, 256), dtype=jnp.float32)
        W = jax.random.normal(k2, (LATENT, PATCH * PATCH), dtype=jnp.float32) * 0.02
        return {'x': x, 'W': W}
    _L0_tok_all = _L0_tok_setup()
    _L0_tok_in = {k: v for k, v in _L0_tok_all.items() if k in ('W',)}
    del _L0_tok_all

    def _L0_attn_setup():
        import jax, jax.numpy as jnp
        import numpy as np
        DIM = 192
        H = 12
        HD = DIM // H
        TTT_BASE_LR = 1.0
        EPS = 1e-06

        def ln_fwd(x, gamma, beta):
            mu = jnp.mean(x, axis=-1, keepdims=True)
            var = jnp.mean((x - mu) ** 2, axis=-1, keepdims=True)
            x_hat = (x - mu) / jnp.sqrt(var + EPS)
            return gamma * x_hat + beta

        def ln_fused_l2_bwd(x, l2_target, gamma, beta):
            D = x.shape[-1]
            mu = jnp.mean(x, axis=-1, keepdims=True)
            var = jnp.mean((x - mu) ** 2, axis=-1, keepdims=True)
            std = jnp.sqrt(var + EPS)
            x_hat = (x - mu) / std
            y = gamma * x_hat + beta
            grad_out = y - l2_target
            g = grad_out * gamma
            z = (D * g - jnp.sum(g, -1, keepdims=True) - x_hat * jnp.sum(g * x_hat, -1, keepdims=True)) / (D * std)
            return z
        key = jax.random.key(seed)
        ks = jax.random.split(key, 10)
        B, N, C = (16, 256, DIM)
        return {'x': jax.random.normal(ks[0], (B, N, C), jnp.float32), 'qkv_weight': jax.random.normal(ks[1], (3 * C, C), jnp.float32) * 0.02, 'q_bias': jnp.zeros((C,), jnp.float32), 'v_bias': jnp.zeros((C,), jnp.float32), 'proj_weight': jax.random.normal(ks[2], (C, C), jnp.float32) * 0.02, 'proj_bias': jnp.zeros((C,), jnp.float32), 'ttt_lr_weight': jax.random.normal(ks[3], (H, 1, C), jnp.float32) * 0.02, 'ttt_lr_bias': jnp.zeros((H, 1), jnp.float32), 'ttt_norm_weight': jnp.ones((H, HD), jnp.float32), 'ttt_norm_bias': jnp.zeros((H, HD), jnp.float32), 'W1': jax.random.normal(ks[4], (H, HD, HD), jnp.float32) * 0.02, 'b1': jnp.zeros((H, 1, HD), jnp.float32)}
    _L0_attn_all = _L0_attn_setup()
    _L0_attn_in = {k: v for k, v in _L0_attn_all.items() if k in ('qkv_weight', 'q_bias', 'v_bias', 'proj_weight', 'proj_bias', 'ttt_lr_weight', 'ttt_lr_bias', 'ttt_norm_weight', 'ttt_norm_bias', 'W1', 'b1')}
    del _L0_attn_all

    def _L0_ffn_setup():
        import jax, jax.numpy as jnp
        import numpy as np
        DIM = 192
        HIDDEN = 192
        NUM_EXPERTS = 4
        B, S = (16, 512)
        key = jax.random.key(seed)
        ks = jax.random.split(key, 7)
        sd = 1.0 / np.sqrt(DIM)
        sh = 1.0 / np.sqrt(HIDDEN)
        return {'x': jax.random.normal(ks[0], (B, S, DIM), dtype=jnp.float32), 'router_w': jax.random.uniform(ks[1], (DIM, NUM_EXPERTS), jnp.float32, -sd, sd), 'router_b': jax.random.uniform(ks[2], (NUM_EXPERTS,), jnp.float32, -sd, sd), 'w1': jax.random.uniform(ks[3], (NUM_EXPERTS, DIM, HIDDEN), jnp.float32, -sd, sd), 'b1': jax.random.uniform(ks[4], (NUM_EXPERTS, HIDDEN), jnp.float32, -sd, sd), 'w2': jax.random.uniform(ks[5], (NUM_EXPERTS, HIDDEN, DIM), jnp.float32, -sd, sd), 'b2': jax.random.uniform(ks[6], (NUM_EXPERTS, DIM), jnp.float32, -sd, sd)}
    _L0_ffn_all = _L0_ffn_setup()
    _L0_ffn_in = {k: v for k, v in _L0_ffn_all.items() if k in ('router_w', 'router_b', 'w1', 'b1', 'w2', 'b2')}
    del _L0_ffn_all

    def _L1_attn_setup():
        import jax, jax.numpy as jnp
        import numpy as np
        N_HEAD = 12
        N_EMBD = 192
        BLOCK = 512
        THETA = 10000.0

        def _rope_tables(head_dim, end, theta=THETA):
            half = head_dim // 2
            freqs = 1.0 / theta ** (jnp.arange(0, head_dim, 2, dtype=jnp.float32) / head_dim)
            t = jnp.arange(end, dtype=jnp.float32)
            ang = jnp.outer(t, freqs)
            return (jnp.cos(ang), jnp.sin(ang))

        def _apply_rope(x, cos, sin):
            B, H, T, hd = x.shape
            xr = x.reshape(B, H, T, hd // 2, 2)
            x0, x1 = (xr[..., 0], xr[..., 1])
            c = cos[None, None, :T, :]
            s = sin[None, None, :T, :]
            o0 = x0 * c - x1 * s
            o1 = x0 * s + x1 * c
            return jnp.stack([o0, o1], axis=-1).reshape(B, H, T, hd)
        key = jax.random.key(seed)
        ks = jax.random.split(key, 9)
        B, T, C = (2, 512, N_EMBD)
        std = 0.02
        return {'x': jax.random.normal(ks[0], (B, T, C), jnp.float32), 'norm_scale': jnp.ones((C,), jnp.float32), 'norm_bias': jnp.zeros((C,), jnp.float32), 'W_attn': jax.random.normal(ks[1], (C, 3 * C), jnp.float32) * std, 'b_attn': jax.random.normal(ks[2], (3 * C,), jnp.float32) * std, 'W_proj': jax.random.normal(ks[3], (C, C), jnp.float32) * std, 'b_proj': jax.random.normal(ks[4], (C,), jnp.float32) * std, 'sinks': jax.random.normal(ks[5], (N_HEAD,), jnp.float32) * 0.5, 'rezero': jax.random.normal(ks[6], (1,), jnp.float32) * 0.1}
    _L1_attn_all = _L1_attn_setup()
    _L1_attn_in = {k: v for k, v in _L1_attn_all.items() if k in ('norm_scale', 'norm_bias', 'W_attn', 'b_attn', 'W_proj', 'b_proj', 'sinks', 'rezero')}
    del _L1_attn_all

    def _L1_ffn_setup():
        import jax, jax.numpy as jnp
        import numpy as np
        EPS_NORM = 1e-06
        EPS_LN = 1e-05

        def _layernorm(x, g, b):
            mu = jnp.mean(x, axis=-1, keepdims=True)
            var = jnp.mean(jnp.square(x - mu), axis=-1, keepdims=True)
            return (x - mu) * jax.lax.rsqrt(var + EPS_LN) * g + b
        key = jax.random.key(seed)
        ks = jax.random.split(key, 6)
        b, m, d = (8, 256, 192)
        n, p = (64, 16)
        h = 2 * d
        x = jax.random.normal(ks[0], (b, m, d), dtype=jnp.float32)
        phi = jax.random.normal(ks[1], (n, p, d), dtype=jnp.float32)
        ln_g = jnp.ones((n, d), dtype=jnp.float32)
        ln_b = jnp.zeros((n, d), dtype=jnp.float32)
        w1 = jax.random.normal(ks[2], (n, d, h), dtype=jnp.float32) * (1.0 / np.sqrt(d))
        b1 = jax.random.normal(ks[3], (n, h), dtype=jnp.float32) * 0.01
        w2 = jax.random.normal(ks[4], (n, h, d), dtype=jnp.float32) * (1.0 / np.sqrt(h))
        b2 = jax.random.normal(ks[5], (n, d), dtype=jnp.float32) * 0.01
        return {'x': x, 'phi': phi, 'ln_g': ln_g, 'ln_b': ln_b, 'w1': w1, 'b1': b1, 'w2': w2, 'b2': b2}
    _L1_ffn_all = _L1_ffn_setup()
    _L1_ffn_in = {k: v for k, v in _L1_ffn_all.items() if k in ('phi', 'ln_g', 'ln_b', 'w1', 'b1', 'w2', 'b2')}
    del _L1_ffn_all
    return {'x': x, 'L0_tok_W': _L0_tok_in['W'], 'L0_attn_qkv_weight': _L0_attn_in['qkv_weight'], 'L0_attn_q_bias': _L0_attn_in['q_bias'], 'L0_attn_v_bias': _L0_attn_in['v_bias'], 'L0_attn_proj_weight': _L0_attn_in['proj_weight'], 'L0_attn_proj_bias': _L0_attn_in['proj_bias'], 'L0_attn_ttt_lr_weight': _L0_attn_in['ttt_lr_weight'], 'L0_attn_ttt_lr_bias': _L0_attn_in['ttt_lr_bias'], 'L0_attn_ttt_norm_weight': _L0_attn_in['ttt_norm_weight'], 'L0_attn_ttt_norm_bias': _L0_attn_in['ttt_norm_bias'], 'L0_attn_W1': _L0_attn_in['W1'], 'L0_attn_b1': _L0_attn_in['b1'], 'L0_ffn_router_w': _L0_ffn_in['router_w'], 'L0_ffn_router_b': _L0_ffn_in['router_b'], 'L0_ffn_w1': _L0_ffn_in['w1'], 'L0_ffn_b1': _L0_ffn_in['b1'], 'L0_ffn_w2': _L0_ffn_in['w2'], 'L0_ffn_b2': _L0_ffn_in['b2'], 'L1_attn_norm_scale': _L1_attn_in['norm_scale'], 'L1_attn_norm_bias': _L1_attn_in['norm_bias'], 'L1_attn_W_attn': _L1_attn_in['W_attn'], 'L1_attn_b_attn': _L1_attn_in['b_attn'], 'L1_attn_W_proj': _L1_attn_in['W_proj'], 'L1_attn_b_proj': _L1_attn_in['b_proj'], 'L1_attn_sinks': _L1_attn_in['sinks'], 'L1_attn_rezero': _L1_attn_in['rezero'], 'L1_ffn_phi': _L1_ffn_in['phi'], 'L1_ffn_ln_g': _L1_ffn_in['ln_g'], 'L1_ffn_ln_b': _L1_ffn_in['ln_b'], 'L1_ffn_w1': _L1_ffn_in['w1'], 'L1_ffn_b1': _L1_ffn_in['b1'], 'L1_ffn_w2': _L1_ffn_in['w2'], 'L1_ffn_b2': _L1_ffn_in['b2']}

def reference(x, L0_tok_W, L0_attn_qkv_weight, L0_attn_q_bias, L0_attn_v_bias, L0_attn_proj_weight, L0_attn_proj_bias, L0_attn_ttt_lr_weight, L0_attn_ttt_lr_bias, L0_attn_ttt_norm_weight, L0_attn_ttt_norm_bias, L0_attn_W1, L0_attn_b1, L0_ffn_router_w, L0_ffn_router_b, L0_ffn_w1, L0_ffn_b1, L0_ffn_w2, L0_ffn_b2, L1_attn_norm_scale, L1_attn_norm_bias, L1_attn_W_attn, L1_attn_b_attn, L1_attn_W_proj, L1_attn_b_proj, L1_attn_sinks, L1_attn_rezero, L1_ffn_phi, L1_ffn_ln_g, L1_ffn_ln_b, L1_ffn_w1, L1_ffn_b1, L1_ffn_w2, L1_ffn_b2):
    import jax
    import jax.numpy as jnp

    def _L0_tok_ref(x, W):
        import jax, jax.numpy as jnp
        import numpy as np
        PATCH = 16
        LATENT = 192

        def _extract_patches(x, p):
            B, C, H, W_ = x.shape
            nh, nw = (H // p, W_ // p)
            patches = x.reshape(B, C, nh, p, nw, p).transpose(0, 1, 2, 4, 3, 5)
            return patches.reshape(B, nh * nw, C * p * p)
        patches = _extract_patches(x, PATCH)
        return jnp.einsum('bnk,ok->bno', patches, W)

    def _L0_attn_ref(x, qkv_weight, q_bias, v_bias, proj_weight, proj_bias, ttt_lr_weight, ttt_lr_bias, ttt_norm_weight, ttt_norm_bias, W1, b1):
        import jax, jax.numpy as jnp
        import numpy as np
        DIM = 192
        H = 12
        HD = DIM // H
        TTT_BASE_LR = 1.0
        EPS = 1e-06

        def ln_fwd(x, gamma, beta):
            mu = jnp.mean(x, axis=-1, keepdims=True)
            var = jnp.mean((x - mu) ** 2, axis=-1, keepdims=True)
            x_hat = (x - mu) / jnp.sqrt(var + EPS)
            return gamma * x_hat + beta

        def ln_fused_l2_bwd(x, l2_target, gamma, beta):
            D = x.shape[-1]
            mu = jnp.mean(x, axis=-1, keepdims=True)
            var = jnp.mean((x - mu) ** 2, axis=-1, keepdims=True)
            std = jnp.sqrt(var + EPS)
            x_hat = (x - mu) / std
            y = gamma * x_hat + beta
            grad_out = y - l2_target
            g = grad_out * gamma
            z = (D * g - jnp.sum(g, -1, keepdims=True) - x_hat * jnp.sum(g * x_hat, -1, keepdims=True)) / (D * std)
            return z
        B, N, C = x.shape
        num_mini_batch = 1
        m = N // num_mini_batch
        qkv_bias = jnp.concatenate([q_bias, jnp.zeros_like(q_bias), v_bias])
        qkv = x @ qkv_weight.T + qkv_bias
        qkv = qkv.reshape(B, N, 3, H, HD).transpose(2, 0, 3, 1, 4)
        q, k, v = (qkv[0], qkv[1], qkv[2])
        ttt_lr = jnp.einsum('bnc,hdc->bhnd', x, ttt_lr_weight) + ttt_lr_bias.reshape(1, H, 1, 1)
        ttt_lr_eta = TTT_BASE_LR * jax.nn.sigmoid(ttt_lr) / HD
        gamma = ttt_norm_weight.reshape(H, 1, HD)
        beta = ttt_norm_bias.reshape(H, 1, HD)

        def compute_mini_batch(carry, inp):
            W1c, b1c = carry
            XQ, XK, XV, eta = inp
            Z1 = XK @ W1c + b1c
            g = ln_fused_l2_bwd(Z1, XV - XK, gamma, beta)
            g = g * eta / m
            grad_W1 = jnp.einsum('bhmd,bhme->bhde', XK, g)
            grad_b1 = jnp.sum(g, axis=2, keepdims=True)
            W1n = W1c - grad_W1
            b1n = b1c - grad_b1
            Z1_bar = ln_fwd(XQ @ W1n + b1n, gamma, beta)
            return ((W1n, b1n), XQ + Z1_bar)

        def to_scan(t):
            return t.reshape(B, H, num_mini_batch, m, t.shape[-1]).transpose(2, 0, 1, 3, 4)
        xs = (to_scan(q), to_scan(k), to_scan(v), to_scan(ttt_lr_eta))
        init = (jnp.broadcast_to(W1, (B, H, HD, HD)), jnp.broadcast_to(b1, (B, H, 1, HD)))
        _, XQW = jax.lax.scan(compute_mini_batch, init, xs)
        out = XQW.transpose(1, 2, 0, 3, 4).reshape(B, H, N, HD)
        out = out.transpose(0, 2, 1, 3).reshape(B, N, C)
        out = out @ proj_weight.T + proj_bias
        return out

    def _L0_ffn_ref(x, router_w, router_b, w1, b1, w2, b2):
        import jax, jax.numpy as jnp
        import numpy as np
        DIM = 192
        HIDDEN = 192
        NUM_EXPERTS = 4
        B, S = (16, 512)
        logits = jnp.einsum('bsd,de->bse', x, router_w) + router_b
        probs = jax.nn.softmax(logits, axis=-1)
        idx = jnp.argmax(probs, axis=-1)
        dispatch = jax.nn.one_hot(idx, NUM_EXPERTS, dtype=x.dtype)
        h = jnp.einsum('bsd,edh->besh', x, w1) + b1[None, :, None, :]
        h = jax.nn.gelu(h, approximate=False)
        y = jnp.einsum('besh,ehd->besd', h, w2) + b2[None, :, None, :]
        out = jnp.einsum('besd,bse->bsd', y, dispatch)
        out = out + x
        return out

    def _L1_attn_ref(x, norm_scale, norm_bias, W_attn, b_attn, W_proj, b_proj, sinks, rezero):
        import jax, jax.numpy as jnp
        import numpy as np
        N_HEAD = 12
        N_EMBD = 192
        BLOCK = 512
        THETA = 10000.0

        def _rope_tables(head_dim, end, theta=THETA):
            half = head_dim // 2
            freqs = 1.0 / theta ** (jnp.arange(0, head_dim, 2, dtype=jnp.float32) / head_dim)
            t = jnp.arange(end, dtype=jnp.float32)
            ang = jnp.outer(t, freqs)
            return (jnp.cos(ang), jnp.sin(ang))

        def _apply_rope(x, cos, sin):
            B, H, T, hd = x.shape
            xr = x.reshape(B, H, T, hd // 2, 2)
            x0, x1 = (xr[..., 0], xr[..., 1])
            c = cos[None, None, :T, :]
            s = sin[None, None, :T, :]
            o0 = x0 * c - x1 * s
            o1 = x0 * s + x1 * c
            return jnp.stack([o0, o1], axis=-1).reshape(B, H, T, hd)
        B, T, C = x.shape
        H = N_HEAD
        hd = C // H
        xn = norm_scale * x + norm_bias
        qkv = xn @ W_attn + b_attn
        q, k, v = jnp.split(qkv, 3, axis=-1)
        q = q.reshape(B, T, H, hd).transpose(0, 2, 1, 3)
        k = k.reshape(B, T, H, hd).transpose(0, 2, 1, 3)
        v = v.reshape(B, T, H, hd).transpose(0, 2, 1, 3)
        cos, sin = _rope_tables(hd, T)
        q = _apply_rope(q, cos, sin)
        k = _apply_rope(k, cos, sin)
        scale = 1.0 / jnp.sqrt(jnp.float32(hd))
        att = jnp.einsum('bhqd,bhkd->bhqk', q, k) * scale
        causal = jnp.tril(jnp.ones((T, T), dtype=bool))
        att = jnp.where(causal[None, None], att, -jnp.inf)
        sink_col = jnp.broadcast_to(sinks.reshape(1, H, 1, 1), (B, H, T, 1))
        att = jnp.concatenate([sink_col, att], axis=-1)
        att = jax.nn.softmax(att, axis=-1)[..., 1:]
        y = jnp.einsum('bhqk,bhkd->bhqd', att, v)
        y = y.transpose(0, 2, 1, 3).reshape(B, T, C)
        y = (y @ W_proj + b_proj) * rezero
        return y

    def _L1_ffn_ref(x, phi, ln_g, ln_b, w1, b1, w2, b2):
        import jax, jax.numpy as jnp
        import numpy as np
        EPS_NORM = 1e-06
        EPS_LN = 1e-05

        def _layernorm(x, g, b):
            mu = jnp.mean(x, axis=-1, keepdims=True)
            var = jnp.mean(jnp.square(x - mu), axis=-1, keepdims=True)
            return (x - mu) * jax.lax.rsqrt(var + EPS_LN) * g + b
        phi_n = phi * jax.lax.rsqrt(jnp.sum(jnp.square(phi), axis=0, keepdims=True) + EPS_NORM)
        bsz, m, d = x.shape
        n, p, _ = phi_n.shape
        logits = jnp.einsum('bmd,npd->bmnp', x, phi_n)
        D = jax.nn.softmax(logits, axis=1)
        C = jax.nn.softmax(logits.reshape(bsz, m, n * p), axis=-1)
        Xs = jnp.einsum('bmd,bmnp->bnpd', x, D)
        hdn = _layernorm(Xs, ln_g[:, None, :], ln_b[:, None, :])
        hdn = jnp.einsum('bnpd,ndh->bnph', hdn, w1) + b1[:, None, :]
        hdn = jax.nn.gelu(hdn, approximate=False)
        Ys = jnp.einsum('bnph,nhd->bnpd', hdn, w2) + b2[:, None, :]
        Ys = Ys.reshape(bsz, n * p, d)
        Y = jnp.einsum('bsd,bms->bmd', Ys, C)
        return Y
    h = _L0_tok_ref(x, L0_tok_W)
    h = h + _L0_attn_ref(_layernorm(h, axis=-1), L0_attn_qkv_weight, L0_attn_q_bias, L0_attn_v_bias, L0_attn_proj_weight, L0_attn_proj_bias, L0_attn_ttt_lr_weight, L0_attn_ttt_lr_bias, L0_attn_ttt_norm_weight, L0_attn_ttt_norm_bias, L0_attn_W1, L0_attn_b1)
    h = h + _L0_ffn_ref(_layernorm(h, axis=-1), L0_ffn_router_w, L0_ffn_router_b, L0_ffn_w1, L0_ffn_b1, L0_ffn_w2, L0_ffn_b2)
    h = h + _L1_attn_ref(_layernorm(h, axis=-1), L1_attn_norm_scale, L1_attn_norm_bias, L1_attn_W_attn, L1_attn_b_attn, L1_attn_W_proj, L1_attn_b_proj, L1_attn_sinks, L1_attn_rezero)
    h = h + _L1_ffn_ref(_layernorm(h, axis=-1), L1_ffn_phi, L1_ffn_ln_g, L1_ffn_ln_b, L1_ffn_w1, L1_ffn_b1, L1_ffn_w2, L1_ffn_b2)
    return h

_drawn_inputs = setup_inputs


def setup_inputs(seed=0):
    import zlib

    import numpy as np

    out = dict(_drawn_inputs(seed))
    spreads = {'L0_attn_q_bias': (0.0, 0.1),
     'L0_attn_v_bias': (0.0, 0.1),
     'L0_attn_proj_bias': (0.0, 0.1),
     'L0_attn_ttt_lr_bias': (0.0, 0.49),
     'L0_attn_ttt_norm_weight': (1.0, 0.2),
     'L0_attn_ttt_norm_bias': (0.0, 0.1),
     'L0_attn_b1': (0.0, 0.1),
     'L1_attn_norm_scale': (1.0, 0.6),
     'L1_attn_norm_bias': (0.0, 0.8),
     'L1_ffn_ln_g': (1.0, 0.6),
     'L1_ffn_ln_b': (0.0, 0.8)}
    factors = {'L0_attn_ttt_lr_weight': 3.777,
     'L0_ffn_b1': 5.76,
     'L1_attn_W_attn': 8.0,
     'L1_attn_b_attn': 8.0,
     'L1_attn_W_proj': 8.0,
     'L1_attn_b_proj': 43.633,
     'L1_attn_sinks': 23.8,
     'L1_ffn_b1': 64.0,
     'L1_ffn_b2': 58.396}
    for name, (base, spread) in spreads.items():
        noise = np.random.default_rng([zlib.crc32(name.encode()), seed]).standard_normal(out[name].shape)
        drawn = base * np.exp(spread * noise) if base else spread * noise
        out[name] = jnp.asarray(drawn.astype(out[name].dtype))
    for name, factor in factors.items():
        out[name] = (out[name] * factor).astype(out[name].dtype)
    return out
```

```python
from contextlib import ExitStack

import numpy as np

import concourse.bass as bass
from concourse import mybir

ALU = mybir.AluOpType
ACT = mybir.ActivationFunctionType
AX_X = mybir.AxisListType.X
F32 = mybir.dt.float32
BF16 = mybir.dt.bfloat16

IMAGES = 64
SIDE, PATCH = 224, 16
GRID = SIDE // PATCH
TOKENS = GRID * GRID
TT = 2
TP = TOKENS // TT
D = 192
DC = 2
DP = D // DC
HEADS, HD = 12, 16
PAIRS = IMAGES // 2
LN_EPS = 1e-5
TTT_EPS = 1e-6


class Steps:

    def __init__(self, eng, sem, before):
        self.eng, self.sem, self.before, self.n = eng, sem, before, 0

    def done(self, ins):
        ins.then_inc(self.sem, 1)
        self.n += 1

    def settle(self):
        self.eng.wait_ge(self.sem, self.before + self.n)


class Stage:

    def __init__(self, nc, ctx, name):
        self.nc, self.ctx, self.name = nc, ctx, name

    def sb(self, name, shape, dt=F32):
        return self.ctx.enter_context(self.nc.sbuf_tensor(f"{self.name}_{name}", shape, dt))

    def psum_banks(self, n=8):
        return [self.ctx.enter_context(self.nc.psum_tensor(f"{self.name}_bank{i}", [128, 512], F32)) for i in range(n)]

    def sem(self, name):
        return self.nc.alloc_semaphore(f"{self.name}_{name}")


def tiles(bank, rows, groups, width, pitch=None):
    pitch = pitch or width
    return bank[0:rows, 0:groups * pitch].rearrange("p (g w) -> p g w", g=groups)[:, :, 0:width]


def ttt_stage(nc, a, H, ident):
    TTT_STEPS_DVE = 28
    with ExitStack() as ctx:
        st = Stage(nc, ctx, "ttt")
        sb, sem = st.sb, st.sem
        banks = st.psum_banks()

        w_tok = sb("w_tok", [128, 2, D])
        w_in = sb("w_in", [DP + 1, DC, 3 * D + HEADS])
        w_qT = sb("w_qT", [DP + 1, DC, D])
        w_q = sb("w_q", [DP, DC, D + 1])
        w_k = sb("w_k", [DP, DC, D])
        w_kT = sb("w_kT", [DP + 1, DC, D])
        w_vT = sb("w_vT", [DP + 1, DC, D])
        w_pT = sb("w_pT", [DP, DC, D])
        w_pg = sb("w_pg", [DP, DC, D])
        w_qp = sb("w_qp", [DP + 1, DC, D])
        p_bias = sb("p_bias", [DP + 1, D])
        gamma_row = sb("gamma_row", [TP, D])
        gamma2 = sb("gamma2", [TP, D])
        gamma_col = sb("gamma_col", [DP, DC])
        beta_col = sb("beta_col", [DP, DC])
        q_col = sb("q_col", [DP, DC])
        w_1c = sb("w_1c", [DP + 1, DC, DP])
        head_mask = sb("head_mask", [DP + 1, D])
        sums = sb("sums", [DP + 1, HEADS])
        mhalf = sb("mhalf", [TP, 2 * HEADS])

        two = range(2)
        xp = [sb(f"xp{b}", [128, 2, TOKENS]) for b in two]
        xn = [sb(f"xn{b}", [TP, TT, D]) for b in two]
        xnT = [sb(f"xnT{b}", [DP + 1, DC, TOKENS]) for b in two]
        stats = [sb(f"stats{b}", [TP, TT, 6]) for b in two]
        mv = [sb(f"mv{b}", [TP, TT, 2]) for b in two]
        veps = [sb(f"veps{b}", [TP, TT]) for b in two]
        rstd = [sb(f"rstd{b}", [TP, TT]) for b in two]
        zt = [sb(f"zt{b}", [TP, TT, 2, D]) for b in two]
        k1 = [sb(f"k1{b}", [TP, TT, DC, DP + 1]) for b in two]
        qT = [sb(f"qT{b}", [DP + 1, DC, TOKENS]) for b in two]
        lr = [sb(f"lr{b}", [TP, TT, HEADS]) for b in two]
        coef = [sb(f"coef{b}", [TP, TT * HEADS]) for b in two]
        sq = [sb(f"sq{b}", [TP, TT, D]) for b in two]
        gvar = [sb(f"gvar{b}", [TP, TT * HEADS]) for b in two]
        grstd = [sb(f"grstd{b}", [TP, TT * HEADS]) for b in two]
        xh = [sb(f"xh{b}", [TP, TT, D]) for b in two]
        g = [sb(f"g{b}", [TP, TT, D]) for b in two]
        gx = [sb(f"gx{b}", [TP, TT, D]) for b in two]
        sgx = [sb(f"sgx{b}", [TP, TT * HEADS]) for b in two]
        gsum = [sb(f"gsum{b}", [DP + 1, HEADS]) for b in two]
        gc = [sb(f"gc{b}", [DP + 1, D]) for b in two]
        w_1n = [sb(f"w_1n{b}", [DP + 1, DC, DP]) for b in two]
        zb = [sb(f"zb{b}", [TP, TT, D]) for b in two]
        zbT = [sb(f"zbT{b}", [DP, DC, TOKENS]) for b in two]

        cleared = sem("cleared")
        weights_in = sem("weights_in")
        prep_dve = sem("prep_dve")
        prep_pe = sem("prep_pe")
        weights_ready = sem("weights_ready")
        x_in = [sem("x_in0"), sem("x_in1")]
        tok_done = sem("tok_done")
        h_kept = sem("h_kept")
        veps_done = sem("veps_done")
        rstd_done = sem("rstd_done")
        xn_done = sem("xn_done")
        xnT_psum = sem("xnT_psum")
        xnT_done = sem("xnT_done")
        proj_in_done = sem("proj_in_done")
        acts_in_done = sem("acts_in_done")
        sq_done = sem("sq_done")
        gvar_done = sem("gvar_done")
        grstd_done = sem("grstd_done")
        xh_done = sem("xh_done")
        g2x_done = sem("g2x_done")
        g_done = sem("g_done")
        gx_done = sem("gx_done")
        grad_in_done = sem("grad_in_done")
        grad_done = sem("grad_done")
        w1n_done = sem("w1n_done")
        zbar_psum = sem("zbar_psum")
        zbar_sq_done = sem("zbar_sq_done")
        zvar_done = sem("zvar_done")
        zrstd_done = sem("zrstd_done")
        zb_done = sem("zb_done")
        zbT_psum = sem("zbT_psum")
        zbT_done = sem("zbT_done")
        out_psum = sem("out_psum")
        h_added = sem("h_added")
        dve_steps = sem("dve_steps")
        act_steps = sem("act_steps")
        zbar_copied = sem("zbar_copied")

        WEIGHT_DMAS = 26 + HEADS
        block = ctx.enter_context(nc.Block())

        def grp(ap, n):
            return ap.rearrange("p t (h e) -> p (t h) e", e=HD) if n == 3 else ap.rearrange("p (h e) -> p h e", e=HD)

        @block.sync
        def _(sp):
            count = [0]

            def load(dst, src):
                sp.dma_start(dst, src).then_inc(weights_in, 16)
                count[0] += 1

            load(w_tok[:], a["tok_wT"])
            sp.dma_start(xp[0][:], a["patches"][0]).then_inc(x_in[0], 16)
            sp.dma_start(xp[1][:], a["patches"][1]).then_inc(x_in[1], 16)
            sp.wait_ge(cleared, 1)
            q_rows, k_rows = 0, 1
            load(w_in[0:DP, :, 2 * D:3 * D], a["qkv_T"][:, k_rows])
            load(w_in[0:DP, :, 3 * D:], a["lr_wT"])
            load(w_in[DP:DP + 1, 0, 3 * D:], a["lr_bias"])
            load(w_qT[0:DP], a["qkv_T"][:, q_rows])
            load(w_qT[DP:DP + 1, 0], a["q_bias"])
            load(w_q[:, :, 0:DP], a["qkv"][:, q_rows, :, 0:DP])
            load(w_q[:, :, DP + 1:], a["qkv"][:, q_rows, :, DP:])
            load(q_col[:], a["q_bias_col"])
            load(w_k[:], a["qkv"][:, k_rows])
            load(w_kT[0:DP], a["qkv_T"][:, k_rows])
            load(w_kT[DP:DP + 1, 0], a["ttt_beta"])
            load(w_kT[DP:DP + 1, 1], a["ttt_beta"])
            load(w_vT[0:DP], a["qkv_T"][:, 2])
            load(w_vT[DP:DP + 1, 0], a["v_bias"])
            load(w_vT[DP:DP + 1, 1], a["v_bias"])
            load(w_pT[:], a["proj_T"])
            load(p_bias[DP:DP + 1, :], a["proj_bias"])
            load(gamma_row[:], a["ttt_gamma"].partition_broadcast(TP).rearrange("p o d -> p (o d)"))
            load(gamma_col[:], a["ttt_gamma_col"])
            load(beta_col[:], a["ttt_beta_col"])
            for h in range(HEADS):
                c, r = h // 6, h % 6 * HD
                load(w_1c[r:r + HD, c, r:r + HD], a["W1"][h])
            load(w_1c[DP:DP + 1], a["b1"])
            load(head_mask[:, 0:DP], a["head_mask"])
            load(head_mask[:, DP:], a["head_mask"])
            load(ident[:], a["ident"])
            load(mhalf[:], a["mhalf"][0:TP, 0:2 * HEADS])
            assert count[0] == WEIGHT_DMAS, count
            with sp.Fori(0, PAIRS - 1) as i:
                for b in two:
                    sp.wait_ge(tok_done, i * 2 + (b + 1))
                    sp.dma_start(xp[b][:], a["patches"][i * 2 + (b + 2)]).then_inc(x_in[b], 16)

        @block.gpsimd
        def _(pool):
            pool.wait_ge(weights_ready, 1)
            with pool.Fori(0, PAIRS) as i:
                for b in two:
                    n1 = i * 2 + (b + 1)
                    pool.wait_ge(veps_done, n1)
                    nc.gpsimd.tensor_tensor(rstd[b][:], veps[b][:], mhalf[:, 0:TT], ALU.pow).then_inc(rstd_done, 1)
                for b in two:
                    n1 = i * 2 + (b + 1)
                    pool.wait_ge(gvar_done, n1)
                    nc.gpsimd.tensor_tensor(grstd[b][:], gvar[b][:], mhalf[:], ALU.pow).then_inc(grstd_done, 1)
                for b in two:
                    n1 = i * 2 + (b + 1)
                    pool.wait_ge(xh_done, n1)
                    nc.gpsimd.tensor_tensor(g[b][:, 0], xh[b][:, 0], gamma2[:], ALU.mult)
                    nc.gpsimd.tensor_tensor(g[b][:, 1], xh[b][:, 1], gamma2[:], ALU.mult).then_inc(g2x_done, 1)
                for b in two:
                    n1 = i * 2 + (b + 1)
                    pool.wait_ge(g_done, n1)
                    nc.gpsimd.tensor_tensor(gx[b][:], g[b][:], xh[b][:], ALU.mult).then_inc(gx_done, 1)
                for b in two:
                    n1 = i * 2 + (b + 1)
                    pool.wait_ge(zvar_done, n1)
                    nc.gpsimd.tensor_tensor(grstd[b][:], gvar[b][:], mhalf[:], ALU.pow).then_inc(zrstd_done, 1)

        @block.tensor
        def _(pe):
            pe.wait_ge(weights_in, 16 * WEIGHT_DMAS)
            pe.wait_ge(prep_dve, 1)
            for dc in range(DC):
                nc.tensor.matmul(banks[0][0:DP + 1, 0:D], w_q[:, dc, 0:DP + 1], w_pT[:, dc], start=dc == 0, stop=dc == 1)
            for dc in range(DC):
                mm = nc.tensor.matmul(banks[1][0:DP, 0:D], w_q[:, dc, DP + 1:], w_pT[:, dc], start=dc == 0, stop=dc == 1)
            mm.then_inc(prep_pe, 1)
            pe.wait_ge(prep_dve, 2)
            for ic in range(DC):
                for c in range(DC):
                    mm = nc.tensor.matmul(banks[2 + ic][0:DP, c * DP:(c + 1) * DP], w_k[:, c, ic * DP:(ic + 1) * DP],
                                          w_1c[0:DP, c], start=True, stop=True)
            mm.then_inc(prep_pe, 1)
            pe.wait_ge(weights_ready, 1)

            with pe.Fori(0, PAIRS) as i:
                def transposes(src, bank, b, signal):
                    for t in range(TT):
                        for c in range(DC):
                            mm = nc.tensor.transpose(bank[0:DP, c * TOKENS + t * TP:c * TOKENS + (t + 1) * TP],
                                                     src[b][:, t, c * DP:(c + 1) * DP], ident[0:TP, 0:TP])
                    mm.then_inc(signal, 1)

                for b in two:
                    pe.wait_ge(x_in[b], i * 16 + 16)
                    out = tiles(banks[4 * b], TP, TT, D)
                    for t in range(TT):
                        for c in range(2):
                            mm = nc.tensor.matmul(out[:, t], xp[b][:, c, t * TP:(t + 1) * TP], w_tok[:, c],
                                                  start=c == 0, stop=c == 1)
                    mm.then_inc(tok_done, 1)
                for b in two:
                    n1 = i * 2 + (b + 1)
                    pe.wait_ge(xn_done, n1)
                    transposes(xn, banks[4 * b + 1], b, xnT_psum)
                for b in two:
                    n1 = i * 2 + (b + 1)
                    pe.wait_ge(xnT_done, n1)
                    pe.wait_ge(h_added, n1)
                    for t in range(TT):
                        for c in range(DC):
                            K = DP + 1 - c
                            nc.tensor.matmul(banks[4 * b + 2 + t][0:TP, 0:2 * D], xnT[b][0:K, c, t * TP:(t + 1) * TP],
                                             w_in[0:K, c, 0:2 * D], start=c == 0, stop=c == 1)
                        for c in range(DC):
                            K = DP + 1 - c
                            nc.tensor.matmul(banks[4 * b][0:TP, t * (D + HEADS):(t + 1) * (D + HEADS)],
                                             xnT[b][0:K, c, t * TP:(t + 1) * TP], w_in[0:K, c, 2 * D:],
                                             start=c == 0, stop=c == 1)
                    for m in range(DC):
                        for c in range(DC):
                            K = DP + 1 - c
                            mm = nc.tensor.matmul(banks[4 * b + 1][0:DP, m * TOKENS:(m + 1) * TOKENS],
                                                  w_qT[0:K, c, m * DP:(m + 1) * DP], xnT[b][0:K, c],
                                                  start=c == 0, stop=c == 1)
                    mm.then_inc(proj_in_done, 1)
                for b in two:
                    n1 = i * 2 + (b + 1)
                    pe.wait_ge(grad_in_done, n1)
                    for c in range(DC):
                        for t in range(TT):
                            mm = nc.tensor.matmul(banks[4 * b][0:DP + 1, c * DP:(c + 1) * DP], k1[b][:, t, c],
                                                  g[b][:, t, c * DP:(c + 1) * DP], start=t == 0, stop=t == 1)
                    mm.then_inc(grad_done, 1)
                for b in two:
                    n1 = i * 2 + (b + 1)
                    pe.wait_ge(w1n_done, n1)
                    for t in range(TT):
                        for c in range(DC):
                            mm = nc.tensor.matmul(banks[4 * b + 1][0:TP, t * D + c * DP:t * D + (c + 1) * DP],
                                                  qT[b][:, c, t * TP:(t + 1) * TP], w_1n[b][:, c], start=True, stop=True)
                    mm.then_inc(zbar_psum, 1)
                for b in two:
                    n1 = i * 2 + (b + 1)
                    pe.wait_ge(zb_done, n1)
                    transposes(zb, banks[4 * b + 2], b, zbT_psum)
                for b in two:
                    n1 = i * 2 + (b + 1)
                    pe.wait_ge(zbT_done, n1)
                    for t in range(TT):
                        o = banks[4 * b + 3][0:TP, t * D:(t + 1) * D]
                        ts = slice(t * TP, (t + 1) * TP)
                        nc.tensor.matmul(o, xnT[b][0:DP + 1, 0, ts], w_qp[:, 0], start=True, stop=False)
                        nc.tensor.matmul(o, xnT[b][0:DP, 1, ts], w_qp[0:DP, 1], start=False, stop=False)
                        nc.tensor.matmul(o, zbT[b][:, 0, ts], w_pg[:, 0], start=False, stop=False)
                        mm = nc.tensor.matmul(o, zbT[b][:, 1, ts], w_pg[:, 1], start=False, stop=True)
                    mm.then_inc(out_psum, 1)

        @block.scalar
        def _(act):
            act.wait_ge(weights_ready, 1)
            with act.Fori(0, PAIRS) as i:
                for b in two:
                    n1 = i * 2 + (b + 1)
                    act.wait_ge(tok_done, n1)
                    nc.scalar.copy(H[:, i * 2 + b], banks[4 * b][0:TP, 0:TT * D]).then_inc(h_kept, 1)
                for b in two:
                    n1 = i * 2 + (b + 1)
                    act.wait_ge(xnT_psum, n1)
                    nc.scalar.copy(xnT[b][0:DP].rearrange("p c t -> p (c t)"),
                                   banks[4 * b + 1][0:DP, 0:DC * TOKENS]).then_inc(xnT_done, 1)
                for b in two:
                    n1 = i * 2 + (b + 1)
                    act.wait_ge(proj_in_done, n1)
                    for t in range(TT):
                        ins = nc.scalar.copy(zt[b][:, t].rearrange("p a d -> p (a d)"), banks[4 * b + 2 + t][0:TP, 0:2 * D])
                    ins.then_inc(act_steps, 1)
                    act.wait_ge(act_steps, n1)
                    nc.scalar.activation(sq[b][:], zt[b][:, :, 0], ACT.Square).then_inc(sq_done, 1)
                    kl = banks[4 * b][0:TP, 0:TT * (D + HEADS)].rearrange("p (t w) -> p t w", t=TT)
                    nc.scalar.activation(lr[b][:], kl[:, :, D:], ACT.Exp, scale=-1.0)
                    for t in range(TT):
                        nc.scalar.copy(k1[b][:, t, :, 0:DP], kl[:, t, 0:D].rearrange("p (c e) -> p c e", c=DC))
                    nc.scalar.copy(qT[b][0:DP].rearrange("p c t -> p (c t)"),
                                   banks[4 * b + 1][0:DP, 0:DC * TOKENS]).then_inc(acts_in_done, 1)
                for b in two:
                    n1 = i * 2 + (b + 1)
                    act.wait_ge(zbar_psum, n1)
                    nc.scalar.activation(sq[b][:], tiles(banks[4 * b + 1], TP, TT, D), ACT.Square).then_inc(zbar_sq_done, 1)
                for b in two:
                    n1 = i * 2 + (b + 1)
                    act.wait_ge(zbT_psum, n1)
                    nc.scalar.copy(zbT[b][:].rearrange("p c t -> p (c t)"),
                                   banks[4 * b + 2][0:DP, 0:DC * TOKENS]).then_inc(zbT_done, 1)

        @block.vector
        def _(dve):
            nc.vector.memset(w_in[:], 0.0)
            nc.vector.memset(w_1c[:], 0.0)
            for b in two:
                nc.vector.memset(xnT[b][DP:DP + 1], 1.0)
                nc.vector.memset(qT[b][DP:DP + 1], 1.0)
                nc.vector.memset(k1[b][:], 1.0)
            nc.vector.memset(w_q[:], 0.0).then_inc(cleared, 1)
            dve.wait_ge(weights_in, 16 * WEIGHT_DMAS)
            dve.wait_ge(cleared, 1)
            prep = Steps(dve, dve_steps, 0)
            for dc in range(DC):
                ins = nc.vector.tensor_tensor(w_q[:, dc, DP:DP + 1], q_col[:, dc:dc + 1], beta_col[:, dc:dc + 1], ALU.add)
            ins.then_inc(prep_dve, 1)
            prep.done(nc.vector.tensor_reduce(sums[:], w_1c[:].rearrange("p c (h e) -> p (c h) e", e=HD), AX_X, ALU.add))
            prep.settle()
            w1g = w_1c[:].rearrange("p c (h e) -> p (c h) e", e=HD)
            nc.vector.scalar_tensor_tensor(w1g, sums[:].unsqueeze(2).to_broadcast([DP + 1, HEADS, HD]), -1.0 / HD, w1g,
                                           ALU.mult, ALU.add).then_inc(prep_dve, 1)
            for c in range(DC):
                prep.done(nc.vector.tensor_tensor(w_vT[:, c], w_vT[:, c], w_kT[:, c], ALU.subtract))
            prep.done(nc.vector.tensor_tensor(gamma2[:], gamma_row[:], gamma_row[:], ALU.mult))
            prep.settle()
            for c in range(DC):
                prep.done(nc.vector.tensor_tensor(w_in[0:DP + 1, c, D:2 * D], w_vT[:, c], gamma_row[0:DP + 1], ALU.mult))
                prep.done(nc.vector.tensor_scalar(w_pg[:, c], w_pT[:, c], gamma_col[:, c:c + 1], None, ALU.mult))
            dve.wait_ge(prep_pe, 2)
            dve.wait_ge(prep_dve, 2)
            prep.done(nc.vector.tensor_tensor(w_qp[DP:DP + 1, 0], banks[0][DP:DP + 1, 0:D], p_bias[DP:DP + 1], ALU.add))
            prep.done(nc.vector.tensor_copy(w_qp[0:DP, 0], banks[0][0:DP, 0:D]))
            prep.done(nc.vector.tensor_copy(w_qp[0:DP, 1], banks[1][0:DP, 0:D]))
            prep.done(nc.vector.tensor_copy(w_in[DP:DP + 1, 0, 0:D], w_1c[DP:DP + 1].rearrange("p c e -> p (c e)")))
            prep.done(nc.vector.tensor_copy(w_in[0:DP, 0, 0:D], banks[2][0:DP, 0:D]))
            prep.done(nc.vector.tensor_copy(w_in[0:DP, 1, 0:D], banks[3][0:DP, 0:D]))
            prep.settle()
            dve.sem_inc(h_added, 2)
            dve.sem_inc(weights_ready, 1)

            with dve.Fori(0, PAIRS) as i:
                own = Steps(dve, dve_steps, i * TTT_STEPS_DVE + prep.n)
                for b in two:
                    n1 = i * 2 + (b + 1)
                    dve.wait_ge(h_kept, n1)
                    layernorm_dve(nc, dve, own, H, i * 2 + b, stats[b], mv[b], veps[b], veps_done)
                for b in two:
                    n1 = i * 2 + (b + 1)
                    dve.wait_ge(rstd_done, n1)
                    for t in range(TT):
                        ins = nc.vector.tensor_scalar(xn[b][:, t], H[:, i * 2 + b, t * D:(t + 1) * D], mv[b][:, t, 0:1],
                                                      rstd[b][:, t:t + 1], ALU.subtract, ALU.mult)
                    ins.then_inc(xn_done, 1)

                def group_var(b, signal):
                    own.done(nc.vector.tensor_reduce(gvar[b][:], grp(sq[b][:], 3), AX_X, ALU.add))
                    own.settle()
                    nc.vector.tensor_scalar(gvar[b][:], gvar[b][:], 1.0 / HD, TTT_EPS, ALU.mult, ALU.add).then_inc(signal, 1)

                def spread(stat):
                    return stat.unsqueeze(2).to_broadcast([TP, TT * HEADS, HD])

                for b in two:
                    n1 = i * 2 + (b + 1)
                    dve.wait_ge(sq_done, n1)
                    group_var(b, gvar_done)
                for b in two:
                    n1 = i * 2 + (b + 1)
                    dve.wait_ge(grstd_done, n1)
                    for t in range(TT):
                        hs = slice(t * HEADS, (t + 1) * HEADS)
                        ins = nc.vector.tensor_tensor(grp(xh[b][:, t], 2), grp(zt[b][:, t, 0], 2),
                                                      grstd[b][:, hs].unsqueeze(2).to_broadcast([TP, HEADS, HD]), ALU.mult)
                    ins.then_inc(xh_done, 1)
                    dve.wait_ge(acts_in_done, n1)
                    own.done(nc.vector.tensor_scalar(coef[b][:], lr[b][:].rearrange("p t h -> p (t h)"), 1.0, None, ALU.add))
                    own.settle()
                    own.done(nc.vector.reciprocal(coef[b][:], coef[b][:]))
                    own.settle()
                    own.done(nc.vector.scalar_tensor_tensor(coef[b][:], coef[b][:], 1.0 / (HD * TOKENS), grstd[b][:],
                                                            ALU.mult, ALU.mult))
                for b in two:
                    n1 = i * 2 + (b + 1)
                    dve.wait_ge(g2x_done, n1)
                    nc.vector.tensor_tensor(g[b][:], g[b][:], zt[b][:, :, 1], ALU.subtract).then_inc(g_done, 1)
                for b in two:
                    n1 = i * 2 + (b + 1)
                    dve.wait_ge(gx_done, n1)
                    own.done(nc.vector.tensor_reduce(sgx[b][:], grp(gx[b][:], 3), AX_X, ALU.add))
                    own.settle()
                    own.done(nc.vector.scalar_tensor_tensor(grp(gx[b][:], 3), grp(xh[b][:], 3), 1.0 / HD, spread(sgx[b][:]),
                                                            ALU.mult, ALU.mult))
                    own.settle()
                    own.done(nc.vector.tensor_tensor(g[b][:], g[b][:], gx[b][:], ALU.subtract))
                    own.settle()
                    nc.vector.tensor_tensor(grp(g[b][:], 3), grp(g[b][:], 3), spread(coef[b][:]), ALU.mult)\
                      .then_inc(grad_in_done, 1)
                for b in two:
                    n1 = i * 2 + (b + 1)
                    dve.wait_ge(grad_done, n1)
                    grad = banks[4 * b][0:DP + 1, 0:D]
                    own.done(nc.vector.tensor_reduce(gsum[b][:], grp(grad, 2), AX_X, ALU.add))
                    own.settle()
                    own.done(nc.vector.scalar_tensor_tensor(grp(gc[b][:], 2), gsum[b][:].unsqueeze(2).to_broadcast([DP + 1, HEADS, HD]),
                                                            -1.0 / HD, grp(grad, 2), ALU.mult, ALU.add))
                    own.settle()
                    own.done(nc.vector.tensor_tensor(gc[b][:], gc[b][:], head_mask[:], ALU.mult))
                    own.settle()
                    nc.vector.tensor_tensor(w_1n[b][:].rearrange("p c e -> p (c e)"), w_1c[:].rearrange("p c e -> p (c e)"),
                                            gc[b][:], ALU.subtract).then_inc(w1n_done, 1)
                for b in two:
                    n1 = i * 2 + (b + 1)
                    dve.wait_ge(zbar_sq_done, n1)
                    group_var(b, zvar_done)
                for b in two:
                    n1 = i * 2 + (b + 1)
                    dve.wait_ge(zrstd_done, n1)
                    nc.vector.tensor_tensor(grp(zb[b][:], 3), banks[4 * b + 1][0:TP, 0:TT * D].rearrange("p (g e) -> p g e", e=HD),
                                            spread(grstd[b][:]), ALU.mult).then_inc(zb_done, 1)
                for b in two:
                    n1 = i * 2 + (b + 1)
                    dve.wait_ge(out_psum, n1)
                    nc.vector.tensor_tensor(H[:, i * 2 + b], H[:, i * 2 + b], banks[4 * b + 3][0:TP, 0:TT * D], ALU.add)\
                      .then_inc(h_added, 1)
                assert own.n == TTT_STEPS_DVE, own.n


def layernorm_dve(nc, dve, own, H, index, stats, mv, veps, veps_done):
    for t in range(TT):
        own.done(nc.vector.bn_stats(stats[:, t], H[:, index, t * D:(t + 1) * D]))
    own.settle()
    nc.vector.memset(veps[:], 0.0)
    for t in range(TT):
        ins = nc.vector.bn_aggr(mv[:, t], stats[:, t])
    own.done(ins)
    own.settle()
    nc.vector.tensor_scalar(veps[:], mv[:, :, 1], LN_EPS, None, ALU.add).then_inc(veps_done, 1)


def normalise_dve(nc, H, index, mv, rstd, xn, xn_done):
    for t in range(TT):
        ins = nc.vector.tensor_scalar(xn[:, t, 0:D], H[:, index, t * D:(t + 1) * D], mv[:, t, 0:1],
                                      rstd[:, t:t + 1], ALU.subtract, ALU.mult)
    ins.then_inc(xn_done, 1)


def transposes_pe(nc, src, bank, ident, signal):
    for t in range(TT):
        for c in range(DC):
            mm = nc.tensor.transpose(bank[0:DP, c * TOKENS + t * TP:c * TOKENS + (t + 1) * TP],
                                     src[:, t, c * DP:(c + 1) * DP], ident[0:TP, 0:TP])
    mm.then_inc(signal, 1)


EXPERTS = 4


def moe_stage(nc, a, H, ident):
    MOE_STEPS_DVE = 24
    with ExitStack() as ctx:
        st = Stage(nc, ctx, "moe")
        sb, sem = st.sb, st.sem
        banks = st.psum_banks()
        two = range(2)

        w_1 = sb("w_1", [DP + 1, DC, EXPERTS, D])
        w_2 = sb("w_2", [DP + 1, DC, EXPERTS, D])
        w_r = sb("w_r", [DP + 1, DC, EXPERTS])
        mhalf = sb("mhalf", [TP, TT])
        xn = [sb(f"xn{b}", [TP, TT, D]) for b in two]
        xnT = [sb(f"xnT{b}", [DP + 1, DC, TOKENS]) for b in two]
        stats = [sb(f"stats{b}", [TP, TT, 6]) for b in two]
        mv = [sb(f"mv{b}", [TP, TT, 2]) for b in two]
        veps = [sb(f"veps{b}", [TP, TT]) for b in two]
        rstd = [sb(f"rstd{b}", [TP, TT]) for b in two]
        logits = [sb(f"logits{b}", [TP, TT, EXPERTS]) for b in two]
        top = [sb(f"top{b}", [TP, TT]) for b in two]
        chosen = [sb(f"chosen{b}", [TP, TT, EXPERTS]) for b in two]
        left = [sb(f"left{b}", [TP, TT]) for b in two]
        hidT = [[sb(f"hidT{b}{e}", [DP + 1, DC, TOKENS]) for e in range(2)] for b in two]
        acc = [sb(f"acc{b}", [TP, TT, D]) for b in two]

        rows_set = sem("rows_set")
        weights_in = sem("weights_in")
        veps_done = sem("veps_done")
        rstd_done = sem("rstd_done")
        xn_done = sem("xn_done")
        xnT_psum = sem("xnT_psum")
        xnT_done = sem("xnT_done")
        logits_psum = sem("logits_psum")
        logits_read = sem("logits_read")
        hid_psum = sem("hid_psum")
        gelu_done = sem("gelu_done")
        y_psum = sem("y_psum")
        y_used = sem("y_used")
        dve_steps = sem("dve_steps")

        LOADS = 8
        block = ctx.enter_context(nc.Block())

        @block.sync
        def _(sp):
            for dst, src in ((w_1[0:DP], a["moe_w1"]), (w_1[DP:DP + 1, 0], a["moe_b1"]), (w_2[0:DP], a["moe_w2"]),
                             (w_2[DP:DP + 1, 0], a["moe_b2"]), (w_r[0:DP], a["router_w"]), (w_r[DP:DP + 1, 0], a["router_b"]),
                             (mhalf[:], a["mhalf"][0:TP, 0:TT]), (ident[:], a["ident"])):
                sp.dma_start(dst, src).then_inc(weights_in, 16)

        @block.gpsimd
        def _(pool):
            pool.wait_ge(weights_in, 16 * LOADS)
            with pool.Fori(0, PAIRS) as i:
                for b in two:
                    pool.wait_ge(veps_done, i * 2 + (b + 1))
                    nc.gpsimd.tensor_tensor(rstd[b][:], veps[b][:], mhalf[:], ALU.pow).then_inc(rstd_done, 1)

        @block.tensor
        def _(pe):
            pe.wait_ge(weights_in, 16 * LOADS)
            pe.wait_ge(rows_set, 1)
            with pe.Fori(0, PAIRS) as i:
                def hidden(b, e):
                    for m in range(DC):
                        for c in range(DC):
                            K = DP + 1 - c
                            mm = nc.tensor.matmul(banks[4 * b + 2 + e % 2][0:DP, m * TOKENS:(m + 1) * TOKENS],
                                                  w_1[0:K, c, e, m * DP:(m + 1) * DP], xnT[b][0:K, c],
                                                  start=c == 0, stop=c == 1)
                    mm.then_inc(hid_psum, 1)

                def output(b, e):
                    for t in range(TT):
                        for c in range(DC):
                            K = DP + 1 - c
                            mm = nc.tensor.matmul(banks[4 * b + e % 2][0:TP, t * D:(t + 1) * D],
                                                  hidT[b][e % 2][0:K, c, t * TP:(t + 1) * TP], w_2[0:K, c, e],
                                                  start=c == 0, stop=c == 1)
                    mm.then_inc(y_psum, 1)

                for b in two:
                    pe.wait_ge(xn_done, i * 2 + (b + 1))
                    transposes_pe(nc, xn[b], banks[4 * b], ident, xnT_psum)
                for b in two:
                    pe.wait_ge(xnT_done, i * 2 + (b + 1))
                    for t in range(TT):
                        for c in range(DC):
                            K = DP + 1 - c
                            mm = nc.tensor.matmul(banks[4 * b + 1][0:TP, t * EXPERTS:(t + 1) * EXPERTS],
                                                  xnT[b][0:K, c, t * TP:(t + 1) * TP], w_r[0:K, c], start=c == 0, stop=c == 1)
                    mm.then_inc(logits_psum, 1)
                    hidden(b, 0)
                    hidden(b, 1)
                for e in range(EXPERTS):
                    for b in two:
                        pe.wait_ge(gelu_done, i * 8 + (2 * e + b + 1))
                        if e == 1:
                            pe.wait_ge(logits_read, i * 2 + (b + 1))
                        if e >= 2:
                            pe.wait_ge(y_used, i * 8 + (2 * (e - 2) + b + 1))
                        output(b, e)
                        if e < 2:
                            hidden(b, e + 2)

        @block.scalar
        def _(act):
            with act.Fori(0, PAIRS) as i:
                for b in two:
                    act.wait_ge(xnT_psum, i * 2 + (b + 1))
                    nc.scalar.copy(xnT[b][0:DP].rearrange("p c t -> p (c t)"),
                                   banks[4 * b][0:DP, 0:DC * TOKENS]).then_inc(xnT_done, 1)
                arrival = {(0, 0): 1, (0, 1): 2, (1, 0): 3, (1, 1): 4, (0, 2): 5, (1, 2): 6, (0, 3): 7, (1, 3): 8}
                for e in range(EXPERTS):
                    for b in two:
                        act.wait_ge(hid_psum, i * 8 + arrival[b, e])
                        if e >= 2:
                            act.wait_ge(y_psum, i * 8 + (2 * (e - 2) + b + 1))
                        nc.scalar.activation(hidT[b][e % 2][0:DP].rearrange("p c t -> p (c t)"),
                                             banks[4 * b + 2 + e % 2][0:DP, 0:DC * TOKENS], ACT.Gelu).then_inc(gelu_done, 1)

        @block.vector
        def _(dve):
            for b in two:
                nc.vector.memset(xnT[b][DP:DP + 1], 1.0)
                nc.vector.memset(hidT[b][0][DP:DP + 1], 1.0)
                ins = nc.vector.memset(hidT[b][1][DP:DP + 1], 1.0)
            ins.then_inc(rows_set, 1)
            with dve.Fori(0, PAIRS) as i:
                own = Steps(dve, dve_steps, i * MOE_STEPS_DVE)
                for b in two:
                    layernorm_dve(nc, dve, own, H, i * 2 + b, stats[b], mv[b], veps[b], veps_done)
                for b in two:
                    dve.wait_ge(rstd_done, i * 2 + (b + 1))
                    normalise_dve(nc, H, i * 2 + b, mv[b], rstd[b], xn[b], xn_done)
                for b in two:
                    dve.wait_ge(xn_done, i * 2 + (b + 1))
                    own.done(nc.vector.tensor_tensor(acc[b][:].rearrange("p t d -> p (t d)"), H[:, i * 2 + b],
                                                     xn[b][:].rearrange("p t d -> p (t d)"), ALU.add))
                for b in two:
                    dve.wait_ge(logits_psum, i * 2 + (b + 1))
                    nc.vector.tensor_copy(logits[b][:].rearrange("p t e -> p (t e)"),
                                          banks[4 * b + 1][0:TP, 0:TT * EXPERTS]).then_inc(logits_read, 1)
                    dve.wait_ge(logits_read, i * 2 + (b + 1))
                    own.done(nc.vector.tensor_reduce(top[b][:], logits[b][:], AX_X, ALU.max))
                    own.settle()
                    own.done(nc.vector.tensor_tensor(chosen[b][:], logits[b][:], top[b][:].unsqueeze(2).to_broadcast([TP, TT, EXPERTS]),
                                                     ALU.is_equal))
                    own.settle()
                    own.done(nc.vector.tensor_scalar(left[b][:], chosen[b][:, :, 0], -1.0, 1.0, ALU.mult, ALU.add))
                    for e in range(1, EXPERTS):
                        own.settle()
                        own.done(nc.vector.tensor_tensor(chosen[b][:, :, e], chosen[b][:, :, e], left[b][:], ALU.mult))
                        if e < EXPERTS - 1:
                            own.settle()
                            own.done(nc.vector.tensor_tensor(left[b][:], left[b][:], chosen[b][:, :, e], ALU.subtract))
                for e in range(EXPERTS):
                    for b in two:
                        dve.wait_ge(y_psum, i * 8 + (2 * e + b + 1))
                        if e == 0:
                            own.settle()
                        else:
                            dve.wait_ge(y_used, i * 8 + (2 * (e - 1) + b + 1))
                        for t in range(TT):
                            dst = acc[b][:, t] if e < EXPERTS - 1 else H[:, i * 2 + b, t * D:(t + 1) * D]
                            ins = nc.vector.scalar_tensor_tensor(dst, banks[4 * b + e % 2][0:TP, t * D:(t + 1) * D],
                                                                 chosen[b][:, t, e:e + 1], acc[b][:, t], ALU.mult, ALU.add)
                        ins.then_inc(y_used, 1)
                assert own.n == MOE_STEPS_DVE, own.n


GH = 3
GROUPS = HEADS // GH
SLOT = 32
VW = HD + 1
CAUSAL = TOKENS + TP


def attention_stage(nc, a, H, ident):
    ATT_STEPS_DVE = 22
    with ExitStack() as ctx:
        st = Stage(nc, ctx, "att")
        sb, sem = st.sb, st.sem
        ps = ctx.enter_context(nc.psum_tensor("att_psum", [128, 8, 512], F32))
        two = range(2)

        w_in = sb("w_in", [DP + 1, DC, 3 * D])
        w_raw = sb("w_raw", [DP, DC, 3 * D])
        b_raw = sb("b_raw", [DP + 1, 3 * D])
        scale_col = sb("scale_col", [DP, DC])
        shift_col = sb("shift_col", [DP, DC])
        shift_w = sb("shift_w", [DP, DC, DP + 1])
        w_out = sb("w_out", [DP + 1, DC, D])
        rezero = sb("rezero", [DP + 1, 1])
        sinks = sb("sinks", [TP, HEADS])
        cos = sb("cos", [TP, TT, HD])
        sin = sb("sin", [TP, TT, HD])
        mask_qk_f = sb("mask_qk_f", [TP, TP])
        mask_kq_f = sb("mask_kq_f", [TP, TP])
        sel_f = sb("sel_f", [GH * SLOT, HEADS, TP])
        mask_qk = sb("mask_qk", [TP, TP], BF16)
        mask_kq = sb("mask_kq", [TP, TP], BF16)
        sel = sb("sel", [GH * SLOT, HEADS, TP], BF16)
        ident_b = sb("ident_b", [TP, TP], BF16)
        mhalf = sb("mhalf", [TP, TT])

        xn = [sb(f"xn{b}", [TP, TT, D]) for b in two]
        xnT = [sb(f"xnT{b}", [DP + 1, DC, TOKENS]) for b in two]
        stats = [sb(f"stats{b}", [TP, TT, 6]) for b in two]
        mv = [sb(f"mv{b}", [TP, TT, 2]) for b in two]
        veps = [sb(f"veps{b}", [TP, TT]) for b in two]
        rstd = [sb(f"rstd{b}", [TP, TT]) for b in two]
        rot_c = [sb(f"rot_c{b}", [TP, TT, 2 * D]) for b in two]
        rot_s = [sb(f"rot_s{b}", [TP, TT, 2 * D]) for b in two]
        qk = [sb(f"qk{b}", [TP, TT, 2 * HEADS, SLOT]) for b in two]
        qkT = [sb(f"qkT{b}", [GH * SLOT, GROUPS, 2 * TOKENS]) for b in two]
        v1 = [sb(f"v1{b}", [TP, TT, HEADS, VW]) for b in two]
        peak = [sb(f"peak{b}", [TP, TT, HEADS]) for b in two]
        npk_hi = [sb(f"npk_hi{b}", [TP, TT, HEADS], BF16) for b in two]
        npk_lo = [sb(f"npk_lo{b}", [TP, TT, HEADS], BF16) for b in two]
        npk = [sb(f"npk{b}", [TP, TT, GH, SLOT], BF16) for b in two]
        npkT = [sb(f"npkT{b}", [GH * SLOT, TOKENS], BF16) for b in two]
        sink_w = [sb(f"sink_w{b}", [TP, TT, HEADS]) for b in two]
        weights = [[sb(f"weights{b}{g}", [TP, GH, CAUSAL]) for g in range(2)] for b in two]
        den = [sb(f"den{b}", [TP, TT, HEADS]) for b in two]
        y = [sb(f"y{b}", [TP, TT, D]) for b in two]
        yT = [sb(f"yT{b}", [DP + 1, DC, TOKENS]) for b in two]

        cleared = sem("cleared")
        weights_in = sem("weights_in")
        prep_psum = sem("prep_psum")
        weights_ready = sem("weights_ready")
        veps_done = sem("veps_done")
        rstd_done = sem("rstd_done")
        xn_done = sem("xn_done")
        xnT_psum = sem("xnT_psum")
        xnT_done = sem("xnT_done")
        qkv_psum = sem("qkv_psum")
        v_kept = sem("v_kept")
        qk_done = sem("qk_done")
        qkT_psum = sem("qkT_psum")
        qkT_done = sem("qkT_done")
        scores_psum = sem("scores_psum")
        peaks_read = sem("peaks_read")
        npk_done = sem("npk_done")
        sink_arg = sem("sink_arg")
        npkT_psum = sem("npkT_psum")
        npkT_done = sem("npkT_done")
        sink_done = sem("sink_done")
        shifted_psum = sem("shifted_psum")
        exp_done = sem("exp_done")
        pv_done = sem("pv_done")
        y_done = sem("y_done")
        yT_psum = sem("yT_psum")
        yT_done = sem("yT_done")
        out_psum = sem("out_psum")
        dve_steps = sem("dve_steps")
        LOADS = 15
        block = ctx.enter_context(nc.Block())

        @block.sync
        def _(sp):
            sp.wait_ge(cleared, 1)
            loads = ((w_raw[:], a["attn_w"]), (b_raw[DP:DP + 1], a["attn_b"]), (scale_col[:], a["norm_scale"]),
                     (shift_col[:], a["norm_bias"]), (w_out[0:DP], a["attn_pw"]), (w_out[DP:DP + 1, 0], a["attn_pb"]),
                     (rezero[:], a["rezero"].partition_broadcast(DP + 1).rearrange("p o d -> p (o d)")),
                     (sinks[:], a["sinks"].partition_broadcast(TP).rearrange("p o d -> p (o d)")),
                     (cos[:], a["rope_cos"]), (sin[:], a["rope_sin"]), (mask_qk_f[:], a["mask_qk"]),
                     (mask_kq_f[:], a["mask_kq"]), (sel_f[:], a["head_sel"]), (mhalf[:], a["mhalf"][0:TP, 0:TT]),
                     (ident[:], a["ident"]))
            assert len(loads) == LOADS, len(loads)
            for dst, src in loads:
                sp.dma_start(dst, src).then_inc(weights_in, 16)

        @block.gpsimd
        def _(pool):
            pool.wait_ge(weights_in, 16 * LOADS)
            with pool.Fori(0, PAIRS) as i:
                for b in two:
                    pool.wait_ge(veps_done, i * 2 + (b + 1))
                    nc.gpsimd.tensor_tensor(rstd[b][:], veps[b][:], mhalf[:], ALU.pow).then_inc(rstd_done, 1)

        @block.tensor
        def _(pe):
            pe.wait_ge(weights_in, 16 * LOADS)
            pe.wait_ge(prep_psum, 1)
            for part, (lo, hi) in enumerate(((0, 2 * D), (2 * D, 3 * D))):
                for c in range(DC):
                    mm = nc.tensor.matmul(ps[0:DP + 1, part, 0:hi - lo], shift_w[:, c], w_raw[:, c, lo:hi],
                                          start=c == 0, stop=c == 1)
            mm.then_inc(prep_psum, 1)
            pe.wait_ge(weights_ready, 1)
            with pe.Fori(0, PAIRS) as i:
                for b in two:
                    pe.wait_ge(xn_done, i * 2 + (b + 1))
                    transposes_pe(nc, xn[b], ps[:, 4 * b], ident, xnT_psum)
                for b in two:
                    pe.wait_ge(xnT_done, i * 2 + (b + 1))
                    for t in range(TT):
                        for lo, hi, o in ((0, 2 * D, ps[0:TP, 4 * b + 1 + t, 0:2 * D]),
                                          (2 * D, 3 * D, ps[0:TP, 4 * b + 3, t * D:(t + 1) * D])):
                            for c in range(DC):
                                K = DP + 1 - c
                                mm = nc.tensor.matmul(o, xnT[b][0:K, c, t * TP:(t + 1) * TP], w_in[0:K, c, lo:hi],
                                                      start=c == 0, stop=c == 1)
                    mm.then_inc(qkv_psum, 1)
                for b in two:
                    pe.wait_ge(qk_done, i * 2 + (b + 1))
                    pe.wait_ge(v_kept, i * 2 + (b + 1))
                    for g in range(GROUPS):
                        for kind in range(2):
                            for t in range(TT):
                                h0 = kind * HEADS + g * GH
                                mm = nc.tensor.transpose(ps[0:GH * SLOT, 4 * b + g, kind * TOKENS + t * TP:kind * TOKENS + (t + 1) * TP],
                                                         qk[b][:, t, h0:h0 + GH].rearrange("p h s -> p (h s)"), ident[0:TP, 0:TP])
                    mm.then_inc(qkT_psum, 1)
                for g in range(GROUPS):
                    for b in two:
                        if g == 0:
                            pe.wait_ge(qkT_done, i * 2 + (b + 1))
                        else:
                            pe.wait_ge(peaks_read, i * 8 + (2 * (g - 1) + b + 1))
                        for j in range(GH):
                            rows = slice(SLOT * j, SLOT * j + HD)
                            bank = ps[0:TP, 4 * b + j]
                            for t, o, m in ((0, bank[:, 0:TP], bank[:, 0:TP]), (1, bank[:, TP:TP + TOKENS], bank[:, TOKENS:CAUSAL])):
                                nc.tensor.matmul(o, qkT[b][rows, g, t * TP:(t + 1) * TP],
                                                 qkT[b][rows, g, TOKENS:TOKENS + (t + 1) * TP], start=True, stop=True)
                                mm = nc.tensor.matmul(m, ident_b[:], mask_qk[:], start=False, stop=True, skip_group_check=True)
                        mm.then_inc(scores_psum, 1)
                for b in two:
                    pe.wait_ge(npk_done, i * 2 + (b + 1))
                    for t in range(TT):
                        mm = nc.tensor.transpose(ps[0:GH * SLOT, 4 * b + 3, 0:TP].bitcast(BF16)[:, t * TP:(t + 1) * TP],
                                                 npk[b][:, t].rearrange("p j s -> p (j s)"), ident_b[:])
                    mm.then_inc(npkT_psum, 1)
                for g in range(GROUPS):
                    for b in two:
                        if g == 0:
                            pe.wait_ge(npkT_done, i * 2 + (b + 1))
                        for j in range(GH):
                            h = g * GH + j
                            rows = slice(SLOT * j, SLOT * j + HD)
                            slot = slice(SLOT * j, SLOT * (j + 1))
                            bank = ps[0:TP, 4 * b + j]
                            for t, o, m in ((0, bank[:, 0:TOKENS], bank[:, 0:TP]), (1, bank[:, TOKENS:CAUSAL], bank[:, TOKENS:CAUSAL])):
                                nc.tensor.matmul(o, qkT[b][rows, g, TOKENS + t * TP:TOKENS + (t + 1) * TP],
                                                 qkT[b][rows, g, t * TP:TOKENS], start=True, stop=False)
                                nc.tensor.matmul(o, sel[slot, h], npkT[b][slot, t * TP:TOKENS], start=False, stop=True)
                                mm = nc.tensor.matmul(m, ident_b[:], mask_kq[:], start=False, stop=True, skip_group_check=True)
                        mm.then_inc(shifted_psum, 1)
                    for b in two:
                        pe.wait_ge(exp_done, i * 8 + (2 * g + b + 1))
                        for j in range(GH):
                            h = g * GH + j
                            p, o = weights[b][g % 2], ps[0:TP, 4 * b + 3]
                            nc.tensor.matmul(o[:, h * VW:(h + 1) * VW], p[:, j, 0:TP], v1[b][:, 0, h], start=True, stop=True)
                            o1 = o[:, (HEADS + h) * VW:(HEADS + h + 1) * VW]
                            nc.tensor.matmul(o1, p[:, j, TP:TOKENS], v1[b][:, 0, h], start=True, stop=False)
                            mm = nc.tensor.matmul(o1, p[:, j, TOKENS:CAUSAL], v1[b][:, 1, h], start=False, stop=True)
                        mm.then_inc(pv_done, 1)
                for b in two:
                    pe.wait_ge(y_done, i * 2 + (b + 1))
                    transposes_pe(nc, y[b], ps[:, 4 * b], ident, yT_psum)
                for b in two:
                    pe.wait_ge(yT_done, i * 2 + (b + 1))
                    for t in range(TT):
                        for c in range(DC):
                            K = DP + 1 - c
                            mm = nc.tensor.matmul(ps[0:TP, 4 * b + 1, t * D:(t + 1) * D], yT[b][0:K, c, t * TP:(t + 1) * TP],
                                                  w_out[0:K, c], start=c == 0, stop=c == 1)
                    mm.then_inc(out_psum, 1)

        @block.scalar
        def _(act):
            act.wait_ge(weights_ready, 1)
            with act.Fori(0, PAIRS) as i:
                for b in two:
                    act.wait_ge(xnT_psum, i * 2 + (b + 1))
                    nc.scalar.copy(xnT[b][0:DP].rearrange("p c t -> p (c t)"),
                                   ps[0:DP, 4 * b, 0:DC * TOKENS]).then_inc(xnT_done, 1)
                for b in two:
                    act.wait_ge(qkv_psum, i * 2 + (b + 1))
                    for t in range(TT):
                        ins = nc.scalar.copy(v1[b][:, t, :, 0:HD],
                                             ps[0:TP, 4 * b + 3, t * D:(t + 1) * D].rearrange("p (h e) -> p h e", e=HD))
                    ins.then_inc(v_kept, 1)
                for b in two:
                    act.wait_ge(qkT_psum, i * 2 + (b + 1))
                    nc.scalar.copy(qkT[b][:], ps[0:GH * SLOT, 4 * b:4 * b + GROUPS, 0:2 * TOKENS]).then_inc(qkT_done, 1)
                for b in two:
                    act.wait_ge(sink_arg, i * 2 + (b + 1))
                    nc.scalar.activation(sink_w[b][:], sink_w[b][:], ACT.Exp).then_inc(sink_done, 1)
                for g in range(GROUPS):
                    for b in two:
                        act.wait_ge(shifted_psum, i * 8 + (2 * g + b + 1))
                        if g >= 2:
                            act.wait_ge(pv_done, i * 8 + (2 * (g - 2) + b + 1))
                        nc.scalar.activation(weights[b][g % 2][:], ps[0:TP, 4 * b:4 * b + GH, 0:CAUSAL], ACT.Exp)\
                          .then_inc(exp_done, 1)
                for b in two:
                    act.wait_ge(yT_psum, i * 2 + (b + 1))
                    nc.scalar.copy(yT[b][0:DP].rearrange("p c t -> p (c t)"),
                                   ps[0:DP, 4 * b, 0:DC * TOKENS]).then_inc(yT_done, 1)

        @block.vector
        def _(dve):
            nc.vector.memset(shift_w[:], 0.0)
            for b in two:
                nc.vector.memset(xnT[b][DP:DP + 1], 1.0)
                nc.vector.memset(yT[b][DP:DP + 1], 1.0)
                nc.vector.memset(v1[b][:], 1.0)
                nc.vector.memset(npk[b][:], 0.0)
                nc.vector.memset(qk[b][:], 0.0)
            nc.vector.memset(w_in[:], 0.0).then_inc(cleared, 1)
            dve.wait_ge(cleared, 1)
            dve.wait_ge(weights_in, 16 * LOADS)
            nc.vector.tensor_copy(shift_w[:, :, DP], shift_col[:]).then_inc(prep_psum, 1)
            for c in range(DC):
                nc.vector.tensor_scalar(w_in[0:DP, c], w_raw[:, c], scale_col[:, c:c + 1], None, ALU.mult)
            nc.vector.tensor_copy(ident_b[:], ident[0:TP, 0:TP])
            nc.vector.tensor_copy(mask_qk[:], mask_qk_f[:])
            nc.vector.tensor_copy(mask_kq[:], mask_kq_f[:])
            nc.vector.tensor_copy(sel[:], sel_f[:])
            nc.vector.tensor_scalar(w_out[:, 0], w_out[:, 0], rezero[:], None, ALU.mult)
            nc.vector.tensor_scalar(w_out[0:DP, 1], w_out[0:DP, 1], rezero[0:DP], None, ALU.mult)
            dve.wait_ge(prep_psum, 2)
            prep = Steps(dve, dve_steps, 0)
            row = w_in[DP:DP + 1, 0]
            prep.done(nc.vector.tensor_tensor(row[:, 0:2 * D], ps[DP:DP + 1, 0, 0:2 * D], b_raw[DP:DP + 1, 0:2 * D], ALU.add))
            prep.done(nc.vector.tensor_tensor(row[:, 2 * D:], ps[DP:DP + 1, 1, 0:D], b_raw[DP:DP + 1, 2 * D:], ALU.add))
            prep.settle()
            nc.vector.tensor_scalar(w_in[:, :, 0:D], w_in[:, :, 0:D], HD ** -0.5, None, ALU.mult).then_inc(weights_ready, 1)

            with dve.Fori(0, PAIRS) as i:
                own = Steps(dve, dve_steps, i * ATT_STEPS_DVE + prep.n)
                for b in two:
                    layernorm_dve(nc, dve, own, H, i * 2 + b, stats[b], mv[b], veps[b], veps_done)
                for b in two:
                    dve.wait_ge(rstd_done, i * 2 + (b + 1))
                    normalise_dve(nc, H, i * 2 + b, mv[b], rstd[b], xn[b], xn_done)
                for b in two:
                    dve.wait_ge(qkv_psum, i * 2 + (b + 1))
                    for t in range(TT):
                        src = ps[0:TP, 4 * b + 1 + t, 0:2 * D].rearrange("p (h e) -> p h e", e=HD)
                        dc = rot_c[b][:, t].rearrange("p (h e) -> p h e", e=HD)
                        ds = rot_s[b][:, t].rearrange("p (h e) -> p h e", e=HD)
                        half = [TP, 2 * HEADS, HD // 2]
                        nc.vector.tensor_tensor(dc, src, cos[:, t].unsqueeze(1).to_broadcast([TP, 2 * HEADS, HD]), ALU.mult)
                        for one, other in ((0, 1), (1, 0)):
                            ins = nc.vector.tensor_tensor(ds[:, :, one::2], src[:, :, other::2],
                                                          sin[:, t, one::2].unsqueeze(1).to_broadcast(half), ALU.mult)
                    own.done(ins)
                    own.settle()
                    for t in range(TT):
                        ins = nc.vector.tensor_tensor(qk[b][:, t, :, 0:HD], rot_c[b][:, t].rearrange("p (h e) -> p h e", e=HD),
                                                      rot_s[b][:, t].rearrange("p (h e) -> p h e", e=HD), ALU.add)
                    ins.then_inc(qk_done, 1)
                for g in range(GROUPS):
                    for b in two:
                        dve.wait_ge(scores_psum, i * 8 + (2 * g + b + 1))
                        hs = slice(g * GH, (g + 1) * GH)
                        nc.vector.tensor_reduce(peak[b][:, 0, hs], ps[0:TP, 4 * b:4 * b + GH, 0:TP], AX_X, ALU.max)
                        nc.vector.tensor_reduce(peak[b][:, 1, hs], ps[0:TP, 4 * b:4 * b + GH, TP:CAUSAL], AX_X, ALU.max)\
                          .then_inc(peaks_read, 1)
                every_t = sinks[:].unsqueeze(1).to_broadcast([TP, TT, HEADS])
                for b in two:
                    dve.wait_ge(peaks_read, i * 8 + (6 + b + 1))
                    own.done(nc.vector.tensor_tensor(peak[b][:], peak[b][:], every_t, ALU.max))
                    own.settle()
                    own.done(nc.vector.tensor_scalar(npk_hi[b][:], peak[b][:], -1.0, None, ALU.mult))
                    own.settle()
                    own.done(nc.vector.scalar_tensor_tensor(npk_lo[b][:], peak[b][:], -1.0, npk_hi[b][:], ALU.mult, ALU.subtract))
                    own.settle()
                    nc.vector.tensor_copy(npk[b][:, :, :, 0:HEADS], npk_hi[b][:].unsqueeze(2).to_broadcast([TP, TT, GH, HEADS]))
                    nc.vector.tensor_copy(npk[b][:, :, :, HEADS:2 * HEADS],
                                          npk_lo[b][:].unsqueeze(2).to_broadcast([TP, TT, GH, HEADS])).then_inc(npk_done, 1)
                    own.done(nc.vector.tensor_tensor(sink_w[b][:], npk_hi[b][:], npk_lo[b][:], ALU.add))
                    own.settle()
                    nc.vector.tensor_tensor(sink_w[b][:], sink_w[b][:], every_t, ALU.add).then_inc(sink_arg, 1)
                for b in two:
                    dve.wait_ge(npkT_psum, i * 2 + (b + 1))
                    nc.vector.tensor_copy(npkT[b][:], ps[0:GH * SLOT, 4 * b + 3, 0:TP].bitcast(BF16)).then_inc(npkT_done, 1)
                for b in two:
                    dve.wait_ge(pv_done, i * 8 + (6 + b + 1))
                    dve.wait_ge(sink_done, i * 2 + (b + 1))
                    o = ps[0:TP, 4 * b + 3, 0:TT * HEADS * VW].rearrange("p (t h e) -> p t h e", t=TT, e=VW)
                    own.done(nc.vector.tensor_tensor(den[b][:], o[:, :, :, HD], sink_w[b][:], ALU.add))
                    own.settle()
                    own.done(nc.vector.reciprocal(den[b][:], den[b][:]))
                    own.settle()
                    o = ps[0:TP, 4 * b + 3, 0:TT * HEADS * VW].rearrange("p (g e) -> p g e", e=VW)
                    nc.vector.tensor_tensor(y[b][:].rearrange("p t (h e) -> p (t h) e", e=HD), o[:, :, 0:HD],
                                            den[b][:].rearrange("p t h -> p (t h)").unsqueeze(2).to_broadcast([TP, TT * HEADS, HD]),
                                            ALU.mult).then_inc(y_done, 1)
                for b in two:
                    dve.wait_ge(out_psum, i * 2 + (b + 1))
                    own.done(nc.vector.tensor_tensor(H[:, i * 2 + b], H[:, i * 2 + b], ps[0:TP, 4 * b + 1, 0:TT * D], ALU.add))
                    own.settle()
                assert own.n == ATT_STEPS_DVE, own.n


SLOTS = 1024
ST = SLOTS // 128
QUARTERS = 4
QW = SLOTS // QUARTERS
PHI_EPS = 1e-6


def dispatch_stage(nc, a, H, ident, phi, neg_row_max, slots_dram):
    DIS_STEPS_DVE = 46
    with ExitStack() as ctx:
        st = Stage(nc, ctx, "dis")
        sb, sem = st.sb, st.sem
        ps = ctx.enter_context(nc.psum_tensor("dis_psum", [128, 8, 512], F32))
        two = range(2)

        phi_sq = sb("phi_sq", [DP, DC, SLOTS])
        phi_sum = sb("phi_sum", [DP, DC, ST, 2])
        mhalf = sb("mhalf", [128, 24])
        ident_b = sb("ident_b", [128, 128], BF16)
        ones = sb("ones", [2, TP], BF16)
        xn = [sb(f"xn{b}", [TP, TT, D + 1]) for b in two]
        xnT = [sb(f"xnT{b}", [DP, DC, TOKENS]) for b in two]
        stats = [sb(f"stats{b}", [TP, TT, 6]) for b in two]
        mv = [sb(f"mv{b}", [TP, TT, 2]) for b in two]
        veps = [sb(f"veps{b}", [TP, TT]) for b in two]
        rstd = [sb(f"rstd{b}", [TP, TT]) for b in two]
        col_peak = [sb(f"col_peak{b}", [128, 2]) for b in two]
        col_parts = [sb(f"col_parts{b}", [128, 2, 2], BF16) for b in two]
        col_row = [sb(f"col_row{b}", [2, QW], BF16) for b in two]
        row_peak = [sb(f"row_peak{b}", [TP, TT, QUARTERS]) for b in two]
        weights = [sb(f"weights{b}", [TP, TT, QW]) for b in two]
        sstats = [sb(f"sstats{b}", [128, 2, 6]) for b in two]
        smv = [sb(f"smv{b}", [128, 2, 2]) for b in two]
        sden = [sb(f"sden{b}", [128, 2]) for b in two]
        sveps = [sb(f"sveps{b}", [128, 2]) for b in two]
        srstd = [sb(f"srstd{b}", [128, 2]) for b in two]
        slot_in = [sb(f"slot_in{b}", [128, ST, D]) for b in two]

        weights_in = sem("weights_in")
        prep = sem("prep")
        phi_rstd = sem("phi_rstd")
        phi_ready = sem("phi_ready")
        veps_done = sem("veps_done")
        rstd_done = sem("rstd_done")
        xn_done = sem("xn_done")
        xnT_psum = sem("xnT_psum")
        xnT_done = sem("xnT_done")
        logits_psum = sem("logits_psum")
        peaks_done = sem("peaks_done")
        col_row_psum = sem("col_row_psum")
        col_row_done = sem("col_row_done")
        shifted_psum = sem("shifted_psum")
        exp_done = sem("exp_done")
        slots_psum = sem("slots_psum")
        sveps_done = sem("sveps_done")
        srstd_done = sem("srstd_done")
        slots_done = sem("slots_done")
        stored = [sem("stored0"), sem("stored1")]
        dve_steps = sem("dve_steps")
        block = ctx.enter_context(nc.Block())

        @block.sync
        def _(sp):
            sp.dma_start(phi[:], a["phi"]).then_inc(weights_in, 16)
            sp.dma_start(mhalf[:], a["mhalf"]).then_inc(weights_in, 16)
            sp.dma_start(ident[:], a["ident"]).then_inc(weights_in, 16)
            with sp.Fori(0, PAIRS) as i:
                for b in two:
                    sp.wait_ge(slots_done, i * 8 + (6 + b + 1))
                    sp.dma_start(slots_dram[:, i * 2 + b], slot_in[b][:].rearrange("p j d -> p (j d)")).then_inc(stored[b], 16)
            for b in two:
                sp.wait_ge(stored[b], 16 * PAIRS + 16)

        @block.gpsimd
        def _(pool):
            pool.wait_ge(prep, 1)
            nc.gpsimd.tensor_tensor(phi_sum[:].rearrange("p c j r -> p (c j r)")[:, 0:16], phi_sum[:].rearrange("p c j r -> p (c j r)")[:, 0:16],
                                    mhalf[0:DP, 0:16], ALU.pow)
            nc.gpsimd.tensor_tensor(phi_sum[:].rearrange("p c j r -> p (c j r)")[:, 16:32], phi_sum[:].rearrange("p c j r -> p (c j r)")[:, 16:32],
                                    mhalf[0:DP, 0:16], ALU.pow).then_inc(phi_rstd, 1)
            with pool.Fori(0, PAIRS) as i:
                for b in two:
                    pool.wait_ge(veps_done, i * 2 + (b + 1))
                    nc.gpsimd.tensor_tensor(rstd[b][:], veps[b][:], mhalf[0:TP, 0:TT], ALU.pow).then_inc(rstd_done, 1)
                for q in range(QUARTERS):
                    for b in two:
                        pool.wait_ge(sveps_done, i * 8 + (2 * q + b + 1))
                        nc.gpsimd.tensor_tensor(srstd[b][:], sveps[b][:], mhalf[:, 0:2], ALU.pow).then_inc(srstd_done, 1)

        @block.tensor
        def _(pe):
            pe.wait_ge(phi_ready, 1)
            with pe.Fori(0, PAIRS) as i:
                def slot_sums(q, b):
                    pe.wait_ge(exp_done, i * 8 + (2 * q + b + 1))
                    if q > 0:
                        pe.wait_ge(slots_done, i * 8 + (2 * (q - 1) + b + 1))
                    for s in range(2):
                        for t in range(TT):
                            mm = nc.tensor.matmul(ps[0:128, 4 * b + 2, s * (D + 1):(s + 1) * (D + 1)],
                                                  weights[b][:, t, s * 128:(s + 1) * 128], xn[b][:, t], start=t == 0, stop=t == 1)
                    mm.then_inc(slots_psum, 1)

                for b in two:
                    pe.wait_ge(xn_done, i * 2 + (b + 1))
                    transposes_pe(nc, xn[b], ps[:, 4 * b + 3], ident, xnT_psum)
                for q in range(QUARTERS):
                    for b in two:
                        if q == 0:
                            pe.wait_ge(xnT_done, i * 2 + (b + 1))
                        else:
                            pe.wait_ge(exp_done, i * 8 + (2 * (q - 1) + b + 1))
                        for s in range(2):
                            for c in range(DC):
                                nc.tensor.matmul(ps[0:128, 4 * b, s * TOKENS:(s + 1) * TOKENS],
                                                 phi[:, c, (2 * q + s) * 128:(2 * q + s + 1) * 128], xnT[b][:, c],
                                                 start=c == 0, stop=c == 1)
                        for t in range(TT):
                            for c in range(DC):
                                mm = nc.tensor.matmul(ps[0:TP, 4 * b + 1, t * QW:(t + 1) * QW], xnT[b][:, c, t * TP:(t + 1) * TP],
                                                      phi[:, c, q * QW:(q + 1) * QW], start=t == 0 and c == 0, stop=c == 1,
                                                      skip_group_check=True)
                        mm.then_inc(logits_psum, 1)
                    for b in two:
                        pe.wait_ge(peaks_done, i * 8 + (2 * q + b + 1))
                        for s in range(2):
                            mm = nc.tensor.transpose(ps[0:2, 4 * b + 3, 0:128].bitcast(BF16)[:, s * 128:(s + 1) * 128],
                                                     col_parts[b][:, s], ident_b[:])
                        mm.then_inc(col_row_psum, 1)
                        if q > 0:
                            slot_sums(q - 1, b)
                    for b in two:
                        pe.wait_ge(col_row_done, i * 8 + (2 * q + b + 1))
                        for t in range(TT):
                            mm = nc.tensor.matmul(ps[0:TP, 4 * b + 1, t * QW:(t + 1) * QW], ones[:], col_row[b][:],
                                                  start=False, stop=True, skip_group_check=True)
                        mm.then_inc(shifted_psum, 1)
                for b in two:
                    slot_sums(QUARTERS - 1, b)

        @block.scalar
        def _(act):
            with act.Fori(0, PAIRS) as i:
                for b in two:
                    act.wait_ge(xnT_psum, i * 2 + (b + 1))
                    nc.scalar.copy(xnT[b][:].rearrange("p c t -> p (c t)"), ps[0:DP, 4 * b + 3, 0:DC * TOKENS]).then_inc(xnT_done, 1)
                for q in range(QUARTERS):
                    for b in two:
                        act.wait_ge(shifted_psum, i * 8 + (2 * q + b + 1))
                        nc.scalar.activation(weights[b][:].rearrange("p t s -> p (t s)"), ps[0:TP, 4 * b + 1, 0:TT * QW], ACT.Exp)\
                          .then_inc(exp_done, 1)

        @block.vector
        def _(dve):
            for b in two:
                nc.vector.memset(xn[b][:], 1.0)
            nc.vector.memset(ones[:], 1.0)
            dve.wait_ge(weights_in, 48)
            own = Steps(dve, dve_steps, 0)
            nc.vector.tensor_copy(ident_b[:], ident[:])
            own.done(nc.vector.tensor_tensor(phi_sq[:], phi[:], phi[:], ALU.mult))
            own.settle()
            for c in range(DC):
                own.done(nc.vector.tensor_reduce(phi_sum[:, c], phi_sq[:, c].rearrange("p (j n r) -> p j r n", j=ST, r=2), AX_X, ALU.add))
            own.settle()
            nc.vector.tensor_scalar(phi_sum[:], phi_sum[:], PHI_EPS, None, ALU.add).then_inc(prep, 1)
            dve.wait_ge(phi_rstd, 1)
            for c in range(DC):
                v = phi[:, c].rearrange("p (j n r) -> p j n r", j=ST, r=2)
                ins = nc.vector.tensor_tensor(v, v, phi_sum[:, c].unsqueeze(2).to_broadcast([DP, ST, SLOTS // ST // 2, 2]), ALU.mult)
            own.done(ins)
            own.settle()
            dve.sem_inc(phi_ready, 1)
            dve.sem_inc(stored[0], 16)
            dve.sem_inc(stored[1], 16)
            before = own.n

            with dve.Fori(0, PAIRS) as i:
                own = Steps(dve, dve_steps, i * DIS_STEPS_DVE + before)

                def slot_stats(q, b):
                    dve.wait_ge(slots_psum, i * 8 + (2 * q + b + 1))
                    raw = ps[0:128, 4 * b + 2, 0:2 * (D + 1)].rearrange("p (s d) -> p s d", s=2)
                    for s in range(2):
                        nc.vector.bn_stats(sstats[b][:, s], raw[:, s, 0:D])
                    own.done(nc.vector.tensor_copy(sden[b][:], raw[:, :, D]))
                    own.settle()
                    own.done(nc.vector.tensor_tensor(sden[b][:], sden[b][:], sden[b][:], ALU.mult))
                    for s in range(2):
                        ins = nc.vector.bn_aggr(smv[b][:, s], sstats[b][:, s])
                    own.done(ins)
                    own.settle()
                    nc.vector.scalar_tensor_tensor(sveps[b][:], sden[b][:], LN_EPS, smv[b][:, :, 1], ALU.mult, ALU.add)\
                      .then_inc(sveps_done, 1)

                def slot_norm(q, b):
                    dve.wait_ge(srstd_done, i * 8 + (2 * q + b + 1))
                    if q == 0:
                        dve.wait_ge(stored[b], i * 16 + 16)
                    for s in range(2):
                        ins = nc.vector.tensor_scalar(slot_in[b][:, 2 * q + s], ps[0:128, 4 * b + 2, s * (D + 1):s * (D + 1) + D],
                                                      smv[b][:, s, 0:1], srstd[b][:, s:s + 1], ALU.subtract, ALU.mult)
                    ins.then_inc(slots_done, 1)

                for b in two:
                    layernorm_dve(nc, dve, own, H, i * 2 + b, stats[b], mv[b], veps[b], veps_done)
                for b in two:
                    dve.wait_ge(rstd_done, i * 2 + (b + 1))
                    normalise_dve(nc, H, i * 2 + b, mv[b], rstd[b], xn[b], xn_done)
                for q in range(QUARTERS):
                    for b in two:
                        dve.wait_ge(logits_psum, i * 8 + (2 * q + b + 1))
                        own.done(nc.vector.tensor_reduce(col_peak[b][:], ps[0:128, 4 * b, 0:2 * TOKENS].rearrange("p (s t) -> p s t", s=2),
                                                         AX_X, ALU.max, negate=True))
                        own.settle()
                        own.done(nc.vector.tensor_copy(col_parts[b][:, :, 0], col_peak[b][:]))
                        nc.vector.tensor_reduce(row_peak[b][:, :, q], ps[0:TP, 4 * b + 1, 0:TT * QW].rearrange("p (t s) -> p t s", t=TT),
                                                AX_X, ALU.max)
                        own.settle()
                        nc.vector.tensor_tensor(col_parts[b][:, :, 1], col_peak[b][:], col_parts[b][:, :, 0], ALU.subtract)\
                          .then_inc(peaks_done, 1)
                    for b in two:
                        dve.wait_ge(col_row_psum, i * 8 + (2 * q + b + 1))
                        nc.vector.tensor_copy(col_row[b][:], ps[0:2, 4 * b + 3, 0:128].bitcast(BF16)).then_inc(col_row_done, 1)
                    if q > 0:
                        for b in two:
                            slot_stats(q - 1, b)
                        for b in two:
                            slot_norm(q - 1, b)
                for b in two:
                    dve.wait_ge(peaks_done, i * 8 + (6 + b + 1))
                    nc.vector.tensor_reduce(neg_row_max[:, i * 2 + b], row_peak[b][:], AX_X, ALU.max, negate=True)
                    slot_stats(QUARTERS - 1, b)
                for b in two:
                    slot_norm(QUARTERS - 1, b)
                assert own.n == DIS_STEPS_DVE, own.n


SOFT_EXPERTS = 64
ROWS = 128 * ST
HALF = ROWS // 2
HID = 2 * D
HC = HID // 128


def experts_stage(nc, a, ident, slots_dram, outs_dram):
    PAIRS_E = SOFT_EXPERTS // 2
    with ExitStack() as ctx:
        st = Stage(nc, ctx, "exp")
        sb, sem = st.sb, st.sem
        ps = ctx.enter_context(nc.psum_tensor("exp_psum", [128, 8, 512], F32))
        two = range(2)

        gain = sb("gain", [DP, SOFT_EXPERTS, DC])
        shift = sb("shift", [DP, SOFT_EXPERTS, DC])
        w_1 = [sb(f"w_1{b}", [DP + 1, DC, HID]) for b in two]
        w_2 = [sb(f"w_2{b}", [128, HC, D]) for b in two]
        b_2 = [sb(f"b_2{b}", [128, D]) for b in two]
        x = [sb(f"x{b}", [128, ST, D]) for b in two]
        xT = [[sb(f"xT{b}{h}", [DP + 1, DC, HALF]) for h in two] for b in two]
        hid = [sb(f"hid{h}", [128, HC, HALF]) for h in two]
        y = [sb(f"y{b}", [128, ST, D]) for b in two]

        ident_in = sem("ident_in")
        vectors_in = sem("vectors_in")
        loaded = [sem("loaded0"), sem("loaded1")]
        xT_psum = sem("xT_psum")
        xT_done = sem("xT_done")
        hid_psum = sem("hid_psum")
        hid_done = sem("hid_done")
        y_psum = sem("y_psum")
        y_done = sem("y_done")
        stored = [sem("stored0"), sem("stored1")]
        x_dram = slots_dram.rearrange("(e r) n f -> e (r n) f", r=2)
        y_dram = outs_dram.rearrange("(e r) n f -> e (r n) f", r=2)
        block = ctx.enter_context(nc.Block())

        @block.sync
        def _(sp):
            sp.dma_start(ident[:], a["ident"]).then_inc(ident_in, 16)
            sp.dma_start(gain[:], a["ln_g"]).then_inc(vectors_in, 16)
            sp.dma_start(shift[:], a["ln_b"]).then_inc(vectors_in, 16)

            def load(b, e):
                sp.dma_start(x[b][:].rearrange("p j d -> p (j d)"),
                             x_dram[e]).then_inc(loaded[b], 16)
                sp.dma_start(w_1[b][0:DP], a["soft_w1"][e]).then_inc(loaded[b], 16)
                sp.dma_start(w_1[b][DP:DP + 1, 0], a["soft_b1"][e]).then_inc(loaded[b], 16)
                sp.dma_start(w_2[b][:], a["soft_w2"][e]).then_inc(loaded[b], 16)
                sp.dma_start(b_2[b][:], a["soft_b2"][e].partition_broadcast(128).rearrange("p o d -> p (o d)"))\
                  .then_inc(loaded[b], 16)

            for b in two:
                load(b, b)
            def store(b, i):
                sp.wait_ge(y_done, i * 4 + (2 * b + 3))
                sp.dma_start(y_dram[i * 2 + b], y[b][:].rearrange("p j d -> p (j d)")).then_inc(stored[b], 16)

            with sp.Fori(0, PAIRS_E - 1) as i:
                for b in two:
                    store(b, i)
                    load(b, i * 2 + (b + 2))
            for b in two:
                store(b, PAIRS_E - 1)
                sp.wait_ge(stored[b], 16 * PAIRS_E + 16)

        @block.tensor
        def _(pe):
            def turn(b, h, k):
                if h == 0:
                    pe.wait_ge(loaded[b], (k - 2 * b) * 20 + 80)
                if not (isinstance(k, int) and k == 0):
                    pe.wait_ge(xT_done, k)
                for c in range(DC):
                    for j in range(4):
                        mm = nc.tensor.transpose(ps[0:DP, c, j * 128:(j + 1) * 128], x[b][:, 4 * h + j, c * DP:(c + 1) * DP], ident[:])
                mm.then_inc(xT_psum, 1)

            def hidden(b, h, k):
                pe.wait_ge(xT_done, k + 1)
                for m in range(HC):
                    pe.wait_ge(hid_done, k * HC + (m + 1))
                    for c in range(DC):
                        K = DP + 1 - c
                        mm = nc.tensor.matmul(ps[0:128, 2 + m], w_1[b][0:K, c, m * 128:(m + 1) * 128], xT[b][h][0:K, c],
                                              start=c == 0, stop=c == 1)
                    mm.then_inc(hid_psum, 1)

            def output(b, h, k):
                pe.wait_ge(hid_done, k * HC + 2 * HC)
                pe.wait_ge(y_done, k + 1)
                for j in range(4):
                    for m in range(HC):
                        mm = nc.tensor.matmul(ps[0:128, 5 + j // 2, (j % 2) * D:(j % 2 + 1) * D],
                                              hid[h][:, m, j * 128:(j + 1) * 128], w_2[b][:, m], start=m == 0, stop=m == HC - 1)
                mm.then_inc(y_psum, 1)

            def pair(i, last):
                for b in two:
                    k = i * 4 + 2 * b
                    turn(b, 1, k + 1)
                    hidden(b, 0, k)
                    hidden(b, 1, k + 1)
                    output(b, 0, k)
                    if not (last and b == 1):
                        turn(1 - b, 0, k + 2)
                    output(b, 1, k + 1)

            pe.wait_ge(ident_in, 16)
            turn(0, 0, 0)
            with pe.Fori(0, PAIRS_E - 1) as i:
                pair(i, False)
            pair(PAIRS_E - 1, True)

        @block.scalar
        def _(act):
            act.sem_inc(hid_done, HC)
            with act.Fori(0, PAIRS_E) as i:
                for b in two:
                    for h in two:
                        for m in range(HC):
                            act.wait_ge(hid_psum, i * (4 * HC) + ((2 * b + h) * HC + m + 1))
                            nc.scalar.activation(hid[h][:, m], ps[0:128, 2 + m], ACT.Gelu)\
                              .then_inc(hid_done, 1)

        @block.vector
        def _(dve):
            def take_xT(b, h, e, k):
                dve.wait_ge(xT_psum, k + 1)
                for c in range(DC):
                    ins = nc.vector.tensor_scalar(xT[b][h][0:DP, c], ps[0:DP, c], gain[:, e, c:c + 1], shift[:, e, c:c + 1], ALU.mult, ALU.add)
                ins.then_inc(xT_done, 1)

            def take_y(b, h, i, k):
                dve.wait_ge(y_psum, k + 1)
                if h == 0:
                    dve.wait_ge(stored[b], i * 16 + 16)
                for s in range(2):
                    ins = nc.vector.tensor_tensor(y[b][:, 4 * h + 2 * s:4 * h + 2 * s + 2],
                                                  ps[0:128, 5 + s, 0:2 * D].rearrange("p (j d) -> p j d", j=2),
                                                  b_2[b][:].unsqueeze(1).to_broadcast([128, 2, D]), ALU.add)
                ins.then_inc(y_done, 1)

            def pair(i, last):
                for b in two:
                    k = i * 4 + 2 * b
                    take_xT(b, 1, i * 2 + b, k + 1)
                    take_y(b, 0, i, k)
                    if not (last and b == 1):
                        take_xT(1 - b, 0, i * 2 + (b + 1), k + 2)
                    take_y(b, 1, i, k + 1)

            dve.wait_ge(vectors_in, 32)
            for b in two:
                for h in two:
                    nc.vector.memset(xT[b][h][DP:DP + 1], 1.0)
            dve.sem_inc(y_done, 1)
            dve.sem_inc(stored[0], 16)
            dve.sem_inc(stored[1], 16)
            take_xT(0, 0, 0, 0)
            with dve.Fori(0, PAIRS_E - 1) as i:
                pair(i, False)
            pair(PAIRS_E - 1, True)


def combine_stage(nc, a, H, ident, phi, neg_row_max, outs_dram, out):
    COM_STEPS_DVE = 10
    with ExitStack() as ctx:
        st = Stage(nc, ctx, "com")
        sb, sem = st.sb, st.sem
        ps = ctx.enter_context(nc.psum_tensor("com_psum", [128, 8, 512], F32))
        two = range(2)

        mhalf = sb("mhalf", [TP, TT])
        ident_b = sb("ident_b", [TP, TP], BF16)
        ones = sb("ones", [2, 128], BF16)
        xn = [sb(f"xn{b}", [TP, TT, D]) for b in two]
        xnT = [sb(f"xnT{b}", [DP, DC, TOKENS]) for b in two]
        stats = [sb(f"stats{b}", [TP, TT, 6]) for b in two]
        mv = [sb(f"mv{b}", [TP, TT, 2]) for b in two]
        veps = [sb(f"veps{b}", [TP, TT]) for b in two]
        rstd = [sb(f"rstd{b}", [TP, TT]) for b in two]
        parts = [sb(f"parts{b}", [TP, TT, 2], BF16) for b in two]
        row = [sb(f"row{b}", [2, TOKENS], BF16) for b in two]
        weights = [[sb(f"weights{b}{q}", [128, 2, TOKENS]) for q in two] for b in two]
        y = [sb(f"y{b}", [128, ST, D + 1]) for b in two]
        rden = [sb(f"rden{b}", [TP, TT]) for b in two]
        res = [sb(f"res{b}", [TP, TT, D]) for b in two]

        consts_in = sem("consts_in")
        ready = sem("ready")
        y_in = [sem("y_in0"), sem("y_in1")]
        veps_done = sem("veps_done")
        rstd_done = sem("rstd_done")
        xn_done = sem("xn_done")
        parts_done = sem("parts_done")
        xnT_psum = sem("xnT_psum")
        xnT_done = sem("xnT_done")
        row_psum = sem("row_psum")
        row_done = sem("row_done")
        shifted_psum = sem("shifted_psum")
        exp_done = sem("exp_done")
        mixed = sem("mixed")
        res_done = sem("res_done")
        stored = [sem("stored0"), sem("stored1")]
        dve_steps = sem("dve_steps")
        block = ctx.enter_context(nc.Block())

        @block.sync
        def _(sp):
            sp.dma_start(ident[:], a["ident"]).then_inc(consts_in, 16)
            sp.dma_start(mhalf[:], a["mhalf"][0:TP, 0:TT]).then_inc(consts_in, 16)

            def load(b, n):
                sp.dma_start(y[b][:, :, 0:D], outs_dram[:, n].rearrange("p (j d) -> p j d", j=ST)).then_inc(y_in[b], 16)

            sp.wait_ge(ready, 1)
            for b in two:
                load(b, b)
            def store(b, i):
                sp.wait_ge(res_done, i * 2 + (b + 3))
                sp.dma_start(out[i * 2 + b].rearrange("(t p) d -> p t d", t=TT), res[b][:]).then_inc(stored[b], 16)

            with sp.Fori(0, PAIRS - 1) as i:
                for b in two:
                    sp.wait_ge(mixed, i * 2 + (b + 1))
                    load(b, i * 2 + (b + 2))
                for b in two:
                    store(b, i)
            for b in two:
                store(b, PAIRS - 1)
                sp.wait_ge(stored[b], 16 * PAIRS + 16)

        @block.gpsimd
        def _(pool):
            pool.wait_ge(consts_in, 32)
            with pool.Fori(0, PAIRS) as i:
                for b in two:
                    pool.wait_ge(veps_done, i * 2 + (b + 1))
                    nc.gpsimd.tensor_tensor(rstd[b][:], veps[b][:], mhalf[:], ALU.pow).then_inc(rstd_done, 1)

        @block.tensor
        def _(pe):
            pe.wait_ge(ready, 1)
            with pe.Fori(0, PAIRS) as i:
                def mix(q, b):
                    pe.wait_ge(exp_done, i * 8 + (2 * q + b + 1))
                    if q == 0:
                        pe.wait_ge(y_in[b], i * 16 + 16)
                        pe.wait_ge(res_done, i * 2 + (b + 1))
                    for t in range(TT):
                        for s in range(2):
                            j = 2 * q + s
                            mm = nc.tensor.matmul(ps[0:TP, 4 * b + 2, t * (D + 1):(t + 1) * (D + 1)],
                                                  weights[b][q % 2][:, s, t * TP:(t + 1) * TP], y[b][:, j],
                                                  start=j == 0 and t == 0, stop=j == ST - 1, skip_group_check=True)
                    if q == QUARTERS - 1:
                        mm.then_inc(mixed, 1)

                for b in two:
                    pe.wait_ge(xn_done, i * 2 + (b + 1))
                    transposes_pe(nc, xn[b], ps[:, 4 * b + 3], ident, xnT_psum)
                for b in two:
                    pe.wait_ge(xnT_done, i * 2 + (b + 1))
                    pe.wait_ge(parts_done, i * 2 + (b + 1))
                    for t in range(TT):
                        mm = nc.tensor.transpose(ps[0:2, 4 * b + 3, 0:TP].bitcast(BF16)[:, t * TP:(t + 1) * TP], parts[b][:, t], ident_b[:])
                    mm.then_inc(row_psum, 1)
                for q in range(QUARTERS):
                    for b in two:
                        if q == 0:
                            pe.wait_ge(row_done, i * 2 + (b + 1))
                        for s in range(2):
                            j = 2 * q + s
                            o = ps[0:128, 4 * b + q % 2, s * TOKENS:(s + 1) * TOKENS]
                            for c in range(DC):
                                nc.tensor.matmul(o, phi[:, c, j * 128:(j + 1) * 128], xnT[b][:, c], start=c == 0, stop=False)
                            mm = nc.tensor.matmul(o, ones[:], row[b][:], start=False, stop=True)
                        mm.then_inc(shifted_psum, 1)
                    if q > 0:
                        for b in two:
                            mix(q - 1, b)
                for b in two:
                    mix(QUARTERS - 1, b)

        @block.scalar
        def _(act):
            with act.Fori(0, PAIRS) as i:
                for b in two:
                    act.wait_ge(xnT_psum, i * 2 + (b + 1))
                    nc.scalar.copy(xnT[b][:].rearrange("p c t -> p (c t)"), ps[0:DP, 4 * b + 3, 0:DC * TOKENS]).then_inc(xnT_done, 1)
                for q in range(QUARTERS):
                    for b in two:
                        act.wait_ge(shifted_psum, i * 8 + (2 * q + b + 1))
                        nc.scalar.activation(weights[b][q % 2][:].rearrange("p s t -> p (s t)"),
                                             ps[0:128, 4 * b + q % 2, 0:2 * TOKENS], ACT.Exp).then_inc(exp_done, 1)

        @block.vector
        def _(dve):
            dve.wait_ge(consts_in, 32)
            nc.vector.memset(ones[:], 1.0)
            nc.vector.tensor_copy(ident_b[:], ident[0:TP, 0:TP])
            nc.vector.memset(y[0][:], 1.0)
            nc.vector.memset(y[1][:], 1.0).then_inc(ready, 1)
            dve.sem_inc(res_done, 2)
            dve.sem_inc(stored[0], 16)
            dve.sem_inc(stored[1], 16)
            with dve.Fori(0, PAIRS) as i:
                own = Steps(dve, dve_steps, i * COM_STEPS_DVE)
                for b in two:
                    layernorm_dve(nc, dve, own, H, i * 2 + b, stats[b], mv[b], veps[b], veps_done)
                for b in two:
                    own.done(nc.vector.tensor_copy(parts[b][:, :, 0], neg_row_max[:, i * 2 + b]))
                    own.settle()
                    nc.vector.tensor_tensor(parts[b][:, :, 1], neg_row_max[:, i * 2 + b], parts[b][:, :, 0], ALU.subtract)\
                      .then_inc(parts_done, 1)
                for b in two:
                    dve.wait_ge(rstd_done, i * 2 + (b + 1))
                    normalise_dve(nc, H, i * 2 + b, mv[b], rstd[b], xn[b], xn_done)
                for b in two:
                    dve.wait_ge(row_psum, i * 2 + (b + 1))
                    nc.vector.tensor_copy(row[b][:], ps[0:2, 4 * b + 3, 0:TP].bitcast(BF16)).then_inc(row_done, 1)
                for b in two:
                    dve.wait_ge(mixed, i * 2 + (b + 1))
                    acc = ps[0:TP, 4 * b + 2, 0:TT * (D + 1)].rearrange("p (t d) -> p t d", t=TT)
                    own.done(nc.vector.reciprocal(rden[b][:], acc[:, :, D]))
                    own.settle()
                    dve.wait_ge(stored[b], i * 16 + 16)
                    for t in range(TT):
                        ins = nc.vector.scalar_tensor_tensor(res[b][:, t], acc[:, t, 0:D], rden[b][:, t:t + 1],
                                                             H[:, i * 2 + b, t * D:(t + 1) * D], ALU.mult, ALU.add)
                    ins.then_inc(res_done, 1)
                assert own.n == COM_STEPS_DVE, own.n


def build(nc, a, out):
    slots_dram = nc.dram_tensor("slots", (128, IMAGES, ST * D), F32, kind="Internal").ap()
    outs_dram = nc.dram_tensor("slot_outs", (128, IMAGES, ST * D), F32, kind="Internal").ap()
    with (
        nc.sbuf_tensor("h", [TP, IMAGES, TT * D], F32) as H,
        nc.sbuf_tensor("ident", [128, 128], F32) as ident,
        nc.sbuf_tensor("phi", [DP, DC, SLOTS], F32) as phi,
        nc.sbuf_tensor("neg_row_max", [TP, IMAGES, TT], F32) as neg_row_max,
    ):
        ttt_stage(nc, a, H, ident)
        moe_stage(nc, a, H, ident)
        attention_stage(nc, a, H, ident)
        dispatch_stage(nc, a, H, ident, phi, neg_row_max, slots_dram)
        experts_stage(nc, a, ident, slots_dram, outs_dram)
        combine_stage(nc, a, H, ident, phi, neg_row_max, outs_dram, out)


def laid_out(np, v):
    f = {k: np.asarray(x) for k, x in v.items()}
    c = np.ascontiguousarray

    def chunks(w):
        return c(w.reshape(DC, DP, *w.shape[1:]).swapaxes(0, 1))

    def row(x):
        return c(x.reshape(1, -1))

    x = f["x"].reshape(IMAGES, GRID, PATCH, GRID, PATCH).transpose(0, 2, 4, 1, 3)
    qkv = f["L0_attn_qkv_weight"].reshape(3, D, D)
    slots = 128 * 8
    phi = f["L1_ffn_phi"].reshape(128, 8, D).transpose(2, 1, 0).reshape(D, slots)
    return {
        "patches": c(x.reshape(IMAGES, 2, 128, TOKENS).transpose(0, 2, 1, 3)),
        "tok_wT": c(f["L0_tok_W"].T.reshape(2, 128, D).transpose(1, 0, 2)),
        "qkv": c(qkv.reshape(3, DC, DP, D).transpose(2, 0, 1, 3)),
        "qkv_T": c(qkv.transpose(0, 2, 1).reshape(3, DC, DP, D).transpose(2, 0, 1, 3)),
        "q_bias": row(f["L0_attn_q_bias"]),
        "q_bias_col": chunks(f["L0_attn_q_bias"]),
        "v_bias": row(f["L0_attn_v_bias"]),
        "lr_wT": chunks(f["L0_attn_ttt_lr_weight"].reshape(HEADS, D).T),
        "lr_bias": row(f["L0_attn_ttt_lr_bias"]),
        "proj_T": chunks(f["L0_attn_proj_weight"].T),
        "proj_bias": row(f["L0_attn_proj_bias"]),
        "ttt_gamma": row(f["L0_attn_ttt_norm_weight"]),
        "ttt_gamma_col": chunks(f["L0_attn_ttt_norm_weight"].reshape(D)),
        "ttt_beta": row(f["L0_attn_ttt_norm_bias"]),
        "ttt_beta_col": chunks(f["L0_attn_ttt_norm_bias"].reshape(D)),
        "W1": f["L0_attn_W1"],
        "b1": c(f["L0_attn_b1"].reshape(1, DC, DP)),
        "router_w": chunks(f["L0_ffn_router_w"]),
        "router_b": row(f["L0_ffn_router_b"]),
        "moe_w1": c(f["L0_ffn_w1"].reshape(4, DC, DP, D).transpose(2, 1, 0, 3)),
        "moe_b1": c(f["L0_ffn_b1"].reshape(1, 4, D)),
        "moe_w2": c(f["L0_ffn_w2"].reshape(4, DC, DP, D).transpose(2, 1, 0, 3)),
        "moe_b2": c(f["L0_ffn_b2"].reshape(1, 4, D)),
        "norm_scale": chunks(f["L1_attn_norm_scale"]),
        "norm_bias": chunks(f["L1_attn_norm_bias"]),
        "attn_w": chunks(f["L1_attn_W_attn"]),
        "attn_b": row(f["L1_attn_b_attn"]),
        "attn_pw": chunks(f["L1_attn_W_proj"]),
        "attn_pb": row(f["L1_attn_b_proj"]),
        "sinks": row(f["L1_attn_sinks"]),
        "rezero": row(f["L1_attn_rezero"]),
        "phi": chunks(phi),
        "ln_g": c(f["L1_ffn_ln_g"].reshape(64, DC, DP).transpose(2, 0, 1)),
        "ln_b": c(f["L1_ffn_ln_b"].reshape(64, DC, DP).transpose(2, 0, 1)),
        "soft_w1": c(f["L1_ffn_w1"].reshape(64, DC, DP, 2 * D).transpose(0, 2, 1, 3)),
        "soft_b1": f["L1_ffn_b1"].reshape(64, 1, 2 * D),
        "soft_w2": c(f["L1_ffn_w2"].reshape(64, 3, 128, D).transpose(0, 2, 1, 3)),
        "soft_b2": f["L1_ffn_b2"].reshape(64, 1, D),
    }


def constants(np):
    r = np.arange(DP + 1)
    head_mask = (r[:, None] // HD == r[None, :DP] // HD) | (r[:, None] == DP)
    ang = np.outer(np.arange(TOKENS), 1.0 / 10000.0 ** (np.arange(0, HD, 2, dtype=np.float32) / HD)).astype(np.float32)
    cos = np.repeat(np.cos(ang), 2, axis=1).reshape(TT, TP, HD).transpose(1, 0, 2)
    sin = np.stack([-np.sin(ang), np.sin(ang)], axis=2).reshape(TT, TP, HD).transpose(1, 0, 2)
    k, q = np.arange(TP)[:, None], np.arange(TP)[None, :]
    rows, heads = np.arange(96)[:, None], np.arange(HEADS)[None, :]
    head_sel = (rows // 32 == heads % 3) & ((rows % 32 == heads) | (rows % 32 == heads + HEADS))
    return {
        "ident": np.eye(128, dtype=np.float32),
        "head_mask": head_mask.astype(np.float32),
        "mhalf": np.full((128, 24), -0.5, np.float32),
        "rope_cos": np.ascontiguousarray(cos.astype(np.float32)),
        "rope_sin": np.ascontiguousarray(sin.astype(np.float32)),
        "head_sel": np.ascontiguousarray(np.repeat(head_sel[:, :, None], TP, axis=2).astype(np.float32)),
        "mask_kq": np.where(k > q, np.float32(-1e30), np.float32(0.0)).astype(np.float32),
        "mask_qk": np.where(q > k, np.float32(-1e30), np.float32(0.0)).astype(np.float32),
    }


def kernel(**inputs):
    import numpy as _np
    import concourse.bacc as _bacc
    from concourse import mybir as _mybir
    from concourse.bass_utils import run_bass_kernel_spmd as _run

    nc = _bacc.Bacc("TRN2", target_bir_lowering=False, num_devices=1)
    data, aps = {}, {}
    for name, array in {**laid_out(_np, inputs), **constants(_np)}.items():
        data[f"in_{name}"] = array
        aps[name] = nc.dram_tensor(f"in_{name}", array.shape, _mybir.dt.from_np(array.dtype), kind="ExternalInput").ap()
    out = nc.dram_tensor("out", (IMAGES, TOKENS, D), F32, kind="ExternalOutput").ap()
    build(nc, aps, out)
    r = _run(nc, [data], core_ids=[0])
    return r.results[0]["out"]
```

```python
from contextlib import ExitStack

import numpy as np

import concourse.bass as bass
from concourse import mybir

ALU = mybir.AluOpType
ACT = mybir.ActivationFunctionType
AX_X = mybir.AxisListType.X
F32 = mybir.dt.float32
BF16 = mybir.dt.bfloat16

IMAGES = 64
SIDE, PATCH = 224, 16
GRID = SIDE // PATCH
TOKENS = GRID * GRID
TT = 2
TP = TOKENS // TT
D = 192
DC = 2
DP = D // DC
HEADS, HD = 12, 16
PAIRS = IMAGES // 2
LN_EPS = 1e-5
TTT_EPS = 1e-6


class Steps:

    def __init__(self, eng, sem, before):
        self.eng, self.sem, self.before, self.n = eng, sem, before, 0

    def done(self, ins):
        ins.then_inc(self.sem, 1)
        self.n += 1

    def settle(self):
        self.eng.wait_ge(self.sem, self.before + self.n)


class Stage:

    def __init__(self, nc, ctx, name):
        self.nc, self.ctx, self.name = nc, ctx, name

    def sb(self, name, shape, dt=F32):
        return self.ctx.enter_context(self.nc.sbuf_tensor(f"{self.name}_{name}", shape, dt))

    def psum_banks(self, n=8):
        return [self.ctx.enter_context(self.nc.psum_tensor(f"{self.name}_bank{i}", [128, 512], F32)) for i in range(n)]

    def sem(self, name):
        return self.nc.alloc_semaphore(f"{self.name}_{name}")


def tiles(bank, rows, groups, width, pitch=None):
    pitch = pitch or width
    return bank[0:rows, 0:groups * pitch].rearrange("p (g w) -> p g w", g=groups)[:, :, 0:width]


def ttt_stage(nc, a, H, ident):
    TTT_STEPS_DVE = 28
    with ExitStack() as ctx:
        st = Stage(nc, ctx, "ttt")
        sb, sem = st.sb, st.sem
        banks = st.psum_banks()

        w_tok = sb("w_tok", [128, 2, D])
        w_in = sb("w_in", [DP + 1, DC, 3 * D + HEADS])
        w_qT = sb("w_qT", [DP + 1, DC, D])
        w_q = sb("w_q", [DP, DC, D + 1])
        w_k = sb("w_k", [DP, DC, D])
        w_kT = sb("w_kT", [DP + 1, DC, D])
        w_vT = sb("w_vT", [DP + 1, DC, D])
        w_pT = sb("w_pT", [DP, DC, D])
        w_pg = sb("w_pg", [DP, DC, D])
        w_qp = sb("w_qp", [DP + 1, DC, D])
        p_bias = sb("p_bias", [DP + 1, D])
        gamma_row = sb("gamma_row", [TP, D])
        gamma2 = sb("gamma2", [TP, D])
        gamma_col = sb("gamma_col", [DP, DC])
        beta_col = sb("beta_col", [DP, DC])
        q_col = sb("q_col", [DP, DC])
        w_1c = sb("w_1c", [DP + 1, DC, DP])
        head_mask = sb("head_mask", [DP + 1, D])
        sums = sb("sums", [DP + 1, HEADS])
        mhalf = sb("mhalf", [TP, 2 * HEADS])

        two = range(2)
        xp = [sb(f"xp{b}", [128, 2, TOKENS]) for b in two]
        xn = [sb(f"xn{b}", [TP, TT, D]) for b in two]
        xnT = [sb(f"xnT{b}", [DP + 1, DC, TOKENS]) for b in two]
        stats = [sb(f"stats{b}", [TP, TT, 6]) for b in two]
        mv = [sb(f"mv{b}", [TP, TT, 2]) for b in two]
        veps = [sb(f"veps{b}", [TP, TT]) for b in two]
        rstd = [sb(f"rstd{b}", [TP, TT]) for b in two]
        zt = [sb(f"zt{b}", [TP, TT, 2, D]) for b in two]
        k1 = [sb(f"k1{b}", [TP, TT, DC, DP + 1]) for b in two]
        qT = [sb(f"qT{b}", [DP + 1, DC, TOKENS]) for b in two]
        lr = [sb(f"lr{b}", [TP, TT, HEADS]) for b in two]
        coef = [sb(f"coef{b}", [TP, TT * HEADS]) for b in two]
        sq = [sb(f"sq{b}", [TP, TT, D]) for b in two]
        gvar = [sb(f"gvar{b}", [TP, TT * HEADS]) for b in two]
        grstd = [sb(f"grstd{b}", [TP, TT * HEADS]) for b in two]
        xh = [sb(f"xh{b}", [TP, TT, D]) for b in two]
        g = [sb(f"g{b}", [TP, TT, D]) for b in two]
        gx = [sb(f"gx{b}", [TP, TT, D]) for b in two]
        sgx = [sb(f"sgx{b}", [TP, TT * HEADS]) for b in two]
        gsum = [sb(f"gsum{b}", [DP + 1, HEADS]) for b in two]
        gc = [sb(f"gc{b}", [DP + 1, D]) for b in two]
        w_1n = [sb(f"w_1n{b}", [DP + 1, DC, DP]) for b in two]
        zb = [sb(f"zb{b}", [TP, TT, D]) for b in two]
        zbT = [sb(f"zbT{b}", [DP, DC, TOKENS]) for b in two]

        cleared = sem("cleared")
        weights_in = sem("weights_in")
        prep_dve = sem("prep_dve")
        prep_pe = sem("prep_pe")
        weights_ready = sem("weights_ready")
        x_in = [sem("x_in0"), sem("x_in1")]
        tok_done = sem("tok_done")
        h_kept = sem("h_kept")
        veps_done = sem("veps_done")
        rstd_done = sem("rstd_done")
        xn_done = sem("xn_done")
        xnT_psum = sem("xnT_psum")
        xnT_done = sem("xnT_done")
        proj_in_done = sem("proj_in_done")
        acts_in_done = sem("acts_in_done")
        sq_done = sem("sq_done")
        gvar_done = sem("gvar_done")
        grstd_done = sem("grstd_done")
        xh_done = sem("xh_done")
        g2x_done = sem("g2x_done")
        g_done = sem("g_done")
        gx_done = sem("gx_done")
        grad_in_done = sem("grad_in_done")
        grad_done = sem("grad_done")
        w1n_done = sem("w1n_done")
        zbar_psum = sem("zbar_psum")
        zbar_sq_done = sem("zbar_sq_done")
        zvar_done = sem("zvar_done")
        zrstd_done = sem("zrstd_done")
        zb_done = sem("zb_done")
        zbT_psum = sem("zbT_psum")
        zbT_done = sem("zbT_done")
        out_psum = sem("out_psum")
        h_added = sem("h_added")
        dve_steps = sem("dve_steps")
        act_steps = sem("act_steps")
        zbar_copied = sem("zbar_copied")

        WEIGHT_DMAS = 26 + HEADS
        block = ctx.enter_context(nc.Block())

        def grp(ap, n):
            return ap.rearrange("p t (h e) -> p (t h) e", e=HD) if n == 3 else ap.rearrange("p (h e) -> p h e", e=HD)

        @block.sync
        def _(sp):
            count = [0]

            def load(dst, src):
                sp.dma_start(dst, src).then_inc(weights_in, 16)
                count[0] += 1

            load(w_tok[:], a["tok_wT"])
            sp.dma_start(xp[0][:], a["patches"][0]).then_inc(x_in[0], 16)
            sp.dma_start(xp[1][:], a["patches"][1]).then_inc(x_in[1], 16)
            sp.wait_ge(cleared, 1)
            q_rows, k_rows = 0, 1
            load(w_in[0:DP, :, 2 * D:3 * D], a["qkv_T"][:, k_rows])
            load(w_in[0:DP, :, 3 * D:], a["lr_wT"])
            load(w_in[DP:DP + 1, 0, 3 * D:], a["lr_bias"])
            load(w_qT[0:DP], a["qkv_T"][:, q_rows])
            load(w_qT[DP:DP + 1, 0], a["q_bias"])
            load(w_q[:, :, 0:DP], a["qkv"][:, q_rows, :, 0:DP])
            load(w_q[:, :, DP + 1:], a["qkv"][:, q_rows, :, DP:])
            load(q_col[:], a["q_bias_col"])
            load(w_k[:], a["qkv"][:, k_rows])
            load(w_kT[0:DP], a["qkv_T"][:, k_rows])
            load(w_kT[DP:DP + 1, 0], a["ttt_beta"])
            load(w_kT[DP:DP + 1, 1], a["ttt_beta"])
            load(w_vT[0:DP], a["qkv_T"][:, 2])
            load(w_vT[DP:DP + 1, 0], a["v_bias"])
            load(w_vT[DP:DP + 1, 1], a["v_bias"])
            load(w_pT[:], a["proj_T"])
            load(p_bias[DP:DP + 1, :], a["proj_bias"])
            load(gamma_row[:], a["ttt_gamma"].partition_broadcast(TP).rearrange("p o d -> p (o d)"))
            load(gamma_col[:], a["ttt_gamma_col"])
            load(beta_col[:], a["ttt_beta_col"])
            for h in range(HEADS):
                c, r = h // 6, h % 6 * HD
                load(w_1c[r:r + HD, c, r:r + HD], a["W1"][h])
            load(w_1c[DP:DP + 1], a["b1"])
            load(head_mask[:, 0:DP], a["head_mask"])
            load(head_mask[:, DP:], a["head_mask"])
            load(ident[:], a["ident"])
            load(mhalf[:], a["mhalf"][0:TP, 0:2 * HEADS])
            assert count[0] == WEIGHT_DMAS, count
            with sp.Fori(0, PAIRS - 1) as i:
                for b in two:
                    sp.wait_ge(tok_done, i * 2 + (b + 1))
                    sp.dma_start(xp[b][:], a["patches"][i * 2 + (b + 2)]).then_inc(x_in[b], 16)

        @block.gpsimd
        def _(pool):
            pool.wait_ge(weights_ready, 1)
            with pool.Fori(0, PAIRS) as i:
                for b in two:
                    n1 = i * 2 + (b + 1)
                    pool.wait_ge(veps_done, n1)
                    nc.gpsimd.tensor_tensor(rstd[b][:], veps[b][:], mhalf[:, 0:TT], ALU.pow).then_inc(rstd_done, 1)
                for b in two:
                    n1 = i * 2 + (b + 1)
                    pool.wait_ge(gvar_done, n1)
                    nc.gpsimd.tensor_tensor(grstd[b][:], gvar[b][:], mhalf[:], ALU.pow).then_inc(grstd_done, 1)
                for b in two:
                    n1 = i * 2 + (b + 1)
                    pool.wait_ge(xh_done, n1)
                    nc.gpsimd.tensor_tensor(g[b][:, 0], xh[b][:, 0], gamma2[:], ALU.mult)
                    nc.gpsimd.tensor_tensor(g[b][:, 1], xh[b][:, 1], gamma2[:], ALU.mult).then_inc(g2x_done, 1)
                for b in two:
                    n1 = i * 2 + (b + 1)
                    pool.wait_ge(g_done, n1)
                    nc.gpsimd.tensor_tensor(gx[b][:], g[b][:], xh[b][:], ALU.mult).then_inc(gx_done, 1)
                for b in two:
                    n1 = i * 2 + (b + 1)
                    pool.wait_ge(zvar_done, n1)
                    nc.gpsimd.tensor_tensor(grstd[b][:], gvar[b][:], mhalf[:], ALU.pow).then_inc(zrstd_done, 1)

        @block.tensor
        def _(pe):
            pe.wait_ge(weights_in, 16 * WEIGHT_DMAS)
            pe.wait_ge(prep_dve, 1)
            for dc in range(DC):
                nc.tensor.matmul(banks[0][0:DP + 1, 0:D], w_q[:, dc, 0:DP + 1], w_pT[:, dc], start=dc == 0, stop=dc == 1)
            for dc in range(DC):
                mm = nc.tensor.matmul(banks[1][0:DP, 0:D], w_q[:, dc, DP + 1:], w_pT[:, dc], start=dc == 0, stop=dc == 1)
            mm.then_inc(prep_pe, 1)
            pe.wait_ge(prep_dve, 2)
            for ic in range(DC):
                for c in range(DC):
                    mm = nc.tensor.matmul(banks[2 + ic][0:DP, c * DP:(c + 1) * DP], w_k[:, c, ic * DP:(ic + 1) * DP],
                                          w_1c[0:DP, c], start=True, stop=True)
            mm.then_inc(prep_pe, 1)
            pe.wait_ge(weights_ready, 1)

            with pe.Fori(0, PAIRS) as i:
                def transposes(src, bank, b, signal):
                    for t in range(TT):
                        for c in range(DC):
                            mm = nc.tensor.transpose(bank[0:DP, c * TOKENS + t * TP:c * TOKENS + (t + 1) * TP],
                                                     src[b][:, t, c * DP:(c + 1) * DP], ident[0:TP, 0:TP])
                    mm.then_inc(signal, 1)

                for b in two:
                    pe.wait_ge(x_in[b], i * 16 + 16)
                    out = tiles(banks[4 * b], TP, TT, D)
                    for t in range(TT):
                        for c in range(2):
                            mm = nc.tensor.matmul(out[:, t], xp[b][:, c, t * TP:(t + 1) * TP], w_tok[:, c],
                                                  start=c == 0, stop=c == 1)
                    mm.then_inc(tok_done, 1)
                for b in two:
                    n1 = i * 2 + (b + 1)
                    pe.wait_ge(xn_done, n1)
                    transposes(xn, banks[4 * b + 1], b, xnT_psum)
                for b in two:
                    n1 = i * 2 + (b + 1)
                    pe.wait_ge(xnT_done, n1)
                    pe.wait_ge(h_added, n1)
                    for t in range(TT):
                        for c in range(DC):
                            K = DP + 1 - c
                            nc.tensor.matmul(banks[4 * b + 2 + t][0:TP, 0:2 * D], xnT[b][0:K, c, t * TP:(t + 1) * TP],
                                             w_in[0:K, c, 0:2 * D], start=c == 0, stop=c == 1)
                        for c in range(DC):
                            K = DP + 1 - c
                            nc.tensor.matmul(banks[4 * b][0:TP, t * (D + HEADS):(t + 1) * (D + HEADS)],
                                             xnT[b][0:K, c, t * TP:(t + 1) * TP], w_in[0:K, c, 2 * D:],
                                             start=c == 0, stop=c == 1)
                    for m in range(DC):
                        for c in range(DC):
                            K = DP + 1 - c
                            mm = nc.tensor.matmul(banks[4 * b + 1][0:DP, m * TOKENS:(m + 1) * TOKENS],
                                                  w_qT[0:K, c, m * DP:(m + 1) * DP], xnT[b][0:K, c],
                                                  start=c == 0, stop=c == 1)
                    mm.then_inc(proj_in_done, 1)
                for b in two:
                    n1 = i * 2 + (b + 1)
                    pe.wait_ge(grad_in_done, n1)
                    for c in range(DC):
                        for t in range(TT):
                            mm = nc.tensor.matmul(banks[4 * b][0:DP + 1, c * DP:(c + 1) * DP], k1[b][:, t, c],
                                                  g[b][:, t, c * DP:(c + 1) * DP], start=t == 0, stop=t == 1)
                    mm.then_inc(grad_done, 1)
                for b in two:
                    n1 = i * 2 + (b + 1)
                    pe.wait_ge(w1n_done, n1)
                    for t in range(TT):
                        for c in range(DC):
                            mm = nc.tensor.matmul(banks[4 * b + 1][0:TP, t * D + c * DP:t * D + (c + 1) * DP],
                                                  qT[b][:, c, t * TP:(t + 1) * TP], w_1n[b][:, c], start=True, stop=True)
                    mm.then_inc(zbar_psum, 1)
                for b in two:
                    n1 = i * 2 + (b + 1)
                    pe.wait_ge(zb_done, n1)
                    transposes(zb, banks[4 * b + 2], b, zbT_psum)
                for b in two:
                    n1 = i * 2 + (b + 1)
                    pe.wait_ge(zbT_done, n1)
                    for t in range(TT):
                        o = banks[4 * b + 3][0:TP, t * D:(t + 1) * D]
                        ts = slice(t * TP, (t + 1) * TP)
                        nc.tensor.matmul(o, xnT[b][0:DP + 1, 0, ts], w_qp[:, 0], start=True, stop=False)
                        nc.tensor.matmul(o, xnT[b][0:DP, 1, ts], w_qp[0:DP, 1], start=False, stop=False)
                        nc.tensor.matmul(o, zbT[b][:, 0, ts], w_pg[:, 0], start=False, stop=False)
                        mm = nc.tensor.matmul(o, zbT[b][:, 1, ts], w_pg[:, 1], start=False, stop=True)
                    mm.then_inc(out_psum, 1)

        @block.scalar
        def _(act):
            act.wait_ge(weights_ready, 1)
            with act.Fori(0, PAIRS) as i:
                for b in two:
                    n1 = i * 2 + (b + 1)
                    act.wait_ge(tok_done, n1)
                    nc.scalar.copy(H[:, i * 2 + b], banks[4 * b][0:TP, 0:TT * D]).then_inc(h_kept, 1)
                for b in two:
                    n1 = i * 2 + (b + 1)
                    act.wait_ge(xnT_psum, n1)
                    nc.scalar.copy(xnT[b][0:DP].rearrange("p c t -> p (c t)"),
                                   banks[4 * b + 1][0:DP, 0:DC * TOKENS]).then_inc(xnT_done, 1)
                for b in two:
                    n1 = i * 2 + (b + 1)
                    act.wait_ge(proj_in_done, n1)
                    for t in range(TT):
                        ins = nc.scalar.copy(zt[b][:, t].rearrange("p a d -> p (a d)"), banks[4 * b + 2 + t][0:TP, 0:2 * D])
                    ins.then_inc(act_steps, 1)
                    act.wait_ge(act_steps, n1)
                    nc.scalar.activation(sq[b][:], zt[b][:, :, 0], ACT.Square).then_inc(sq_done, 1)
                    kl = banks[4 * b][0:TP, 0:TT * (D + HEADS)].rearrange("p (t w) -> p t w", t=TT)
                    nc.scalar.activation(lr[b][:], kl[:, :, D:], ACT.Exp, scale=-1.0)
                    for t in range(TT):
                        nc.scalar.copy(k1[b][:, t, :, 0:DP], kl[:, t, 0:D].rearrange("p (c e) -> p c e", c=DC))
                    nc.scalar.copy(qT[b][0:DP].rearrange("p c t -> p (c t)"),
                                   banks[4 * b + 1][0:DP, 0:DC * TOKENS]).then_inc(acts_in_done, 1)
                for b in two:
                    n1 = i * 2 + (b + 1)
                    act.wait_ge(zbar_psum, n1)
                    nc.scalar.activation(sq[b][:], tiles(banks[4 * b + 1], TP, TT, D), ACT.Square).then_inc(zbar_sq_done, 1)
                for b in two:
                    n1 = i * 2 + (b + 1)
                    act.wait_ge(zbT_psum, n1)
                    nc.scalar.copy(zbT[b][:].rearrange("p c t -> p (c t)"),
                                   banks[4 * b + 2][0:DP, 0:DC * TOKENS]).then_inc(zbT_done, 1)

        @block.vector
        def _(dve):
            nc.vector.memset(w_in[:], 0.0)
            nc.vector.memset(w_1c[:], 0.0)
            for b in two:
                nc.vector.memset(xnT[b][DP:DP + 1], 1.0)
                nc.vector.memset(qT[b][DP:DP + 1], 1.0)
                nc.vector.memset(k1[b][:], 1.0)
            nc.vector.memset(w_q[:], 0.0).then_inc(cleared, 1)
            dve.wait_ge(weights_in, 16 * WEIGHT_DMAS)
            dve.wait_ge(cleared, 1)
            prep = Steps(dve, dve_steps, 0)
            for dc in range(DC):
                ins = nc.vector.tensor_tensor(w_q[:, dc, DP:DP + 1], q_col[:, dc:dc + 1], beta_col[:, dc:dc + 1], ALU.add)
            ins.then_inc(prep_dve, 1)
            prep.done(nc.vector.tensor_reduce(sums[:], w_1c[:].rearrange("p c (h e) -> p (c h) e", e=HD), AX_X, ALU.add))
            prep.settle()
            w1g = w_1c[:].rearrange("p c (h e) -> p (c h) e", e=HD)
            nc.vector.scalar_tensor_tensor(w1g, sums[:].unsqueeze(2).to_broadcast([DP + 1, HEADS, HD]), -1.0 / HD, w1g,
                                           ALU.mult, ALU.add).then_inc(prep_dve, 1)
            for c in range(DC):
                prep.done(nc.vector.tensor_tensor(w_vT[:, c], w_vT[:, c], w_kT[:, c], ALU.subtract))
            prep.done(nc.vector.tensor_tensor(gamma2[:], gamma_row[:], gamma_row[:], ALU.mult))
            prep.settle()
            for c in range(DC):
                prep.done(nc.vector.tensor_tensor(w_in[0:DP + 1, c, D:2 * D], w_vT[:, c], gamma_row[0:DP + 1], ALU.mult))
                prep.done(nc.vector.tensor_scalar(w_pg[:, c], w_pT[:, c], gamma_col[:, c:c + 1], None, ALU.mult))
            dve.wait_ge(prep_pe, 2)
            dve.wait_ge(prep_dve, 2)
            prep.done(nc.vector.tensor_tensor(w_qp[DP:DP + 1, 0], banks[0][DP:DP + 1, 0:D], p_bias[DP:DP + 1], ALU.add))
            prep.done(nc.vector.tensor_copy(w_qp[0:DP, 0], banks[0][0:DP, 0:D]))
            prep.done(nc.vector.tensor_copy(w_qp[0:DP, 1], banks[1][0:DP, 0:D]))
            prep.done(nc.vector.tensor_copy(w_in[DP:DP + 1, 0, 0:D], w_1c[DP:DP + 1].rearrange("p c e -> p (c e)")))
            prep.done(nc.vector.tensor_copy(w_in[0:DP, 0, 0:D], banks[2][0:DP, 0:D]))
            prep.done(nc.vector.tensor_copy(w_in[0:DP, 1, 0:D], banks[3][0:DP, 0:D]))
            prep.settle()
            dve.sem_inc(h_added, 2)
            dve.sem_inc(weights_ready, 1)

            with dve.Fori(0, PAIRS) as i:
                own = Steps(dve, dve_steps, i * TTT_STEPS_DVE + prep.n)
                for b in two:
                    n1 = i * 2 + (b + 1)
                    dve.wait_ge(h_kept, n1)
                    layernorm_dve(nc, dve, own, H, i * 2 + b, stats[b], mv[b], veps[b], veps_done)
                for b in two:
                    n1 = i * 2 + (b + 1)
                    dve.wait_ge(rstd_done, n1)
                    for t in range(TT):
                        ins = nc.vector.tensor_scalar(xn[b][:, t], H[:, i * 2 + b, t * D:(t + 1) * D], mv[b][:, t, 0:1],
                                                      rstd[b][:, t:t + 1], ALU.subtract, ALU.mult)
                    ins.then_inc(xn_done, 1)

                def group_var(b, signal):
                    own.done(nc.vector.tensor_reduce(gvar[b][:], grp(sq[b][:], 3), AX_X, ALU.add))
                    own.settle()
                    nc.vector.tensor_scalar(gvar[b][:], gvar[b][:], 1.0 / HD, TTT_EPS, ALU.mult, ALU.add).then_inc(signal, 1)

                def spread(stat):
                    return stat.unsqueeze(2).to_broadcast([TP, TT * HEADS, HD])

                for b in two:
                    n1 = i * 2 + (b + 1)
                    dve.wait_ge(sq_done, n1)
                    group_var(b, gvar_done)
                for b in two:
                    n1 = i * 2 + (b + 1)
                    dve.wait_ge(grstd_done, n1)
                    for t in range(TT):
                        hs = slice(t * HEADS, (t + 1) * HEADS)
                        ins = nc.vector.tensor_tensor(grp(xh[b][:, t], 2), grp(zt[b][:, t, 0], 2),
                                                      grstd[b][:, hs].unsqueeze(2).to_broadcast([TP, HEADS, HD]), ALU.mult)
                    ins.then_inc(xh_done, 1)
                    dve.wait_ge(acts_in_done, n1)
                    own.done(nc.vector.tensor_scalar(coef[b][:], lr[b][:].rearrange("p t h -> p (t h)"), 1.0, None, ALU.add))
                    own.settle()
                    own.done(nc.vector.reciprocal(coef[b][:], coef[b][:]))
                    own.settle()
                    own.done(nc.vector.scalar_tensor_tensor(coef[b][:], coef[b][:], 1.0 / (HD * TOKENS), grstd[b][:],
                                                            ALU.mult, ALU.mult))
                for b in two:
                    n1 = i * 2 + (b + 1)
                    dve.wait_ge(g2x_done, n1)
                    nc.vector.tensor_tensor(g[b][:], g[b][:], zt[b][:, :, 1], ALU.subtract).then_inc(g_done, 1)
                for b in two:
                    n1 = i * 2 + (b + 1)
                    dve.wait_ge(gx_done, n1)
                    own.done(nc.vector.tensor_reduce(sgx[b][:], grp(gx[b][:], 3), AX_X, ALU.add))
                    own.settle()
                    own.done(nc.vector.scalar_tensor_tensor(grp(gx[b][:], 3), grp(xh[b][:], 3), 1.0 / HD, spread(sgx[b][:]),
                                                            ALU.mult, ALU.mult))
                    own.settle()
                    own.done(nc.vector.tensor_tensor(g[b][:], g[b][:], gx[b][:], ALU.subtract))
                    own.settle()
                    nc.vector.tensor_tensor(grp(g[b][:], 3), grp(g[b][:], 3), spread(coef[b][:]), ALU.mult)\
                      .then_inc(grad_in_done, 1)
                for b in two:
                    n1 = i * 2 + (b + 1)
                    dve.wait_ge(grad_done, n1)
                    grad = banks[4 * b][0:DP + 1, 0:D]
                    own.done(nc.vector.tensor_reduce(gsum[b][:], grp(grad, 2), AX_X, ALU.add))
                    own.settle()
                    own.done(nc.vector.scalar_tensor_tensor(grp(gc[b][:], 2), gsum[b][:].unsqueeze(2).to_broadcast([DP + 1, HEADS, HD]),
                                                            -1.0 / HD, grp(grad, 2), ALU.mult, ALU.add))
                    own.settle()
                    own.done(nc.vector.tensor_tensor(gc[b][:], gc[b][:], head_mask[:], ALU.mult))
                    own.settle()
                    nc.vector.tensor_tensor(w_1n[b][:].rearrange("p c e -> p (c e)"), w_1c[:].rearrange("p c e -> p (c e)"),
                                            gc[b][:], ALU.subtract).then_inc(w1n_done, 1)
                for b in two:
                    n1 = i * 2 + (b + 1)
                    dve.wait_ge(zbar_sq_done, n1)
                    group_var(b, zvar_done)
                for b in two:
                    n1 = i * 2 + (b + 1)
                    dve.wait_ge(zrstd_done, n1)
                    nc.vector.tensor_tensor(grp(zb[b][:], 3), banks[4 * b + 1][0:TP, 0:TT * D].rearrange("p (g e) -> p g e", e=HD),
                                            spread(grstd[b][:]), ALU.mult).then_inc(zb_done, 1)
                for b in two:
                    n1 = i * 2 + (b + 1)
                    dve.wait_ge(out_psum, n1)
                    nc.vector.tensor_tensor(H[:, i * 2 + b], H[:, i * 2 + b], banks[4 * b + 3][0:TP, 0:TT * D], ALU.add)\
                      .then_inc(h_added, 1)
                assert own.n == TTT_STEPS_DVE, own.n


def layernorm_dve(nc, dve, own, H, index, stats, mv, veps, veps_done):
    for t in range(TT):
        own.done(nc.vector.bn_stats(stats[:, t], H[:, index, t * D:(t + 1) * D]))
    own.settle()
    nc.vector.memset(veps[:], 0.0)
    for t in range(TT):
        ins = nc.vector.bn_aggr(mv[:, t], stats[:, t])
    own.done(ins)
    own.settle()
    nc.vector.tensor_scalar(veps[:], mv[:, :, 1], LN_EPS, None, ALU.add).then_inc(veps_done, 1)


def normalise_dve(nc, H, index, mv, rstd, xn, xn_done):
    for t in range(TT):
        ins = nc.vector.tensor_scalar(xn[:, t, 0:D], H[:, index, t * D:(t + 1) * D], mv[:, t, 0:1],
                                      rstd[:, t:t + 1], ALU.subtract, ALU.mult)
    ins.then_inc(xn_done, 1)


def transposes_pe(nc, src, bank, ident, signal):
    for t in range(TT):
        for c in range(DC):
            mm = nc.tensor.transpose(bank[0:DP, c * TOKENS + t * TP:c * TOKENS + (t + 1) * TP],
                                     src[:, t, c * DP:(c + 1) * DP], ident[0:TP, 0:TP])
    mm.then_inc(signal, 1)


EXPERTS = 4


def moe_stage(nc, a, H, ident):
    MOE_STEPS_DVE = 24
    with ExitStack() as ctx:
        st = Stage(nc, ctx, "moe")
        sb, sem = st.sb, st.sem
        banks = st.psum_banks()
        two = range(2)

        w_1 = sb("w_1", [DP + 1, DC, EXPERTS, D])
        w_2 = sb("w_2", [DP + 1, DC, EXPERTS, D])
        w_r = sb("w_r", [DP + 1, DC, EXPERTS])
        mhalf = sb("mhalf", [TP, TT])
        xn = [sb(f"xn{b}", [TP, TT, D]) for b in two]
        xnT = [sb(f"xnT{b}", [DP + 1, DC, TOKENS]) for b in two]
        stats = [sb(f"stats{b}", [TP, TT, 6]) for b in two]
        mv = [sb(f"mv{b}", [TP, TT, 2]) for b in two]
        veps = [sb(f"veps{b}", [TP, TT]) for b in two]
        rstd = [sb(f"rstd{b}", [TP, TT]) for b in two]
        logits = [sb(f"logits{b}", [TP, TT, EXPERTS]) for b in two]
        top = [sb(f"top{b}", [TP, TT]) for b in two]
        chosen = [sb(f"chosen{b}", [TP, TT, EXPERTS]) for b in two]
        left = [sb(f"left{b}", [TP, TT]) for b in two]
        hidT = [[sb(f"hidT{b}{e}", [DP + 1, DC, TOKENS]) for e in range(2)] for b in two]
        acc = [sb(f"acc{b}", [TP, TT, D]) for b in two]

        rows_set = sem("rows_set")
        weights_in = sem("weights_in")
        veps_done = sem("veps_done")
        rstd_done = sem("rstd_done")
        xn_done = sem("xn_done")
        xnT_psum = sem("xnT_psum")
        xnT_done = sem("xnT_done")
        logits_psum = sem("logits_psum")
        logits_read = sem("logits_read")
        hid_psum = sem("hid_psum")
        gelu_done = sem("gelu_done")
        y_psum = sem("y_psum")
        y_used = sem("y_used")
        dve_steps = sem("dve_steps")

        LOADS = 8
        block = ctx.enter_context(nc.Block())

        @block.sync
        def _(sp):
            for dst, src in ((w_1[0:DP], a["moe_w1"]), (w_1[DP:DP + 1, 0], a["moe_b1"]), (w_2[0:DP], a["moe_w2"]),
                             (w_2[DP:DP + 1, 0], a["moe_b2"]), (w_r[0:DP], a["router_w"]), (w_r[DP:DP + 1, 0], a["router_b"]),
                             (mhalf[:], a["mhalf"][0:TP, 0:TT]), (ident[:], a["ident"])):
                sp.dma_start(dst, src).then_inc(weights_in, 16)

        @block.gpsimd
        def _(pool):
            pool.wait_ge(weights_in, 16 * LOADS)
            with pool.Fori(0, PAIRS) as i:
                for b in two:
                    pool.wait_ge(veps_done, i * 2 + (b + 1))
                    nc.gpsimd.tensor_tensor(rstd[b][:], veps[b][:], mhalf[:], ALU.pow).then_inc(rstd_done, 1)

        @block.tensor
        def _(pe):
            pe.wait_ge(weights_in, 16 * LOADS)
            pe.wait_ge(rows_set, 1)
            with pe.Fori(0, PAIRS) as i:
                def hidden(b, e):
                    for m in range(DC):
                        for c in range(DC):
                            K = DP + 1 - c
                            mm = nc.tensor.matmul(banks[4 * b + 2 + e % 2][0:DP, m * TOKENS:(m + 1) * TOKENS],
                                                  w_1[0:K, c, e, m * DP:(m + 1) * DP], xnT[b][0:K, c],
                                                  start=c == 0, stop=c == 1)
                    mm.then_inc(hid_psum, 1)

                def output(b, e):
                    for t in range(TT):
                        for c in range(DC):
                            K = DP + 1 - c
                            mm = nc.tensor.matmul(banks[4 * b + e % 2][0:TP, t * D:(t + 1) * D],
                                                  hidT[b][e % 2][0:K, c, t * TP:(t + 1) * TP], w_2[0:K, c, e],
                                                  start=c == 0, stop=c == 1)
                    mm.then_inc(y_psum, 1)

                for b in two:
                    pe.wait_ge(xn_done, i * 2 + (b + 1))
                    transposes_pe(nc, xn[b], banks[4 * b], ident, xnT_psum)
                for b in two:
                    pe.wait_ge(xnT_done, i * 2 + (b + 1))
                    for t in range(TT):
                        for c in range(DC):
                            K = DP + 1 - c
                            mm = nc.tensor.matmul(banks[4 * b + 1][0:TP, t * EXPERTS:(t + 1) * EXPERTS],
                                                  xnT[b][0:K, c, t * TP:(t + 1) * TP], w_r[0:K, c], start=c == 0, stop=c == 1)
                    mm.then_inc(logits_psum, 1)
                    hidden(b, 0)
                    hidden(b, 1)
                for e in range(EXPERTS):
                    for b in two:
                        pe.wait_ge(gelu_done, i * 8 + (2 * e + b + 1))
                        if e == 1:
                            pe.wait_ge(logits_read, i * 2 + (b + 1))
                        if e >= 2:
                            pe.wait_ge(y_used, i * 8 + (2 * (e - 2) + b + 1))
                        output(b, e)
                        if e < 2:
                            hidden(b, e + 2)

        @block.scalar
        def _(act):
            with act.Fori(0, PAIRS) as i:
                for b in two:
                    act.wait_ge(xnT_psum, i * 2 + (b + 1))
                    nc.scalar.copy(xnT[b][0:DP].rearrange("p c t -> p (c t)"),
                                   banks[4 * b][0:DP, 0:DC * TOKENS]).then_inc(xnT_done, 1)
                arrival = {(0, 0): 1, (0, 1): 2, (1, 0): 3, (1, 1): 4, (0, 2): 5, (1, 2): 6, (0, 3): 7, (1, 3): 8}
                for e in range(EXPERTS):
                    for b in two:
                        act.wait_ge(hid_psum, i * 8 + arrival[b, e])
                        if e >= 2:
                            act.wait_ge(y_psum, i * 8 + (2 * (e - 2) + b + 1))
                        nc.scalar.activation(hidT[b][e % 2][0:DP].rearrange("p c t -> p (c t)"),
                                             banks[4 * b + 2 + e % 2][0:DP, 0:DC * TOKENS], ACT.Gelu).then_inc(gelu_done, 1)

        @block.vector
        def _(dve):
            for b in two:
                nc.vector.memset(xnT[b][DP:DP + 1], 1.0)
                nc.vector.memset(hidT[b][0][DP:DP + 1], 1.0)
                ins = nc.vector.memset(hidT[b][1][DP:DP + 1], 1.0)
            ins.then_inc(rows_set, 1)
            with dve.Fori(0, PAIRS) as i:
                own = Steps(dve, dve_steps, i * MOE_STEPS_DVE)
                for b in two:
                    layernorm_dve(nc, dve, own, H, i * 2 + b, stats[b], mv[b], veps[b], veps_done)
                for b in two:
                    dve.wait_ge(rstd_done, i * 2 + (b + 1))
                    normalise_dve(nc, H, i * 2 + b, mv[b], rstd[b], xn[b], xn_done)
                for b in two:
                    dve.wait_ge(xn_done, i * 2 + (b + 1))
                    own.done(nc.vector.tensor_tensor(acc[b][:].rearrange("p t d -> p (t d)"), H[:, i * 2 + b],
                                                     xn[b][:].rearrange("p t d -> p (t d)"), ALU.add))
                for b in two:
                    dve.wait_ge(logits_psum, i * 2 + (b + 1))
                    nc.vector.tensor_copy(logits[b][:].rearrange("p t e -> p (t e)"),
                                          banks[4 * b + 1][0:TP, 0:TT * EXPERTS]).then_inc(logits_read, 1)
                    dve.wait_ge(logits_read, i * 2 + (b + 1))
                    own.done(nc.vector.tensor_reduce(top[b][:], logits[b][:], AX_X, ALU.max))
                    own.settle()
                    own.done(nc.vector.tensor_tensor(chosen[b][:], logits[b][:], top[b][:].unsqueeze(2).to_broadcast([TP, TT, EXPERTS]),
                                                     ALU.is_equal))
                    own.settle()
                    own.done(nc.vector.tensor_scalar(left[b][:], chosen[b][:, :, 0], -1.0, 1.0, ALU.mult, ALU.add))
                    for e in range(1, EXPERTS):
                        own.settle()
                        own.done(nc.vector.tensor_tensor(chosen[b][:, :, e], chosen[b][:, :, e], left[b][:], ALU.mult))
                        if e < EXPERTS - 1:
                            own.settle()
                            own.done(nc.vector.tensor_tensor(left[b][:], left[b][:], chosen[b][:, :, e], ALU.subtract))
                for e in range(EXPERTS):
                    for b in two:
                        dve.wait_ge(y_psum, i * 8 + (2 * e + b + 1))
                        if e == 0:
                            own.settle()
                        else:
                            dve.wait_ge(y_used, i * 8 + (2 * (e - 1) + b + 1))
                        for t in range(TT):
                            dst = acc[b][:, t] if e < EXPERTS - 1 else H[:, i * 2 + b, t * D:(t + 1) * D]
                            ins = nc.vector.scalar_tensor_tensor(dst, banks[4 * b + e % 2][0:TP, t * D:(t + 1) * D],
                                                                 chosen[b][:, t, e:e + 1], acc[b][:, t], ALU.mult, ALU.add)
                        ins.then_inc(y_used, 1)
                assert own.n == MOE_STEPS_DVE, own.n


GH = 3
GROUPS = HEADS // GH
SLOT = 32
CAUSAL = TOKENS + TP
SLOTS = 1024
ST = SLOTS // 128
QUARTERS = 4
QW = SLOTS // QUARTERS
PHI_EPS = 1e-6
FIRST = 0


def attention_dispatch_stage(nc, a, H, ident, phi, neg_row_max, slots_dram):
    FRONT_STEPS = 3
    ATT_STEPS = 7
    DIS_STEPS = 23
    with ExitStack() as ctx:
        st = Stage(nc, ctx, "ad")
        sb, sem = st.sb, st.sem
        ps = ctx.enter_context(nc.psum_tensor("ad_psum", [128, 8, 512], F32))
        COLS, ROWS_, SUMS, TURN = 4, 5, 6, 7

        w_in = sb("w_in", [DP + 1, DC, 3 * D])
        w_raw = sb("w_raw", [DP, DC, 3 * D])
        b_raw = sb("b_raw", [DP + 1, 3 * D])
        scale_col = sb("scale_col", [DP, DC])
        shift_col = sb("shift_col", [DP, DC])
        shift_w = sb("shift_w", [DP, DC, DP + 1])
        w_out = sb("w_out", [DP + 1, DC, D])
        rezero = sb("rezero", [DP + 1, 1])
        sinks = sb("sinks", [TP, HEADS])
        cos = sb("cos", [TP, TT, HD])
        sin = sb("sin", [TP, TT, HD])
        mask_qk_f = sb("mask_qk_f", [TP, TP])
        mask_kq_f = sb("mask_kq_f", [TP, TP])
        sel_f = sb("sel_f", [GH * SLOT, HEADS, TP])
        mask_qk = sb("mask_qk", [TP, TP], BF16)
        mask_kq = sb("mask_kq", [TP, TP], BF16)
        sel = sb("sel", [GH * SLOT, HEADS, TP], BF16)
        mhalf = sb("mhalf", [128, 24])
        ident_b = sb("ident_b", [128, 128], BF16)
        phi_sq = sb("phi_sq", [DP, DC, SLOTS])
        phi_sum = sb("phi_sum", [DP, DC, ST, 2])
        ones = sb("ones", [2, TP], BF16)

        xn = sb("xn", [TP, TT, D])
        xnT = sb("xnT", [DP + 1, DC, TOKENS])
        stats = sb("stats", [TP, TT, 6])
        mv = sb("mv", [TP, TT, 2])
        veps = sb("veps", [TP, TT])
        rstd = sb("rstd", [TP, TT])
        rot_c = sb("rot_c", [TP, TT, 2 * D])
        rot_s = sb("rot_s", [TP, TT, 2 * D])
        qk = sb("qk", [TP, TT, 2 * HEADS, SLOT])
        kT = sb("kT", [GH * SLOT, GROUPS, TOKENS])
        qT = sb("qT", [GH * SLOT, GROUPS, GH, TOKENS])
        v1 = sb("v1", [TP, TT, HEADS, SLOT])
        y_raw = sb("y_raw", [GH * SLOT, GROUPS, TOKENS])
        peak = sb("peak", [TP, TT, HEADS])
        npk_hi = sb("npk_hi", [TP, TT, HEADS], BF16)
        npk_lo = sb("npk_lo", [TP, TT, HEADS], BF16)
        npk = sb("npk", [TP, TT, GH, SLOT], BF16)
        npkT = sb("npkT", [GH * SLOT, TOKENS], BF16)
        sink_w = sb("sink_w", [TP, TT, HEADS])
        weights = [sb(f"weights{g}", [TP, GH, CAUSAL]) for g in range(2)]
        den = sb("den", [TP, TT, HEADS])
        y = sb("y", [TP, TT, D])
        yT = sb("yT", [DP + 1, DC, TOKENS])

        d_xn = sb("d_xn", [TP, TT, D + 1])
        d_xnT = sb("d_xnT", [DP, DC, TOKENS])
        d_stats = sb("d_stats", [TP, TT, 6])
        d_mv = sb("d_mv", [TP, TT, 2])
        d_veps = sb("d_veps", [TP, TT])
        d_rstd = sb("d_rstd", [TP, TT])
        col_peak = sb("col_peak", [128, 2])
        col_parts = sb("col_parts", [128, 2, 2], BF16)
        col_row = sb("col_row", [2, QW], BF16)
        row_peak = sb("row_peak", [TP, TT, QUARTERS])
        d_weights = sb("d_weights", [TP, TT, QW])
        s_stats = sb("s_stats", [128, 2, 6])
        s_mv = sb("s_mv", [128, 2, 2])
        s_den = sb("s_den", [128, 2])
        s_veps = sb("s_veps", [128, 2])
        s_rstd = sb("s_rstd", [128, 2])
        slot_in = sb("slot_in", [128, ST, D])

        cleared = sem("cleared")
        weights_in = sem("weights_in")
        prep_psum = sem("prep_psum")
        phi_summed = sem("phi_summed")
        phi_rstd = sem("phi_rstd")
        weights_ready = sem("weights_ready")
        veps_done = sem("veps_done")
        rstd_done = sem("rstd_done")
        xn_done = sem("xn_done")
        xnT_psum = sem("xnT_psum")
        xnT_done = sem("xnT_done")
        qkv_psum = sem("qkv_psum")
        v_kept = sem("v_kept")
        qk_done = sem("qk_done")
        qkT_psum = sem("qkT_psum")
        qkT_done = sem("qkT_done")
        scores_psum = sem("scores_psum")
        peaks_read = sem("peaks_read")
        npk_done = sem("npk_done")
        sink_arg = sem("sink_arg")
        npkT_psum = sem("npkT_psum")
        npkT_done = sem("npkT_done")
        sink_done = sem("sink_done")
        shifted_psum = sem("shifted_psum")
        exp_done = sem("exp_done")
        pv_done = sem("pv_done")
        y_raw_done = sem("y_raw_done")
        y_back = sem("y_back")
        y_done = sem("y_done")
        yT_psum = sem("yT_psum")
        yT_done = sem("yT_done")
        out_psum = sem("out_psum")
        h_added = sem("h_added")
        front_steps = sem("front_steps")
        att_steps = sem("att_steps")
        d_veps_done = sem("d_veps_done")
        d_rstd_done = sem("d_rstd_done")
        d_xn_done = sem("d_xn_done")
        d_xnT_psum = sem("d_xnT_psum")
        d_xnT_done = sem("d_xnT_done")
        cols_psum = sem("cols_psum")
        rows_psum = sem("rows_psum")
        col_parts_done = sem("col_parts_done")
        col_row_psum = sem("col_row_psum")
        col_row_done = sem("col_row_done")
        d_shifted_psum = sem("d_shifted_psum")
        d_exp_done = sem("d_exp_done")
        slots_psum = sem("slots_psum")
        s_veps_done = sem("s_veps_done")
        s_rstd_done = sem("s_rstd_done")
        slots_done = sem("slots_done")
        stored = sem("stored")
        dis_steps = sem("dis_steps")
        LOADS = 16
        block = ctx.enter_context(nc.Block())

        @block.sync
        def _(sp):
            sp.wait_ge(cleared, 1)
            loads = ((w_raw[:], a["attn_w"]), (b_raw[DP:DP + 1], a["attn_b"]), (scale_col[:], a["norm_scale"]),
                     (shift_col[:], a["norm_bias"]), (w_out[0:DP], a["attn_pw"]), (w_out[DP:DP + 1, 0], a["attn_pb"]),
                     (rezero[:], a["rezero"].partition_broadcast(DP + 1).rearrange("p o d -> p (o d)")),
                     (sinks[:], a["sinks"].partition_broadcast(TP).rearrange("p o d -> p (o d)")),
                     (cos[:], a["rope_cos"]), (sin[:], a["rope_sin"]), (mask_qk_f[:], a["mask_qk"]),
                     (mask_kq_f[:], a["mask_kq"]), (sel_f[:], a["head_sel"]), (mhalf[:], a["mhalf"]),
                     (ident[:], a["ident"]), (phi[:], a["phi"]))
            assert len(loads) == LOADS, len(loads)
            for dst, src in loads:
                sp.dma_start(dst, src).then_inc(weights_in, 16)
            with sp.Fori(0, IMAGES) as n:
                sp.wait_ge(slots_done, n * 4 + 4)
                sp.dma_start(slots_dram[:, n], slot_in[:].rearrange("p j d -> p (j d)")).then_inc(stored, 16)
            sp.wait_ge(stored, 16 * IMAGES + 16)

        @block.gpsimd
        def _(pool):
            def power(ready, count, out, x, done):
                pool.wait_ge(ready, count)
                nc.gpsimd.tensor_tensor(out, x, mhalf[0:x.shape[0], 0:x.shape[1]], ALU.pow).then_inc(done, 1)

            pool.wait_ge(weights_in, 16 * LOADS)
            flat = phi_sum[:].rearrange("p c j r -> p (c j r)")
            for part in (flat[:, 0:16], flat[:, 16:32]):
                power(phi_summed, 1, part, part, phi_rstd)

            def root(n):
                power(veps_done, n + 1, rstd[:], veps[:], rstd_done)

            def d_root(n):
                power(d_veps_done, n + 1, d_rstd[:], d_veps[:], d_rstd_done)

            def slot_root(n, q):
                power(s_veps_done, n * 4 + (q + 1), s_rstd[:], s_veps[:], s_rstd_done)

            def body(m, n, f):
                B, C = n is not None, f is not None
                if B: d_root(n)
                if B: slot_root(n, 0)
                if B: slot_root(n, 1)
                if C: root(f)
                if B: slot_root(n, 2)
                if B: slot_root(n, 3)

            body(None, None, 0)
            body(FIRST, None, 1)
            with pool.Fori(0, IMAGES - 2) as n:
                body(n + 1, n, n + 2)
            body(IMAGES - 1, IMAGES - 2, None)
            body(None, IMAGES - 1, None)

        @block.tensor
        def _(pe):
            pe.wait_ge(weights_in, 16 * LOADS)
            pe.wait_ge(prep_psum, 1)
            for part, (lo, hi) in enumerate(((0, 2 * D), (2 * D, 3 * D))):
                for c in range(DC):
                    mm = nc.tensor.matmul(ps[0:DP + 1, part, 0:hi - lo], shift_w[:, c], w_raw[:, c, lo:hi],
                                          start=c == 0, stop=c == 1)
            mm.then_inc(prep_psum, 1)
            pe.wait_ge(weights_ready, 1)

            def turn_x(n):
                pe.wait_ge(xn_done, n + 1)
                transposes_pe(nc, xn, ps[:, 3], ident, xnT_psum)

            def qkv(n, t):
                if t == 0:
                    pe.wait_ge(xnT_done, n + 1)
                for lo, hi, o in ((0, 2 * D, ps[0:TP, 2 * t, 0:2 * D]), (2 * D, 3 * D, ps[0:TP, 3, t * D:(t + 1) * D])):
                    for c in range(DC):
                        K = DP + 1 - c
                        mm = nc.tensor.matmul(o, xnT[0:K, c, t * TP:(t + 1) * TP], w_in[0:K, c, lo:hi],
                                              start=c == 0, stop=c == 1)
                if t == 1:
                    mm.then_inc(qkv_psum, 1)

            def turn_qk(n):
                pe.wait_ge(qk_done, n + 1)
                pe.wait_ge(v_kept, n + 1)
                if n is not FIRST:
                    pe.wait_ge(h_added, n)
                for g in range(GROUPS):
                    for kind in range(2):
                        for t in range(TT):
                            h0 = kind * HEADS + g * GH
                            mm = nc.tensor.transpose(ps[0:GH * SLOT, g, kind * TOKENS + t * TP:kind * TOKENS + (t + 1) * TP],
                                                     qk[:, t, h0:h0 + GH].rearrange("p h s -> p (h s)"), ident[0:TP, 0:TP])
                mm.then_inc(qkT_psum, 1)

            def scores(n, g):
                if g == 0:
                    pe.wait_ge(qkT_done, n * 2 + 2)
                else:
                    pe.wait_ge(peaks_read, n * 4 + g)
                for j in range(GH):
                    for t, o in ((0, ps[0:TP, j, 0:TP]), (1, ps[0:TP, j, TP:CAUSAL])):
                        nc.tensor.matmul(o, qT[:, g, j, t * TP:(t + 1) * TP], kT[:, g, 0:(t + 1) * TP],
                                         start=t == 0, stop=True, skip_group_check=True)
                for j in range(GH):
                    for m in (ps[0:TP, j, 0:TP], ps[0:TP, j, TOKENS:CAUSAL]):
                        mm = nc.tensor.matmul(m, ident_b[0:TP, 0:TP], mask_qk[:], start=False, stop=True, skip_group_check=True)
                mm.then_inc(scores_psum, 1)

            def turn_peaks(n):
                pe.wait_ge(npk_done, n + 1)
                for t in range(TT):
                    mm = nc.tensor.transpose(ps[0:GH * SLOT, 3, 0:TP].bitcast(BF16)[:, t * TP:(t + 1) * TP],
                                             npk[:, t].rearrange("p j s -> p (j s)"), ident_b[0:TP, 0:TP])
                mm.then_inc(npkT_psum, 1)

            def shifted(n, g):
                if g == 0:
                    pe.wait_ge(npkT_done, n + 1)
                else:
                    pe.wait_ge(exp_done, n * 4 + g)
                halves = [((0, ps[0:TP, j, 0:TOKENS], ps[0:TP, j, 0:TP]), (1, ps[0:TP, j, TOKENS:CAUSAL], ps[0:TP, j, TOKENS:CAUSAL]))
                          for j in range(GH)]
                for j in range(GH):
                    for t, o, m in halves[j]:
                        nc.tensor.matmul(o, kT[:, g, t * TP:(t + 1) * TP], qT[:, g, j, t * TP:TOKENS],
                                         start=t == 0, stop=True, skip_group_check=True)
                for j in range(GH):
                    slot = slice(SLOT * j, SLOT * (j + 1))
                    for t, o, m in halves[j]:
                        nc.tensor.matmul(o, sel[slot, g * GH + j], npkT[slot, t * TP:TOKENS], start=False, stop=True,
                                         skip_group_check=True)
                for j in range(GH):
                    for t, o, m in halves[j]:
                        mm = nc.tensor.matmul(m, ident_b[0:TP, 0:TP], mask_kq[:], start=False, stop=True, skip_group_check=True)
                mm.then_inc(shifted_psum, 1)

            def values(n, g):
                pe.wait_ge(exp_done, n * 4 + (g + 1))
                if g == 2:
                    pe.wait_ge(y_raw_done, n * 2 + 1)
                p = weights[g % 2]
                for j in range(GH):
                    h = g * GH + j
                    o = ps[SLOT * j:SLOT * (j + 1), 3, g % 2 * TOKENS:(g % 2 + 1) * TOKENS]
                    nc.tensor.matmul(o, v1[:, 0, h], p[:, j, 0:TOKENS], start=True, stop=True)
                    mm = nc.tensor.matmul(o[:, TP:], v1[:, 1, h], p[:, j, TOKENS:CAUSAL], start=False, stop=True,
                                          skip_group_check=True)
                mm.then_inc(pv_done, 1)

            def turn_back(n):
                pe.wait_ge(y_raw_done, n * 2 + 2)
                for g in range(GROUPS):
                    for t in range(TT):
                        mm = nc.tensor.transpose(ps[0:TP, t, g * GH * SLOT:(g + 1) * GH * SLOT],
                                                 y_raw[:, g, t * TP:(t + 1) * TP], ident[0:GH * SLOT, 0:GH * SLOT])
                mm.then_inc(y_back, 1)

            def turn_y(n):
                pe.wait_ge(y_done, n + 1)
                transposes_pe(nc, y, ps[:, 2], ident, yT_psum)

            def project(n):
                pe.wait_ge(yT_done, n + 1)
                for t in range(TT):
                    for c in range(DC):
                        K = DP + 1 - c
                        mm = nc.tensor.matmul(ps[0:TP, 1, t * D:(t + 1) * D], yT[0:K, c, t * TP:(t + 1) * TP], w_out[0:K, c],
                                              start=c == 0, stop=c == 1)
                mm.then_inc(out_psum, 1)

            def d_turn_x(n):
                pe.wait_ge(d_xn_done, n + 1)
                transposes_pe(nc, d_xn, ps[:, TURN], ident, d_xnT_psum)

            def logits_cols(n, q):
                if q == 0:
                    pe.wait_ge(d_xnT_done, n + 1)
                for s in range(2):
                    for c in range(DC):
                        mm = nc.tensor.matmul(ps[0:128, COLS, s * TOKENS:(s + 1) * TOKENS],
                                              phi[:, c, (2 * q + s) * 128:(2 * q + s + 1) * 128], d_xnT[:, c],
                                              start=c == 0, stop=c == 1)
                mm.then_inc(cols_psum, 1)

            def logits_rows(n, q):
                if q > 0:
                    pe.wait_ge(d_exp_done, n * 4 + q)
                for t in range(TT):
                    for c in range(DC):
                        mm = nc.tensor.matmul(ps[0:TP, ROWS_, t * QW:(t + 1) * QW], d_xnT[:, c, t * TP:(t + 1) * TP],
                                              phi[:, c, q * QW:(q + 1) * QW], start=t == 0 and c == 0, stop=c == 1,
                                              skip_group_check=True)
                mm.then_inc(rows_psum, 1)

            def turn_cols(n, q):
                pe.wait_ge(col_parts_done, n * 4 + (q + 1))
                for s in range(2):
                    mm = nc.tensor.transpose(ps[0:2, TURN, 0:128].bitcast(BF16)[:, s * 128:(s + 1) * 128], col_parts[:, s], ident_b[:])
                mm.then_inc(col_row_psum, 1)

            def shift_logits(n, q):
                pe.wait_ge(col_row_done, n * 4 + (q + 1))
                for t in range(TT):
                    mm = nc.tensor.matmul(ps[0:TP, ROWS_, t * QW:(t + 1) * QW], ones[:], col_row[:],
                                          start=False, stop=True, skip_group_check=True)
                mm.then_inc(d_shifted_psum, 1)

            def slot_sums(n, q):
                pe.wait_ge(d_exp_done, n * 4 + (q + 1))
                if q > 0:
                    pe.wait_ge(slots_done, n * 4 + q)
                for s in range(2):
                    for t in range(TT):
                        mm = nc.tensor.matmul(ps[0:128, SUMS, s * (D + 1):(s + 1) * (D + 1)],
                                              d_weights[:, t, s * 128:(s + 1) * 128], d_xn[:, t], start=t == 0, stop=t == 1)
                mm.then_inc(slots_psum, 1)

            def body(m, n, f):
                A, B, C = m is not None, n is not None, f is not None
                if B: d_turn_x(n)
                if B: logits_cols(n, 0)
                if B: logits_rows(n, 0)
                if A: turn_qk(m)
                if B: turn_cols(n, 0)
                if B: logits_cols(n, 1)
                if A: scores(m, 0)
                if B: shift_logits(n, 0)
                if A: scores(m, 1)
                if B: slot_sums(n, 0)
                if A: scores(m, 2)
                if B: logits_rows(n, 1)
                if B: turn_cols(n, 1)
                if A: scores(m, 3)
                if B: shift_logits(n, 1)
                if B: logits_cols(n, 2)
                if B: slot_sums(n, 1)
                if A: turn_peaks(m)
                if B: logits_rows(n, 2)
                if A: shifted(m, 0)
                if B: turn_cols(n, 2)
                if B: logits_cols(n, 3)
                if B: shift_logits(n, 2)
                if A: shifted(m, 1)
                if A: values(m, 0)
                if B: slot_sums(n, 2)
                if A: shifted(m, 2)
                if A: values(m, 1)
                if B: logits_rows(n, 3)
                if A: shifted(m, 3)
                if B: turn_cols(n, 3)
                if A: values(m, 2)
                if B: shift_logits(n, 3)
                if A: values(m, 3)
                if A: turn_back(m)
                if B: slot_sums(n, 3)
                if A: turn_y(m)
                if C: turn_x(f)
                if A: project(m)
                if C: qkv(f, 0)
                if C: qkv(f, 1)

            body(None, None, 0)
            body(FIRST, None, 1)
            with pe.Fori(0, IMAGES - 2) as n:
                body(n + 1, n, n + 2)
            body(IMAGES - 1, IMAGES - 2, None)
            body(None, IMAGES - 1, None)

        @block.scalar
        def _(act):
            def xnT_out(n):
                act.wait_ge(xnT_psum, n + 1)
                nc.scalar.copy(xnT[0:DP].rearrange("p c t -> p (c t)"), ps[0:DP, 3, 0:DC * TOKENS]).then_inc(xnT_done, 1)

            def v_out(n):
                act.wait_ge(qkv_psum, n + 1)
                for t in range(TT):
                    ins = nc.scalar.copy(v1[:, t, :, 0:HD], ps[0:TP, 3, t * D:(t + 1) * D].rearrange("p (h e) -> p h e", e=HD))
                ins.then_inc(v_kept, 1)

            def qkT_out(n):
                act.wait_ge(qkT_psum, n + 1)
                nc.scalar.copy(kT[:, 0:2], ps[0:GH * SLOT, 0:2, TOKENS:2 * TOKENS])
                for j in range(GH):
                    rows = slice(SLOT * j, SLOT * (j + 1))
                    ins = nc.scalar.copy(qT[rows, 0:2, j], ps[rows, 0:2, 0:TOKENS])
                ins.then_inc(qkT_done, 1)

            def sink_exp(n):
                act.wait_ge(sink_arg, n + 1)
                nc.scalar.activation(sink_w[:], sink_w[:], ACT.Exp).then_inc(sink_done, 1)

            def weights_exp(n, g):
                act.wait_ge(shifted_psum, n * 4 + (g + 1))
                if g >= 2:
                    act.wait_ge(pv_done, n * 4 + (g - 1))
                nc.scalar.activation(weights[g % 2][:], ps[0:TP, 0:GH, 0:CAUSAL], ACT.Exp).then_inc(exp_done, 1)

            def y_raw_out(n, half):
                act.wait_ge(pv_done, n * 4 + (2 * half + 2))
                nc.scalar.copy(y_raw[:, 2 * half:2 * half + 2].rearrange("p g t -> p (g t)"),
                               ps[0:GH * SLOT, 3, 0:2 * TOKENS]).then_inc(y_raw_done, 1)

            def yT_out(n):
                act.wait_ge(yT_psum, n + 1)
                nc.scalar.copy(yT[0:DP].rearrange("p c t -> p (c t)"), ps[0:DP, 2, 0:DC * TOKENS]).then_inc(yT_done, 1)

            def d_xnT_out(n):
                act.wait_ge(d_xnT_psum, n + 1)
                nc.scalar.copy(d_xnT[:].rearrange("p c t -> p (c t)"), ps[0:DP, TURN, 0:DC * TOKENS]).then_inc(d_xnT_done, 1)

            def d_exp(n, q):
                act.wait_ge(d_shifted_psum, n * 4 + (q + 1))
                nc.scalar.activation(d_weights[:].rearrange("p t s -> p (t s)"), ps[0:TP, ROWS_, 0:TT * QW], ACT.Exp)\
                  .then_inc(d_exp_done, 1)

            def body(m, n, f):
                A, B, C = m is not None, n is not None, f is not None
                if B: d_xnT_out(n)
                if A: v_out(m)
                if A: qkT_out(m)
                if B: d_exp(n, 0)
                if B: d_exp(n, 1)
                if A: sink_exp(m)
                if A: weights_exp(m, 0)
                if B: d_exp(n, 2)
                if A: weights_exp(m, 1)
                if A: weights_exp(m, 2)
                if A: y_raw_out(m, 0)
                if A: weights_exp(m, 3)
                if B: d_exp(n, 3)
                if A: y_raw_out(m, 1)
                if A: yT_out(m)
                if C: xnT_out(f)

            act.wait_ge(weights_ready, 1)
            body(None, None, 0)
            body(FIRST, None, 1)
            with act.Fori(0, IMAGES - 2) as n:
                body(n + 1, n, n + 2)
            body(IMAGES - 1, IMAGES - 2, None)
            body(None, IMAGES - 1, None)

        @block.vector
        def _(dve):
            nc.vector.memset(shift_w[:], 0.0)
            nc.vector.memset(xnT[DP:DP + 1], 1.0)
            nc.vector.memset(yT[DP:DP + 1], 1.0)
            nc.vector.memset(v1[:, :, :, HD + 1:], 0.0)
            nc.vector.memset(v1[:, :, :, HD:HD + 1], 1.0)
            nc.vector.memset(npk[:], 0.0)
            nc.vector.memset(qk[:], 0.0)
            nc.vector.memset(qT[:], 0.0)
            nc.vector.memset(d_xn[:], 1.0)
            nc.vector.memset(ones[:], 1.0)
            nc.vector.memset(w_in[:], 0.0).then_inc(cleared, 1)
            dve.wait_ge(cleared, 1)
            dve.wait_ge(weights_in, 16 * LOADS)
            nc.vector.tensor_copy(shift_w[:, :, DP], shift_col[:]).then_inc(prep_psum, 1)
            prep = Steps(dve, att_steps, 0)
            for c in range(DC):
                nc.vector.tensor_scalar(w_in[0:DP, c], w_raw[:, c], scale_col[:, c:c + 1], None, ALU.mult)
            nc.vector.tensor_copy(ident_b[:], ident[:])
            nc.vector.tensor_copy(mask_qk[:], mask_qk_f[:])
            nc.vector.tensor_copy(mask_kq[:], mask_kq_f[:])
            nc.vector.tensor_copy(sel[:], sel_f[:])
            nc.vector.tensor_scalar(w_out[:, 0], w_out[:, 0], rezero[:], None, ALU.mult)
            nc.vector.tensor_scalar(w_out[0:DP, 1], w_out[0:DP, 1], rezero[0:DP], None, ALU.mult)
            prep.done(nc.vector.tensor_tensor(phi_sq[:], phi[:], phi[:], ALU.mult))
            prep.settle()
            for c in range(DC):
                prep.done(nc.vector.tensor_reduce(phi_sum[:, c], phi_sq[:, c].rearrange("p (j n r) -> p j r n", j=ST, r=2), AX_X, ALU.add))
            prep.settle()
            nc.vector.tensor_scalar(phi_sum[:], phi_sum[:], PHI_EPS, None, ALU.add).then_inc(phi_summed, 1)
            dve.wait_ge(prep_psum, 2)
            row = w_in[DP:DP + 1, 0]
            prep.done(nc.vector.tensor_tensor(row[:, 0:2 * D], ps[DP:DP + 1, 0, 0:2 * D], b_raw[DP:DP + 1, 0:2 * D], ALU.add))
            prep.done(nc.vector.tensor_tensor(row[:, 2 * D:], ps[DP:DP + 1, 1, 0:D], b_raw[DP:DP + 1, 2 * D:], ALU.add))
            prep.settle()
            prep.done(nc.vector.tensor_scalar(w_in[:, :, 0:D], w_in[:, :, 0:D], HD ** -0.5, None, ALU.mult))
            dve.wait_ge(phi_rstd, 2)
            for c in range(DC):
                v = phi[:, c].rearrange("p (j n r) -> p j n r", j=ST, r=2)
                prep.done(nc.vector.tensor_tensor(v, v, phi_sum[:, c].unsqueeze(2).to_broadcast([DP, ST, SLOTS // ST // 2, 2]), ALU.mult))
            prep.settle()
            dve.sem_inc(weights_ready, 1)
            dve.sem_inc(stored, 16)

            def rotate(n, own):
                dve.wait_ge(qkv_psum, n + 1)
                for t in range(TT):
                    src = ps[0:TP, 2 * t, 0:2 * D].rearrange("p (h e) -> p h e", e=HD)
                    dc = rot_c[:, t].rearrange("p (h e) -> p h e", e=HD)
                    ds = rot_s[:, t].rearrange("p (h e) -> p h e", e=HD)
                    half = [TP, 2 * HEADS, HD // 2]
                    nc.vector.tensor_tensor(dc, src, cos[:, t].unsqueeze(1).to_broadcast([TP, 2 * HEADS, HD]), ALU.mult)
                    for one, other in ((0, 1), (1, 0)):
                        ins = nc.vector.tensor_tensor(ds[:, :, one::2], src[:, :, other::2],
                                                      sin[:, t, one::2].unsqueeze(1).to_broadcast(half), ALU.mult)
                own.done(ins)
                own.settle()
                for t in range(TT):
                    ins = nc.vector.tensor_tensor(qk[:, t, :, 0:HD], rot_c[:, t].rearrange("p (h e) -> p h e", e=HD),
                                                  rot_s[:, t].rearrange("p (h e) -> p h e", e=HD), ALU.add)
                ins.then_inc(qk_done, 1)

            def peaks(n, g):
                dve.wait_ge(scores_psum, n * 4 + (g + 1))
                hs = slice(g * GH, (g + 1) * GH)
                nc.vector.tensor_reduce(peak[:, 0, hs], ps[0:TP, 0:GH, 0:TP], AX_X, ALU.max)
                nc.vector.tensor_reduce(peak[:, 1, hs], ps[0:TP, 0:GH, TP:CAUSAL], AX_X, ALU.max).then_inc(peaks_read, 1)

            def qkT_half(n):
                dve.wait_ge(qkT_psum, n + 1)
                nc.vector.tensor_copy(kT[:, 2:4], ps[0:GH * SLOT, 2:4, TOKENS:2 * TOKENS])
                for j in range(GH):
                    rows = slice(SLOT * j, SLOT * (j + 1))
                    ins = nc.vector.tensor_copy(qT[rows, 2:4, j], ps[rows, 2:4, 0:TOKENS])
                ins.then_inc(qkT_done, 1)

            every_t = sinks[:].unsqueeze(1).to_broadcast([TP, TT, HEADS])

            def peak_parts(n, own):
                dve.wait_ge(peaks_read, n * 4 + 4)
                own.done(nc.vector.tensor_tensor(peak[:], peak[:], every_t, ALU.max))
                own.settle()
                own.done(nc.vector.tensor_scalar(npk_hi[:], peak[:], -1.0, None, ALU.mult))
                own.settle()
                own.done(nc.vector.scalar_tensor_tensor(npk_lo[:], peak[:], -1.0, npk_hi[:], ALU.mult, ALU.subtract))
                own.settle()
                nc.vector.tensor_copy(npk[:, :, :, 0:HEADS], npk_hi[:].unsqueeze(2).to_broadcast([TP, TT, GH, HEADS]))
                nc.vector.tensor_copy(npk[:, :, :, HEADS:2 * HEADS],
                                      npk_lo[:].unsqueeze(2).to_broadcast([TP, TT, GH, HEADS])).then_inc(npk_done, 1)
                own.done(nc.vector.tensor_tensor(sink_w[:], npk_hi[:], npk_lo[:], ALU.add))
                own.settle()
                nc.vector.tensor_tensor(sink_w[:], sink_w[:], every_t, ALU.add).then_inc(sink_arg, 1)

            def peaks_out(n):
                dve.wait_ge(npkT_psum, n + 1)
                nc.vector.tensor_copy(npkT[:], ps[0:GH * SLOT, 3, 0:TP].bitcast(BF16)).then_inc(npkT_done, 1)

            def attended(n, own):
                dve.wait_ge(y_back, n + 1)
                dve.wait_ge(sink_done, n + 1)
                o = ps[0:TP, 0:TT, 0:HEADS * SLOT].rearrange("p t (h s) -> p t h s", s=SLOT)
                own.done(nc.vector.tensor_tensor(den[:], o[:, :, :, HD], sink_w[:], ALU.add))
                own.settle()
                own.done(nc.vector.reciprocal(den[:], den[:]))
                own.settle()
                for t in range(TT):
                    ins = nc.vector.tensor_tensor(y[:, t].rearrange("p (h e) -> p h e", e=HD), o[:, t, :, 0:HD],
                                                  den[:, t].unsqueeze(2).to_broadcast([TP, HEADS, HD]), ALU.mult)
                ins.then_inc(y_done, 1)

            def add_residual(n):
                dve.wait_ge(out_psum, n + 1)
                nc.vector.tensor_tensor(H[:, n], H[:, n], ps[0:TP, 1, 0:TT * D], ALU.add).then_inc(h_added, 1)

            def col_peaks(n, q, own):
                dve.wait_ge(cols_psum, n * 4 + (q + 1))
                own.done(nc.vector.tensor_reduce(col_peak[:], ps[0:128, COLS, 0:2 * TOKENS].rearrange("p (s t) -> p s t", s=2),
                                                 AX_X, ALU.max, negate=True))
                own.settle()
                own.done(nc.vector.tensor_copy(col_parts[:, :, 0], col_peak[:]))
                own.settle()
                nc.vector.tensor_tensor(col_parts[:, :, 1], col_peak[:], col_parts[:, :, 0], ALU.subtract).then_inc(col_parts_done, 1)

            def row_peaks(n, q):
                dve.wait_ge(rows_psum, n * 4 + (q + 1))
                nc.vector.tensor_reduce(row_peak[:, :, q], ps[0:TP, ROWS_, 0:TT * QW].rearrange("p (t s) -> p t s", t=TT), AX_X, ALU.max)

            def cols_out(n, q):
                dve.wait_ge(col_row_psum, n * 4 + (q + 1))
                nc.vector.tensor_copy(col_row[:], ps[0:2, TURN, 0:128].bitcast(BF16)).then_inc(col_row_done, 1)

            def slot_stats(n, q, own):
                dve.wait_ge(slots_psum, n * 4 + (q + 1))
                raw = ps[0:128, SUMS, 0:2 * (D + 1)].rearrange("p (s d) -> p s d", s=2)
                for s in range(2):
                    nc.vector.bn_stats(s_stats[:, s], raw[:, s, 0:D])
                own.done(nc.vector.tensor_copy(s_den[:], raw[:, :, D]))
                own.settle()
                own.done(nc.vector.tensor_tensor(s_den[:], s_den[:], s_den[:], ALU.mult))
                for s in range(2):
                    ins = nc.vector.bn_aggr(s_mv[:, s], s_stats[:, s])
                own.done(ins)
                own.settle()
                nc.vector.scalar_tensor_tensor(s_veps[:], s_den[:], LN_EPS, s_mv[:, :, 1], ALU.mult, ALU.add).then_inc(s_veps_done, 1)

            def slot_norm(n, q):
                dve.wait_ge(s_rstd_done, n * 4 + (q + 1))
                if q == 0:
                    dve.wait_ge(stored, n * 16 + 16)
                for s in range(2):
                    ins = nc.vector.tensor_scalar(slot_in[:, 2 * q + s], ps[0:128, SUMS, s * (D + 1):s * (D + 1) + D],
                                                  s_mv[:, s, 0:1], s_rstd[:, s:s + 1], ALU.subtract, ALU.mult)
                ins.then_inc(slots_done, 1)

            def layernorm(n, own):
                layernorm_dve(nc, dve, own, H, n, stats, mv, veps, veps_done)

            def normalise(n):
                dve.wait_ge(rstd_done, n + 1)
                normalise_dve(nc, H, n, mv, rstd, xn, xn_done)

            def d_layernorm(n, own):
                dve.wait_ge(h_added, n + 1)
                layernorm_dve(nc, dve, own, H, n, d_stats, d_mv, d_veps, d_veps_done)

            def d_normalise(n):
                dve.wait_ge(d_rstd_done, n + 1)
                normalise_dve(nc, H, n, d_mv, d_rstd, d_xn, d_xn_done)

            def rows_max(n):
                nc.vector.tensor_reduce(neg_row_max[:, n], row_peak[:], AX_X, ALU.max, negate=True)

            def body(m, n, f):
                A, B, C = m is not None, n is not None, f is not None
                if A: att = Steps(dve, att_steps, m * ATT_STEPS + prep.n)
                if B: dis = Steps(dve, dis_steps, n * DIS_STEPS)
                if C: front = Steps(dve, front_steps, f * FRONT_STEPS)
                if B: d_layernorm(n, dis)
                if B: d_normalise(n)
                if A: rotate(m, att)
                if B: col_peaks(n, 0, dis)
                if B: row_peaks(n, 0)
                if A: qkT_half(m)
                if B: cols_out(n, 0)
                if A: peaks(m, 0)
                if B: col_peaks(n, 1, dis)
                if A: peaks(m, 1)
                if B: slot_stats(n, 0, dis)
                if A: peaks(m, 2)
                if B: slot_norm(n, 0)
                if B: row_peaks(n, 1)
                if B: cols_out(n, 1)
                if A: peaks(m, 3)
                if A: peak_parts(m, att)
                if B: col_peaks(n, 2, dis)
                if B: slot_stats(n, 1, dis)
                if A: peaks_out(m)
                if B: slot_norm(n, 1)
                if B: row_peaks(n, 2)
                if B: cols_out(n, 2)
                if B: col_peaks(n, 3, dis)
                if C: layernorm(f, front)
                if B: slot_stats(n, 2, dis)
                if B: row_peaks(n, 3)
                if B: slot_norm(n, 2)
                if B: cols_out(n, 3)
                if C: normalise(f)
                if A: attended(m, att)
                if B: slot_stats(n, 3, dis)
                if B: slot_norm(n, 3)
                if B: rows_max(n)
                if A: add_residual(m)
                assert (not A or att.n == ATT_STEPS) and (not B or dis.n == DIS_STEPS) and (not C or front.n == FRONT_STEPS)

            body(None, None, 0)
            body(FIRST, None, 1)
            with dve.Fori(0, IMAGES - 2) as n:
                body(n + 1, n, n + 2)
            body(IMAGES - 1, IMAGES - 2, None)
            body(None, IMAGES - 1, None)


SOFT_EXPERTS = 64
ROWS = 128 * ST
HALF = ROWS // 2
HID = 2 * D
HC = HID // 128


def experts_stage(nc, a, ident, slots_dram, outs_dram):
    PAIRS_E = SOFT_EXPERTS // 2
    with ExitStack() as ctx:
        st = Stage(nc, ctx, "exp")
        sb, sem = st.sb, st.sem
        ps = ctx.enter_context(nc.psum_tensor("exp_psum", [128, 8, 512], F32))
        two = range(2)

        gain = sb("gain", [DP, SOFT_EXPERTS, DC])
        shift = sb("shift", [DP, SOFT_EXPERTS, DC])
        w_1 = [sb(f"w_1{b}", [DP + 1, DC, HID]) for b in two]
        w_2 = [sb(f"w_2{b}", [128, HC, D]) for b in two]
        b_2 = [sb(f"b_2{b}", [128, D]) for b in two]
        x = [sb(f"x{b}", [128, ST, D]) for b in two]
        xT = [[sb(f"xT{b}{h}", [DP + 1, DC, HALF]) for h in two] for b in two]
        hid = [sb(f"hid{h}", [128, HC, HALF]) for h in two]
        y = [sb(f"y{b}", [128, ST, D]) for b in two]

        ident_in = sem("ident_in")
        vectors_in = sem("vectors_in")
        loaded = [sem("loaded0"), sem("loaded1")]
        xT_psum = sem("xT_psum")
        xT_done = sem("xT_done")
        hid_psum = sem("hid_psum")
        hid_done = sem("hid_done")
        y_psum = sem("y_psum")
        y_done = sem("y_done")
        stored = [sem("stored0"), sem("stored1")]
        x_dram = slots_dram.rearrange("(e r) n f -> e (r n) f", r=2)
        y_dram = outs_dram.rearrange("(e r) n f -> e (r n) f", r=2)
        block = ctx.enter_context(nc.Block())

        @block.sync
        def _(sp):
            sp.dma_start(ident[:], a["ident"]).then_inc(ident_in, 16)
            sp.dma_start(gain[:], a["ln_g"]).then_inc(vectors_in, 16)
            sp.dma_start(shift[:], a["ln_b"]).then_inc(vectors_in, 16)

            def load(b, e):
                sp.dma_start(x[b][:].rearrange("p j d -> p (j d)"),
                             x_dram[e]).then_inc(loaded[b], 16)
                sp.dma_start(w_1[b][0:DP], a["soft_w1"][e]).then_inc(loaded[b], 16)
                sp.dma_start(w_1[b][DP:DP + 1, 0], a["soft_b1"][e]).then_inc(loaded[b], 16)
                sp.dma_start(w_2[b][:], a["soft_w2"][e]).then_inc(loaded[b], 16)
                sp.dma_start(b_2[b][:], a["soft_b2"][e].partition_broadcast(128).rearrange("p o d -> p (o d)"))\
                  .then_inc(loaded[b], 16)

            for b in two:
                load(b, b)
            def store(b, i):
                sp.wait_ge(y_done, i * 4 + (2 * b + 3))
                sp.dma_start(y_dram[i * 2 + b], y[b][:].rearrange("p j d -> p (j d)")).then_inc(stored[b], 16)

            with sp.Fori(0, PAIRS_E - 1) as i:
                for b in two:
                    store(b, i)
                    load(b, i * 2 + (b + 2))
            for b in two:
                store(b, PAIRS_E - 1)
                sp.wait_ge(stored[b], 16 * PAIRS_E + 16)

        @block.tensor
        def _(pe):
            def turn(b, h, k):
                if h == 0:
                    pe.wait_ge(loaded[b], (k - 2 * b) * 20 + 80)
                if not (isinstance(k, int) and k == 0):
                    pe.wait_ge(xT_done, k)
                for c in range(DC):
                    for j in range(4):
                        mm = nc.tensor.transpose(ps[0:DP, c, j * 128:(j + 1) * 128], x[b][:, 4 * h + j, c * DP:(c + 1) * DP], ident[:])
                mm.then_inc(xT_psum, 1)

            def hidden(b, h, k):
                pe.wait_ge(xT_done, k + 1)
                for m in range(HC):
                    pe.wait_ge(hid_done, k * HC + (m + 1))
                    for c in range(DC):
                        K = DP + 1 - c
                        mm = nc.tensor.matmul(ps[0:128, 2 + m], w_1[b][0:K, c, m * 128:(m + 1) * 128], xT[b][h][0:K, c],
                                              start=c == 0, stop=c == 1)
                    mm.then_inc(hid_psum, 1)

            def output(b, h, k):
                pe.wait_ge(hid_done, k * HC + 2 * HC)
                pe.wait_ge(y_done, k + 1)
                for j in range(4):
                    for m in range(HC):
                        mm = nc.tensor.matmul(ps[0:128, 5 + j // 2, (j % 2) * D:(j % 2 + 1) * D],
                                              hid[h][:, m, j * 128:(j + 1) * 128], w_2[b][:, m], start=m == 0, stop=m == HC - 1)
                mm.then_inc(y_psum, 1)

            def pair(i, last):
                for b in two:
                    k = i * 4 + 2 * b
                    turn(b, 1, k + 1)
                    hidden(b, 0, k)
                    hidden(b, 1, k + 1)
                    output(b, 0, k)
                    if not (last and b == 1):
                        turn(1 - b, 0, k + 2)
                    output(b, 1, k + 1)

            pe.wait_ge(ident_in, 16)
            turn(0, 0, 0)
            with pe.Fori(0, PAIRS_E - 1) as i:
                pair(i, False)
            pair(PAIRS_E - 1, True)

        @block.scalar
        def _(act):
            act.sem_inc(hid_done, HC)
            with act.Fori(0, PAIRS_E) as i:
                for b in two:
                    for h in two:
                        for m in range(HC):
                            act.wait_ge(hid_psum, i * (4 * HC) + ((2 * b + h) * HC + m + 1))
                            nc.scalar.activation(hid[h][:, m], ps[0:128, 2 + m], ACT.Gelu)\
                              .then_inc(hid_done, 1)

        @block.vector
        def _(dve):
            def take_xT(b, h, e, k):
                dve.wait_ge(xT_psum, k + 1)
                for c in range(DC):
                    ins = nc.vector.tensor_scalar(xT[b][h][0:DP, c], ps[0:DP, c], gain[:, e, c:c + 1], shift[:, e, c:c + 1], ALU.mult, ALU.add)
                ins.then_inc(xT_done, 1)

            def take_y(b, h, i, k):
                dve.wait_ge(y_psum, k + 1)
                if h == 0:
                    dve.wait_ge(stored[b], i * 16 + 16)
                for s in range(2):
                    ins = nc.vector.tensor_tensor(y[b][:, 4 * h + 2 * s:4 * h + 2 * s + 2],
                                                  ps[0:128, 5 + s, 0:2 * D].rearrange("p (j d) -> p j d", j=2),
                                                  b_2[b][:].unsqueeze(1).to_broadcast([128, 2, D]), ALU.add)
                ins.then_inc(y_done, 1)

            def pair(i, last):
                for b in two:
                    k = i * 4 + 2 * b
                    take_xT(b, 1, i * 2 + b, k + 1)
                    take_y(b, 0, i, k)
                    if not (last and b == 1):
                        take_xT(1 - b, 0, i * 2 + (b + 1), k + 2)
                    take_y(b, 1, i, k + 1)

            dve.wait_ge(vectors_in, 32)
            for b in two:
                for h in two:
                    nc.vector.memset(xT[b][h][DP:DP + 1], 1.0)
            dve.sem_inc(y_done, 1)
            dve.sem_inc(stored[0], 16)
            dve.sem_inc(stored[1], 16)
            take_xT(0, 0, 0, 0)
            with dve.Fori(0, PAIRS_E - 1) as i:
                pair(i, False)
            pair(PAIRS_E - 1, True)


def combine_stage(nc, a, H, ident, phi, neg_row_max, outs_dram, out):
    COM_STEPS_DVE = 10
    with ExitStack() as ctx:
        st = Stage(nc, ctx, "com")
        sb, sem = st.sb, st.sem
        ps = ctx.enter_context(nc.psum_tensor("com_psum", [128, 8, 512], F32))
        two = range(2)

        mhalf = sb("mhalf", [TP, TT])
        ident_b = sb("ident_b", [TP, TP], BF16)
        ones = sb("ones", [2, 128], BF16)
        xn = [sb(f"xn{b}", [TP, TT, D]) for b in two]
        xnT = [sb(f"xnT{b}", [DP, DC, TOKENS]) for b in two]
        stats = [sb(f"stats{b}", [TP, TT, 6]) for b in two]
        mv = [sb(f"mv{b}", [TP, TT, 2]) for b in two]
        veps = [sb(f"veps{b}", [TP, TT]) for b in two]
        rstd = [sb(f"rstd{b}", [TP, TT]) for b in two]
        parts = [sb(f"parts{b}", [TP, TT, 2], BF16) for b in two]
        row = [sb(f"row{b}", [2, TOKENS], BF16) for b in two]
        weights = [[sb(f"weights{b}{q}", [128, 2, TOKENS]) for q in two] for b in two]
        y = [sb(f"y{b}", [128, ST, D + 1]) for b in two]
        rden = [sb(f"rden{b}", [TP, TT]) for b in two]
        res = [sb(f"res{b}", [TP, TT, D]) for b in two]

        consts_in = sem("consts_in")
        ready = sem("ready")
        y_in = [sem("y_in0"), sem("y_in1")]
        veps_done = sem("veps_done")
        rstd_done = sem("rstd_done")
        xn_done = sem("xn_done")
        parts_done = sem("parts_done")
        xnT_psum = sem("xnT_psum")
        xnT_done = sem("xnT_done")
        row_psum = sem("row_psum")
        row_done = sem("row_done")
        shifted_psum = sem("shifted_psum")
        exp_done = sem("exp_done")
        mixed = sem("mixed")
        res_done = sem("res_done")
        stored = [sem("stored0"), sem("stored1")]
        dve_steps = sem("dve_steps")
        block = ctx.enter_context(nc.Block())

        @block.sync
        def _(sp):
            sp.dma_start(ident[:], a["ident"]).then_inc(consts_in, 16)
            sp.dma_start(mhalf[:], a["mhalf"][0:TP, 0:TT]).then_inc(consts_in, 16)

            def load(b, n):
                sp.dma_start(y[b][:, :, 0:D], outs_dram[:, n].rearrange("p (j d) -> p j d", j=ST)).then_inc(y_in[b], 16)

            sp.wait_ge(ready, 1)
            for b in two:
                load(b, b)
            def store(b, i):
                sp.wait_ge(res_done, i * 2 + (b + 3))
                sp.dma_start(out[i * 2 + b].rearrange("(t p) d -> p t d", t=TT), res[b][:]).then_inc(stored[b], 16)

            with sp.Fori(0, PAIRS - 1) as i:
                for b in two:
                    sp.wait_ge(mixed, i * 2 + (b + 1))
                    load(b, i * 2 + (b + 2))
                for b in two:
                    store(b, i)
            for b in two:
                store(b, PAIRS - 1)
                sp.wait_ge(stored[b], 16 * PAIRS + 16)

        @block.gpsimd
        def _(pool):
            pool.wait_ge(consts_in, 32)
            with pool.Fori(0, PAIRS) as i:
                for b in two:
                    pool.wait_ge(veps_done, i * 2 + (b + 1))
                    nc.gpsimd.tensor_tensor(rstd[b][:], veps[b][:], mhalf[:], ALU.pow).then_inc(rstd_done, 1)

        @block.tensor
        def _(pe):
            pe.wait_ge(ready, 1)
            with pe.Fori(0, PAIRS) as i:
                def mix(q, b):
                    pe.wait_ge(exp_done, i * 8 + (2 * q + b + 1))
                    if q == 0:
                        pe.wait_ge(y_in[b], i * 16 + 16)
                        pe.wait_ge(res_done, i * 2 + (b + 1))
                    for t in range(TT):
                        for s in range(2):
                            j = 2 * q + s
                            mm = nc.tensor.matmul(ps[0:TP, 4 * b + 2, t * (D + 1):(t + 1) * (D + 1)],
                                                  weights[b][q % 2][:, s, t * TP:(t + 1) * TP], y[b][:, j],
                                                  start=j == 0 and t == 0, stop=j == ST - 1, skip_group_check=True)
                    if q == QUARTERS - 1:
                        mm.then_inc(mixed, 1)

                for b in two:
                    pe.wait_ge(xn_done, i * 2 + (b + 1))
                    transposes_pe(nc, xn[b], ps[:, 4 * b + 3], ident, xnT_psum)
                for b in two:
                    pe.wait_ge(xnT_done, i * 2 + (b + 1))
                    pe.wait_ge(parts_done, i * 2 + (b + 1))
                    for t in range(TT):
                        mm = nc.tensor.transpose(ps[0:2, 4 * b + 3, 0:TP].bitcast(BF16)[:, t * TP:(t + 1) * TP], parts[b][:, t], ident_b[:])
                    mm.then_inc(row_psum, 1)
                for q in range(QUARTERS):
                    for b in two:
                        if q == 0:
                            pe.wait_ge(row_done, i * 2 + (b + 1))
                        for s in range(2):
                            j = 2 * q + s
                            o = ps[0:128, 4 * b + q % 2, s * TOKENS:(s + 1) * TOKENS]
                            for c in range(DC):
                                nc.tensor.matmul(o, phi[:, c, j * 128:(j + 1) * 128], xnT[b][:, c], start=c == 0, stop=False)
                            mm = nc.tensor.matmul(o, ones[:], row[b][:], start=False, stop=True)
                        mm.then_inc(shifted_psum, 1)
                    if q > 0:
                        for b in two:
                            mix(q - 1, b)
                for b in two:
                    mix(QUARTERS - 1, b)

        @block.scalar
        def _(act):
            with act.Fori(0, PAIRS) as i:
                for b in two:
                    act.wait_ge(xnT_psum, i * 2 + (b + 1))
                    nc.scalar.copy(xnT[b][:].rearrange("p c t -> p (c t)"), ps[0:DP, 4 * b + 3, 0:DC * TOKENS]).then_inc(xnT_done, 1)
                for q in range(QUARTERS):
                    for b in two:
                        act.wait_ge(shifted_psum, i * 8 + (2 * q + b + 1))
                        nc.scalar.activation(weights[b][q % 2][:].rearrange("p s t -> p (s t)"),
                                             ps[0:128, 4 * b + q % 2, 0:2 * TOKENS], ACT.Exp).then_inc(exp_done, 1)

        @block.vector
        def _(dve):
            dve.wait_ge(consts_in, 32)
            nc.vector.memset(ones[:], 1.0)
            nc.vector.tensor_copy(ident_b[:], ident[0:TP, 0:TP])
            nc.vector.memset(y[0][:], 1.0)
            nc.vector.memset(y[1][:], 1.0).then_inc(ready, 1)
            dve.sem_inc(res_done, 2)
            dve.sem_inc(stored[0], 16)
            dve.sem_inc(stored[1], 16)
            with dve.Fori(0, PAIRS) as i:
                own = Steps(dve, dve_steps, i * COM_STEPS_DVE)
                for b in two:
                    layernorm_dve(nc, dve, own, H, i * 2 + b, stats[b], mv[b], veps[b], veps_done)
                for b in two:
                    own.done(nc.vector.tensor_copy(parts[b][:, :, 0], neg_row_max[:, i * 2 + b]))
                    own.settle()
                    nc.vector.tensor_tensor(parts[b][:, :, 1], neg_row_max[:, i * 2 + b], parts[b][:, :, 0], ALU.subtract)\
                      .then_inc(parts_done, 1)
                for b in two:
                    dve.wait_ge(rstd_done, i * 2 + (b + 1))
                    normalise_dve(nc, H, i * 2 + b, mv[b], rstd[b], xn[b], xn_done)
                for b in two:
                    dve.wait_ge(row_psum, i * 2 + (b + 1))
                    nc.vector.tensor_copy(row[b][:], ps[0:2, 4 * b + 3, 0:TP].bitcast(BF16)).then_inc(row_done, 1)
                for b in two:
                    dve.wait_ge(mixed, i * 2 + (b + 1))
                    acc = ps[0:TP, 4 * b + 2, 0:TT * (D + 1)].rearrange("p (t d) -> p t d", t=TT)
                    own.done(nc.vector.reciprocal(rden[b][:], acc[:, :, D]))
                    own.settle()
                    dve.wait_ge(stored[b], i * 16 + 16)
                    for t in range(TT):
                        ins = nc.vector.scalar_tensor_tensor(res[b][:, t], acc[:, t, 0:D], rden[b][:, t:t + 1],
                                                             H[:, i * 2 + b, t * D:(t + 1) * D], ALU.mult, ALU.add)
                    ins.then_inc(res_done, 1)
                assert own.n == COM_STEPS_DVE, own.n


def build(nc, a, out):
    slots_dram = nc.dram_tensor("slots", (128, IMAGES, ST * D), F32, kind="Internal").ap()
    outs_dram = nc.dram_tensor("slot_outs", (128, IMAGES, ST * D), F32, kind="Internal").ap()
    with (
        nc.sbuf_tensor("h", [TP, IMAGES, TT * D], F32) as H,
        nc.sbuf_tensor("ident", [128, 128], F32) as ident,
        nc.sbuf_tensor("phi", [DP, DC, SLOTS], F32) as phi,
        nc.sbuf_tensor("neg_row_max", [TP, IMAGES, TT], F32) as neg_row_max,
    ):
        ttt_stage(nc, a, H, ident)
        moe_stage(nc, a, H, ident)
        attention_dispatch_stage(nc, a, H, ident, phi, neg_row_max, slots_dram)
        experts_stage(nc, a, ident, slots_dram, outs_dram)
        combine_stage(nc, a, H, ident, phi, neg_row_max, outs_dram, out)


def laid_out(np, v):
    f = {k: np.asarray(x) for k, x in v.items()}
    c = np.ascontiguousarray

    def chunks(w):
        return c(w.reshape(DC, DP, *w.shape[1:]).swapaxes(0, 1))

    def row(x):
        return c(x.reshape(1, -1))

    x = f["x"].reshape(IMAGES, GRID, PATCH, GRID, PATCH).transpose(0, 2, 4, 1, 3)
    qkv = f["L0_attn_qkv_weight"].reshape(3, D, D)
    slots = 128 * 8
    phi = f["L1_ffn_phi"].reshape(128, 8, D).transpose(2, 1, 0).reshape(D, slots)
    return {
        "patches": c(x.reshape(IMAGES, 2, 128, TOKENS).transpose(0, 2, 1, 3)),
        "tok_wT": c(f["L0_tok_W"].T.reshape(2, 128, D).transpose(1, 0, 2)),
        "qkv": c(qkv.reshape(3, DC, DP, D).transpose(2, 0, 1, 3)),
        "qkv_T": c(qkv.transpose(0, 2, 1).reshape(3, DC, DP, D).transpose(2, 0, 1, 3)),
        "q_bias": row(f["L0_attn_q_bias"]),
        "q_bias_col": chunks(f["L0_attn_q_bias"]),
        "v_bias": row(f["L0_attn_v_bias"]),
        "lr_wT": chunks(f["L0_attn_ttt_lr_weight"].reshape(HEADS, D).T),
        "lr_bias": row(f["L0_attn_ttt_lr_bias"]),
        "proj_T": chunks(f["L0_attn_proj_weight"].T),
        "proj_bias": row(f["L0_attn_proj_bias"]),
        "ttt_gamma": row(f["L0_attn_ttt_norm_weight"]),
        "ttt_gamma_col": chunks(f["L0_attn_ttt_norm_weight"].reshape(D)),
        "ttt_beta": row(f["L0_attn_ttt_norm_bias"]),
        "ttt_beta_col": chunks(f["L0_attn_ttt_norm_bias"].reshape(D)),
        "W1": f["L0_attn_W1"],
        "b1": c(f["L0_attn_b1"].reshape(1, DC, DP)),
        "router_w": chunks(f["L0_ffn_router_w"]),
        "router_b": row(f["L0_ffn_router_b"]),
        "moe_w1": c(f["L0_ffn_w1"].reshape(4, DC, DP, D).transpose(2, 1, 0, 3)),
        "moe_b1": c(f["L0_ffn_b1"].reshape(1, 4, D)),
        "moe_w2": c(f["L0_ffn_w2"].reshape(4, DC, DP, D).transpose(2, 1, 0, 3)),
        "moe_b2": c(f["L0_ffn_b2"].reshape(1, 4, D)),
        "norm_scale": chunks(f["L1_attn_norm_scale"]),
        "norm_bias": chunks(f["L1_attn_norm_bias"]),
        "attn_w": chunks(f["L1_attn_W_attn"]),
        "attn_b": row(f["L1_attn_b_attn"]),
        "attn_pw": chunks(f["L1_attn_W_proj"]),
        "attn_pb": row(f["L1_attn_b_proj"]),
        "sinks": row(f["L1_attn_sinks"]),
        "rezero": row(f["L1_attn_rezero"]),
        "phi": chunks(phi),
        "ln_g": c(f["L1_ffn_ln_g"].reshape(64, DC, DP).transpose(2, 0, 1)),
        "ln_b": c(f["L1_ffn_ln_b"].reshape(64, DC, DP).transpose(2, 0, 1)),
        "soft_w1": c(f["L1_ffn_w1"].reshape(64, DC, DP, 2 * D).transpose(0, 2, 1, 3)),
        "soft_b1": f["L1_ffn_b1"].reshape(64, 1, 2 * D),
        "soft_w2": c(f["L1_ffn_w2"].reshape(64, 3, 128, D).transpose(0, 2, 1, 3)),
        "soft_b2": f["L1_ffn_b2"].reshape(64, 1, D),
    }


def constants(np):
    r = np.arange(DP + 1)
    head_mask = (r[:, None] // HD == r[None, :DP] // HD) | (r[:, None] == DP)
    ang = np.outer(np.arange(TOKENS), 1.0 / 10000.0 ** (np.arange(0, HD, 2, dtype=np.float32) / HD)).astype(np.float32)
    cos = np.repeat(np.cos(ang), 2, axis=1).reshape(TT, TP, HD).transpose(1, 0, 2)
    sin = np.stack([-np.sin(ang), np.sin(ang)], axis=2).reshape(TT, TP, HD).transpose(1, 0, 2)
    k, q = np.arange(TP)[:, None], np.arange(TP)[None, :]
    rows, heads = np.arange(96)[:, None], np.arange(HEADS)[None, :]
    head_sel = (rows // 32 == heads % 3) & ((rows % 32 == heads) | (rows % 32 == heads + HEADS))
    return {
        "ident": np.eye(128, dtype=np.float32),
        "head_mask": head_mask.astype(np.float32),
        "mhalf": np.full((128, 24), -0.5, np.float32),
        "rope_cos": np.ascontiguousarray(cos.astype(np.float32)),
        "rope_sin": np.ascontiguousarray(sin.astype(np.float32)),
        "head_sel": np.ascontiguousarray(np.repeat(head_sel[:, :, None], TP, axis=2).astype(np.float32)),
        "mask_kq": np.where(k > q, np.float32(-1e30), np.float32(0.0)).astype(np.float32),
        "mask_qk": np.where(q > k, np.float32(-1e30), np.float32(0.0)).astype(np.float32),
    }


def kernel(**inputs):
    import numpy as _np
    import concourse.bacc as _bacc
    from concourse import mybir as _mybir
    from concourse.bass_utils import run_bass_kernel_spmd as _run

    nc = _bacc.Bacc("TRN2", target_bir_lowering=False, num_devices=1)
    data, aps = {}, {}
    for name, array in {**laid_out(_np, inputs), **constants(_np)}.items():
        data[f"in_{name}"] = array
        aps[name] = nc.dram_tensor(f"in_{name}", array.shape, _mybir.dt.from_np(array.dtype), kind="ExternalInput").ap()
    out = nc.dram_tensor("out", (IMAGES, TOKENS, D), F32, kind="ExternalOutput").ap()
    build(nc, aps, out)
    r = _run(nc, [data], core_ids=[0])
    return r.results[0]["out"]
```

```python
from collections import namedtuple
from contextlib import ExitStack

import numpy as np

import concourse.bass as bass
from concourse import mybir

ALU = mybir.AluOpType
ACT = mybir.ActivationFunctionType
AX_X = mybir.AxisListType.X
F32 = mybir.dt.float32
BF16 = mybir.dt.bfloat16

IMAGES = 64
SIDE, PATCH = 224, 16
GRID = SIDE // PATCH
TOKENS = GRID * GRID
TT = 2
TP = TOKENS // TT
D = 192
DC = 2
DP = D // DC
HEADS, HD = 12, 16
PAIRS = IMAGES // 2
LN_EPS = 1e-5
TTT_EPS = 1e-6


class Steps:

    def __init__(self, eng, sem, before):
        self.eng, self.sem, self.before, self.n = eng, sem, before, 0

    def done(self, ins):
        ins.then_inc(self.sem, 1)
        self.n += 1

    def settle(self):
        self.eng.wait_ge(self.sem, self.before + self.n)


class Stage:

    def __init__(self, nc, ctx, name):
        self.nc, self.ctx, self.name = nc, ctx, name

    def sb(self, name, shape, dt=F32):
        return self.ctx.enter_context(self.nc.sbuf_tensor(f"{self.name}_{name}", shape, dt))

    def psum_banks(self, n=8):
        return [self.ctx.enter_context(self.nc.psum_tensor(f"{self.name}_bank{i}", [128, 512], F32)) for i in range(n)]

    def sem(self, name):
        return self.nc.alloc_semaphore(f"{self.name}_{name}")


def layernorm_dve(nc, dve, own, H, index, stats, mv, veps, veps_done):
    for t in range(TT):
        own.done(nc.vector.bn_stats(stats[:, t], H[:, index, t * D:(t + 1) * D]))
    own.settle()
    nc.vector.memset(veps[:], 0.0)
    for t in range(TT):
        ins = nc.vector.bn_aggr(mv[:, t], stats[:, t])
    own.done(ins)
    own.settle()
    nc.vector.tensor_scalar(veps[:], mv[:, :, 1], LN_EPS, None, ALU.add).then_inc(veps_done, 1)


def normalise_dve(nc, H, index, mv, rstd, xn, xn_done):
    for t in range(TT):
        ins = nc.vector.tensor_scalar(xn[:, t, 0:D], H[:, index, t * D:(t + 1) * D], mv[:, t, 0:1],
                                      rstd[:, t:t + 1], ALU.subtract, ALU.mult)
    ins.then_inc(xn_done, 1)


def transposes_pe(nc, src, bank, ident, signal):
    for t in range(TT):
        for c in range(DC):
            mm = nc.tensor.transpose(bank[0:DP, c * TOKENS + t * TP:c * TOKENS + (t + 1) * TP],
                                     src[:, t, c * DP:(c + 1) * DP], ident[0:TP, 0:TP])
    mm.then_inc(signal, 1)


EXPERTS = 4
FIRST = 0
Image = namedtuple("Image", "n b turn")


def ttt_moe_stage(nc, a, H, ident):
    EARLY_STEPS = 4
    LATE_STEPS = 10
    MOE_STEPS = 12
    with ExitStack() as ctx:
        st = Stage(nc, ctx, "tm")
        sb, sem = st.sb, st.sem
        banks = st.psum_banks()
        Z, KL, QX, GB, HB, YB = banks[0:2], banks[2], banks[3], banks[4], banks[5:7], banks[7]
        two = range(2)

        w_tok = sb("w_tok", [128, 2, D])
        w_in = sb("w_in", [DP + 1, DC, 3 * D + HEADS])
        w_qT = sb("w_qT", [DP + 1, DC, D])
        w_q = sb("w_q", [DP, DC, D + 1])
        w_k = sb("w_k", [DP, DC, D])
        w_kT = sb("w_kT", [DP + 1, DC, D])
        w_vT = sb("w_vT", [DP + 1, DC, D])
        w_pT = sb("w_pT", [DP, DC, D])
        w_pg = sb("w_pg", [DP, DC, D])
        w_qp = sb("w_qp", [DP + 1, DC, D])
        p_bias = sb("p_bias", [DP + 1, D])
        gamma_row = sb("gamma_row", [TP, D])
        gamma2 = sb("gamma2", [TP, D])
        gamma_col = sb("gamma_col", [DP, DC])
        beta_col = sb("beta_col", [DP, DC])
        q_col = sb("q_col", [DP, DC])
        w_1c = sb("w_1c", [DP + 1, DC, DP])
        head_mask = sb("head_mask", [DP + 1, D])
        sums = sb("sums", [DP + 1, HEADS])
        mhalf = sb("mhalf", [TP, 2 * HEADS])

        w_1 = sb("w_1", [DP + 1, DC, EXPERTS, D])
        w_2 = sb("w_2", [DP + 1, DC, EXPERTS, D])
        w_r = sb("w_r", [DP + 1, DC, EXPERTS])

        xp = [sb(f"xp{b}", [128, 2, TOKENS]) for b in two]
        xnT = [sb(f"xnT{b}", [DP + 1, DC, TOKENS]) for b in two]
        xn = sb("xn", [TP, TT, D])
        stats = sb("stats", [TP, TT, 6])
        mv = sb("mv", [TP, TT, 2])
        veps = sb("veps", [TP, TT])
        rstd = sb("rstd", [TP, TT])
        zt = sb("zt", [TP, TT, 2, D])
        sq = sb("sq", [TP, TT, D])
        gvar = sb("gvar", [TP, TT * HEADS])
        grstd = sb("grstd", [TP, TT * HEADS])
        k1 = sb("k1", [TP, TT, DC, DP + 1])
        lr = sb("lr", [TP, TT, HEADS])
        qT = sb("qT", [DP + 1, DC, TOKENS])
        coef = sb("coef", [TP, TT * HEADS])
        xh = sb("xh", [TP, TT, D])
        g = sb("g", [TP, TT, D])
        gx = sb("gx", [TP, TT, D])
        sgx = sb("sgx", [TP, TT * HEADS])
        gsum = sb("gsum", [DP + 1, HEADS])
        gc = sb("gc", [DP + 1, D])
        w_1n = sb("w_1n", [DP + 1, DC, DP])
        zsq = sb("zsq", [TP, TT, D])
        zvar = sb("zvar", [TP, TT * HEADS])
        zrstd = sb("zrstd", [TP, TT * HEADS])
        zb = sb("zb", [TP, TT, D])
        zbT = sb("zbT", [DP, DC, TOKENS])
        m_xn = sb("m_xn", [TP, TT, D])
        m_xnT = sb("m_xnT", [DP + 1, DC, TOKENS])
        m_stats = sb("m_stats", [TP, TT, 6])
        m_mv = sb("m_mv", [TP, TT, 2])
        m_veps = sb("m_veps", [TP, TT])
        m_rstd = sb("m_rstd", [TP, TT])
        logits = sb("logits", [TP, TT, EXPERTS])
        top = sb("top", [TP, TT])
        chosen = sb("chosen", [TP, TT, EXPERTS])
        left = sb("left", [TP, TT])
        hidT = [sb(f"hidT{e}", [DP + 1, DC, TOKENS]) for e in two]
        acc = sb("acc", [TP, TT, D])

        cleared = sem("cleared")
        weights_in = sem("weights_in")
        prep_dve = sem("prep_dve")
        prep_pe = sem("prep_pe")
        weights_ready = sem("weights_ready")
        x_in = [sem("x_in0"), sem("x_in1")]
        tok_done = sem("tok_done")
        h_kept = sem("h_kept")
        veps_done = sem("veps_done")
        rstd_done = sem("rstd_done")
        xn_done = sem("xn_done")
        xnT_psum = sem("xnT_psum")
        xnT_done = sem("xnT_done")
        acts_in_done = sem("acts_in_done")
        sq_done = sem("sq_done")
        gvar_done = sem("gvar_done")
        grstd_done = sem("grstd_done")
        xh_done = sem("xh_done")
        g2x_done = sem("g2x_done")
        g_done = sem("g_done")
        gx_done = sem("gx_done")
        grad_in_done = sem("grad_in_done")
        grad_done = sem("grad_done")
        w1n_done = sem("w1n_done")
        zbar_psum = sem("zbar_psum")
        zbar_sq_done = sem("zbar_sq_done")
        zvar_done = sem("zvar_done")
        zrstd_done = sem("zrstd_done")
        zb_done = sem("zb_done")
        zbT_psum = sem("zbT_psum")
        zbT_done = sem("zbT_done")
        out_psum = sem("out_psum")
        h_added = sem("h_added")

        q_psum = sem("q_psum")
        q_kept = sem("q_kept")
        z_psum = sem("z_psum")
        z_kept = sem("z_kept")
        kl_psum = sem("kl_psum")
        early_steps = sem("early_steps")
        late_steps = sem("late_steps")
        moe_steps = sem("moe_steps")
        prep_steps = sem("prep_steps")
        m_veps_done = sem("m_veps_done")
        m_rstd_done = sem("m_rstd_done")
        m_xn_done = sem("m_xn_done")
        m_xnT_psum = sem("m_xnT_psum")
        m_xnT_done = sem("m_xnT_done")
        logits_psum = sem("logits_psum")
        logits_read = sem("logits_read")
        hid_psum = sem("hid_psum")
        gelu_done = sem("gelu_done")
        y_psum = sem("y_psum")
        y_used = sem("y_used")

        WEIGHT_DMAS = 32 + HEADS
        block = ctx.enter_context(nc.Block())

        def heads(ap):
            if len(ap.shape) == 3:
                return ap.rearrange("p t (h e) -> p (t h) e", e=HD)
            return ap.rearrange("p (h e) -> p h e", e=HD)

        @block.sync
        def _(sp):
            count = [0]

            def load(dst, src):
                sp.dma_start(dst, src).then_inc(weights_in, 16)
                count[0] += 1

            load(w_tok[:], a["tok_wT"])
            sp.dma_start(xp[0][:], a["patches"][0]).then_inc(x_in[0], 16)
            sp.dma_start(xp[1][:], a["patches"][1]).then_inc(x_in[1], 16)
            sp.wait_ge(cleared, 1)
            q_rows, k_rows = 0, 1
            load(w_in[0:DP, :, 2 * D:3 * D], a["qkv_T"][:, k_rows])
            load(w_in[0:DP, :, 3 * D:], a["lr_wT"])
            load(w_in[DP:DP + 1, 0, 3 * D:], a["lr_bias"])
            load(w_qT[0:DP], a["qkv_T"][:, q_rows])
            load(w_qT[DP:DP + 1, 0], a["q_bias"])
            load(w_q[:, :, 0:DP], a["qkv"][:, q_rows, :, 0:DP])
            load(w_q[:, :, DP + 1:], a["qkv"][:, q_rows, :, DP:])
            load(q_col[:], a["q_bias_col"])
            load(w_k[:], a["qkv"][:, k_rows])
            load(w_kT[0:DP], a["qkv_T"][:, k_rows])
            load(w_kT[DP:DP + 1, 0], a["ttt_beta"])
            load(w_kT[DP:DP + 1, 1], a["ttt_beta"])
            load(w_vT[0:DP], a["qkv_T"][:, 2])
            load(w_vT[DP:DP + 1, 0], a["v_bias"])
            load(w_vT[DP:DP + 1, 1], a["v_bias"])
            load(w_pT[:], a["proj_T"])
            load(p_bias[DP:DP + 1, :], a["proj_bias"])
            load(gamma_row[:], a["ttt_gamma"].partition_broadcast(TP).rearrange("p o d -> p (o d)"))
            load(gamma_col[:], a["ttt_gamma_col"])
            load(beta_col[:], a["ttt_beta_col"])
            for h in range(HEADS):
                c, r = h // 6, h % 6 * HD
                load(w_1c[r:r + HD, c, r:r + HD], a["W1"][h])
            load(w_1c[DP:DP + 1], a["b1"])
            load(head_mask[:, 0:DP], a["head_mask"])
            load(head_mask[:, DP:], a["head_mask"])
            load(ident[:], a["ident"])
            load(mhalf[:], a["mhalf"][0:TP, 0:2 * HEADS])
            load(w_1[0:DP], a["moe_w1"])
            load(w_1[DP:DP + 1, 0], a["moe_b1"])
            load(w_2[0:DP], a["moe_w2"])
            load(w_2[DP:DP + 1, 0], a["moe_b2"])
            load(w_r[0:DP], a["router_w"])
            load(w_r[DP:DP + 1, 0], a["router_b"])
            assert count[0] == WEIGHT_DMAS, count
            with sp.Fori(0, PAIRS - 1) as i:
                for b in two:
                    sp.wait_ge(tok_done, i * 2 + (b + 1))
                    sp.dma_start(xp[b][:], a["patches"][i * 2 + (b + 2)]).then_inc(x_in[b], 16)

        @block.gpsimd
        def _(pool):
            def power(ready, image, out, x, done):
                pool.wait_ge(ready, image.n + 1)
                nc.gpsimd.tensor_tensor(out[:], x[:], mhalf[:, 0:x.shape[1]], ALU.pow).then_inc(done, 1)

            def m_root(n):
                power(m_veps_done, n, m_rstd, m_veps, m_rstd_done)

            def root(f):
                power(veps_done, f, rstd, veps, rstd_done)

            def z_root(f):
                power(gvar_done, f, grstd, gvar, grstd_done)

            def zbar_root(m):
                power(zvar_done, m, zrstd, zvar, zrstd_done)

            def gamma2_xh(m):
                pool.wait_ge(xh_done, m.n + 1)
                for t in range(TT):
                    ins = nc.gpsimd.tensor_tensor(g[:, t], xh[:, t], gamma2[:], ALU.mult)
                ins.then_inc(g2x_done, 1)

            def g_xh(m):
                pool.wait_ge(g_done, m.n + 1)
                nc.gpsimd.tensor_tensor(gx[:], g[:], xh[:], ALU.mult).then_inc(gx_done, 1)

            def body(f, m, n):
                if n is not None: m_root(n)
                if m is not None: gamma2_xh(m)
                if m is not None: g_xh(m)
                if f is not None: root(f)
                if m is not None: zbar_root(m)
                if f is not None: z_root(f)

            pool.wait_ge(weights_ready, 1)
            body(Image(FIRST, 0, 0), None, None)
            body(Image(1, 1, 0), Image(0, 0, 0), None)
            with pool.Fori(0, PAIRS - 1) as i:
                body(Image(i * 2 + 2, 0, i + 1), Image(i * 2 + 1, 1, i), Image(i * 2, 0, i))
                body(Image(i * 2 + 3, 1, i + 1), Image(i * 2 + 2, 0, i + 1), Image(i * 2 + 1, 1, i))
            body(None, Image(IMAGES - 1, 1, PAIRS - 1), Image(IMAGES - 2, 0, PAIRS - 1))
            body(None, None, Image(IMAGES - 1, 1, PAIRS - 1))

        @block.tensor
        def _(pe):
            pe.wait_ge(weights_in, 16 * WEIGHT_DMAS)
            pe.wait_ge(prep_dve, 1)
            for dc in range(DC):
                nc.tensor.matmul(banks[0][0:DP + 1, 0:D], w_q[:, dc, 0:DP + 1], w_pT[:, dc], start=dc == 0, stop=dc == 1)
            for dc in range(DC):
                mm = nc.tensor.matmul(banks[1][0:DP, 0:D], w_q[:, dc, DP + 1:], w_pT[:, dc], start=dc == 0, stop=dc == 1)
            mm.then_inc(prep_pe, 1)
            pe.wait_ge(prep_dve, 2)
            for ic in range(DC):
                for c in range(DC):
                    mm = nc.tensor.matmul(banks[2 + ic][0:DP, c * DP:(c + 1) * DP], w_k[:, c, ic * DP:(ic + 1) * DP],
                                          w_1c[0:DP, c], start=True, stop=True)
            mm.then_inc(prep_pe, 1)
            pe.wait_ge(weights_ready, 1)


            def embed(f):
                pe.wait_ge(x_in[f.b], f.turn * 16 + 16)
                if f.n is not FIRST:
                    pe.wait_ge(z_kept, f.n)
                for t in range(TT):
                    for c in range(2):
                        mm = nc.tensor.matmul(Z[0][0:TP, t * D:(t + 1) * D], xp[f.b][:, c, t * TP:(t + 1) * TP], w_tok[:, c],
                                              start=c == 0, stop=c == 1)
                mm.then_inc(tok_done, 1)

            def turn_x(f):
                pe.wait_ge(xn_done, f.n + 1)
                if f.n is not FIRST:
                    pe.wait_ge(q_kept, f.n)
                transposes_pe(nc, xn, QX, ident, xnT_psum)

            def project(f, o, lo, hi, t):
                for c in range(DC):
                    K = DP + 1 - c
                    mm = nc.tensor.matmul(o, xnT[f.b][0:K, c, t * TP:(t + 1) * TP], w_in[0:K, c, lo:hi], start=c == 0, stop=c == 1)
                return mm

            def project_z(f):
                pe.wait_ge(xnT_done, f.n + 1)
                for t in range(TT):
                    mm = project(f, Z[t][0:TP, 0:2 * D], 0, 2 * D, t)
                mm.then_inc(z_psum, 1)

            def project_kl(f):
                for t in range(TT):
                    mm = project(f, KL[0:TP, t * (D + HEADS):(t + 1) * (D + HEADS)], 2 * D, 3 * D + HEADS, t)
                mm.then_inc(kl_psum, 1)

            def project_q(m):
                for o in range(DC):
                    for c in range(DC):
                        K = DP + 1 - c
                        mm = nc.tensor.matmul(QX[0:DP, o * TOKENS:(o + 1) * TOKENS], w_qT[0:K, c, o * DP:(o + 1) * DP],
                                              xnT[m.b][0:K, c], start=c == 0, stop=c == 1)
                mm.then_inc(q_psum, 1)

            def gradient(m):
                pe.wait_ge(grad_in_done, m.n + 1)
                pe.wait_ge(acts_in_done, m.n + 1)
                for c in range(DC):
                    for t in range(TT):
                        mm = nc.tensor.matmul(GB[0:DP + 1, c * DP:(c + 1) * DP], k1[:, t, c], g[:, t, c * DP:(c + 1) * DP],
                                              start=t == 0, stop=t == 1)
                mm.then_inc(grad_done, 1)

            def zbar(m):
                pe.wait_ge(w1n_done, m.n + 1)
                pe.wait_ge(q_kept, m.n + 1)
                for t in range(TT):
                    for c in range(DC):
                        mm = nc.tensor.matmul(GB[0:TP, t * D + c * DP:t * D + (c + 1) * DP], qT[:, c, t * TP:(t + 1) * TP],
                                              w_1n[:, c], start=True, stop=True)
                mm.then_inc(zbar_psum, 1)

            def turn_zb(m):
                pe.wait_ge(zb_done, m.n + 1)
                transposes_pe(nc, zb, KL, ident, zbT_psum)

            def project_out(m):
                for t in range(TT):
                    o, ts = GB[0:TP, t * D:(t + 1) * D], slice(t * TP, (t + 1) * TP)
                    nc.tensor.matmul(o, xnT[m.b][0:DP + 1, 0, ts], w_qp[:, 0], start=t == 0, stop=False, skip_group_check=True)
                    nc.tensor.matmul(o, xnT[m.b][0:DP, 1, ts], w_qp[0:DP, 1], start=False, stop=False, skip_group_check=True)
                pe.wait_ge(zbT_done, m.n + 1)
                for t in range(TT):
                    o, ts = GB[0:TP, t * D:(t + 1) * D], slice(t * TP, (t + 1) * TP)
                    for c in range(DC):
                        mm = nc.tensor.matmul(o, zbT[:, c, ts], w_pg[:, c], start=False, stop=c == 1, skip_group_check=True)
                mm.then_inc(out_psum, 1)

            def m_turn_x(n):
                pe.wait_ge(m_xn_done, n.n + 1)
                transposes_pe(nc, m_xn, YB, ident, m_xnT_psum)

            def router(n):
                pe.wait_ge(m_xnT_done, n.n + 1)
                for t in range(TT):
                    for c in range(DC):
                        K = DP + 1 - c
                        mm = nc.tensor.matmul(YB[0:TP, t * EXPERTS:(t + 1) * EXPERTS], m_xnT[0:K, c, t * TP:(t + 1) * TP],
                                              w_r[0:K, c], start=c == 0, stop=c == 1)
                mm.then_inc(logits_psum, 1)

            def hidden(n, e):
                for o in range(DC):
                    for c in range(DC):
                        K = DP + 1 - c
                        mm = nc.tensor.matmul(HB[e % 2][0:DP, o * TOKENS:(o + 1) * TOKENS], w_1[0:K, c, e, o * DP:(o + 1) * DP],
                                              m_xnT[0:K, c], start=c == 0, stop=c == 1)
                mm.then_inc(hid_psum, 1)

            def output(n, e):
                pe.wait_ge(gelu_done, n.n * 4 + (e + 1))
                if e == 0:
                    pe.wait_ge(logits_read, n.n + 1)
                else:
                    pe.wait_ge(y_used, n.n * 4 + e)
                for t in range(TT):
                    for c in range(DC):
                        K = DP + 1 - c
                        mm = nc.tensor.matmul(YB[0:TP, t * D:(t + 1) * D], hidT[e % 2][0:K, c, t * TP:(t + 1) * TP],
                                              w_2[0:K, c, e], start=c == 0, stop=c == 1)
                mm.then_inc(y_psum, 1)

            def body(f, m, n):
                if m is not None: project_q(m)
                if n is not None: m_turn_x(n)
                if f is not None: embed(f)
                if n is not None: router(n)
                if n is not None: hidden(n, 0)
                if n is not None: hidden(n, 1)
                if m is not None: gradient(m)
                if n is not None: output(n, 0)
                if f is not None: turn_x(f)
                if n is not None: hidden(n, 2)
                if m is not None: zbar(m)
                if f is not None: project_z(f)
                if n is not None: output(n, 1)
                if n is not None: hidden(n, 3)
                if n is not None: output(n, 2)
                if m is not None: turn_zb(m)
                if m is not None: project_out(m)
                if n is not None: output(n, 3)
                if f is not None: project_kl(f)

            body(Image(FIRST, 0, 0), None, None)
            body(Image(1, 1, 0), Image(0, 0, 0), None)
            with pe.Fori(0, PAIRS - 1) as i:
                body(Image(i * 2 + 2, 0, i + 1), Image(i * 2 + 1, 1, i), Image(i * 2, 0, i))
                body(Image(i * 2 + 3, 1, i + 1), Image(i * 2 + 2, 0, i + 1), Image(i * 2 + 1, 1, i))
            body(None, Image(IMAGES - 1, 1, PAIRS - 1), Image(IMAGES - 2, 0, PAIRS - 1))
            body(None, None, Image(IMAGES - 1, 1, PAIRS - 1))

        @block.scalar
        def _(act):
            def flat(ap):
                return ap.rearrange("p c t -> p (c t)")

            def h_out(f):
                act.wait_ge(tok_done, f.n + 1)
                nc.scalar.copy(H[:, f.n], Z[0][0:TP, 0:TT * D]).then_inc(h_kept, 1)

            def xnT_out(f):
                act.wait_ge(xnT_psum, f.n + 1)
                nc.scalar.copy(flat(xnT[f.b][0:DP]), QX[0:DP, 0:DC * TOKENS]).then_inc(xnT_done, 1)

            def z_out(f):
                act.wait_ge(z_psum, f.n + 1)
                for t in range(TT):
                    nc.scalar.activation(sq[:, t], Z[t][0:TP, 0:D], ACT.Square).then_inc(sq_done, 1)
                for t in range(TT):
                    ins = nc.scalar.copy(zt[:, t].rearrange("p a d -> p (a d)"), Z[t][0:TP, 0:2 * D])
                ins.then_inc(z_kept, 1)

            def kl_out(f):
                act.wait_ge(kl_psum, f.n + 1)
                kl = KL[0:TP, 0:TT * (D + HEADS)].rearrange("p (t w) -> p t w", t=TT)
                nc.scalar.activation(lr[:], kl[:, :, D:], ACT.Exp, scale=-1.0)
                for t in range(TT):
                    ins = nc.scalar.copy(k1[:, t, :, 0:DP], kl[:, t, 0:D].rearrange("p (c e) -> p c e", c=DC))
                ins.then_inc(acts_in_done, 1)

            def q_out(m):
                act.wait_ge(q_psum, m.n + 1)
                nc.scalar.copy(flat(qT[0:DP]), QX[0:DP, 0:DC * TOKENS]).then_inc(q_kept, 1)

            def zbar_squares(m):
                act.wait_ge(zbar_psum, m.n + 1)
                nc.scalar.activation(zsq[:].rearrange("p t d -> p (t d)"), GB[0:TP, 0:TT * D], ACT.Square).then_inc(zbar_sq_done, 1)

            def zbT_out(m):
                act.wait_ge(zbT_psum, m.n + 1)
                nc.scalar.copy(flat(zbT[:]), KL[0:DP, 0:DC * TOKENS]).then_inc(zbT_done, 1)

            def m_xnT_out(n):
                act.wait_ge(m_xnT_psum, n.n + 1)
                nc.scalar.copy(flat(m_xnT[0:DP]), YB[0:DP, 0:DC * TOKENS]).then_inc(m_xnT_done, 1)

            def gelu(n, e):
                act.wait_ge(hid_psum, n.n * 4 + (e + 1))
                if e >= 2:
                    act.wait_ge(y_psum, n.n * 4 + (e - 1))
                nc.scalar.activation(flat(hidT[e % 2][0:DP]), HB[e % 2][0:DP, 0:DC * TOKENS], ACT.Gelu).then_inc(gelu_done, 1)

            def body(f, m, n):
                if m is not None: q_out(m)
                if n is not None: m_xnT_out(n)
                if f is not None: h_out(f)
                if n is not None: gelu(n, 0)
                if n is not None: gelu(n, 1)
                if f is not None: xnT_out(f)
                if n is not None: gelu(n, 2)
                if m is not None: zbar_squares(m)
                if f is not None: z_out(f)
                if n is not None: gelu(n, 3)
                if m is not None: zbT_out(m)
                if f is not None: kl_out(f)

            act.wait_ge(weights_ready, 1)
            body(Image(FIRST, 0, 0), None, None)
            body(Image(1, 1, 0), Image(0, 0, 0), None)
            with act.Fori(0, PAIRS - 1) as i:
                body(Image(i * 2 + 2, 0, i + 1), Image(i * 2 + 1, 1, i), Image(i * 2, 0, i))
                body(Image(i * 2 + 3, 1, i + 1), Image(i * 2 + 2, 0, i + 1), Image(i * 2 + 1, 1, i))
            body(None, Image(IMAGES - 1, 1, PAIRS - 1), Image(IMAGES - 2, 0, PAIRS - 1))
            body(None, None, Image(IMAGES - 1, 1, PAIRS - 1))

        @block.vector
        def _(dve):
            nc.vector.memset(w_in[:], 0.0)
            nc.vector.memset(w_1c[:], 0.0)
            for rows in (xnT[0], xnT[1], qT, m_xnT, hidT[0], hidT[1]):
                nc.vector.memset(rows[DP:DP + 1], 1.0)
            nc.vector.memset(k1[:], 1.0)
            nc.vector.memset(w_q[:], 0.0).then_inc(cleared, 1)
            dve.wait_ge(weights_in, 16 * WEIGHT_DMAS)
            dve.wait_ge(cleared, 1)
            prep = Steps(dve, prep_steps, 0)
            for dc in range(DC):
                ins = nc.vector.tensor_tensor(w_q[:, dc, DP:DP + 1], q_col[:, dc:dc + 1], beta_col[:, dc:dc + 1], ALU.add)
            ins.then_inc(prep_dve, 1)
            prep.done(nc.vector.tensor_reduce(sums[:], w_1c[:].rearrange("p c (h e) -> p (c h) e", e=HD), AX_X, ALU.add))
            prep.settle()
            w1g = w_1c[:].rearrange("p c (h e) -> p (c h) e", e=HD)
            nc.vector.scalar_tensor_tensor(w1g, sums[:].unsqueeze(2).to_broadcast([DP + 1, HEADS, HD]), -1.0 / HD, w1g,
                                           ALU.mult, ALU.add).then_inc(prep_dve, 1)
            for c in range(DC):
                prep.done(nc.vector.tensor_tensor(w_vT[:, c], w_vT[:, c], w_kT[:, c], ALU.subtract))
            prep.done(nc.vector.tensor_tensor(gamma2[:], gamma_row[:], gamma_row[:], ALU.mult))
            prep.settle()
            for c in range(DC):
                prep.done(nc.vector.tensor_tensor(w_in[0:DP + 1, c, D:2 * D], w_vT[:, c], gamma_row[0:DP + 1], ALU.mult))
                prep.done(nc.vector.tensor_scalar(w_pg[:, c], w_pT[:, c], gamma_col[:, c:c + 1], None, ALU.mult))
            dve.wait_ge(prep_pe, 2)
            dve.wait_ge(prep_dve, 2)
            prep.done(nc.vector.tensor_tensor(w_qp[DP:DP + 1, 0], banks[0][DP:DP + 1, 0:D], p_bias[DP:DP + 1], ALU.add))
            prep.done(nc.vector.tensor_copy(w_qp[0:DP, 0], banks[0][0:DP, 0:D]))
            prep.done(nc.vector.tensor_copy(w_qp[0:DP, 1], banks[1][0:DP, 0:D]))
            prep.done(nc.vector.tensor_copy(w_in[DP:DP + 1, 0, 0:D], w_1c[DP:DP + 1].rearrange("p c e -> p (c e)")))
            prep.done(nc.vector.tensor_copy(w_in[0:DP, 0, 0:D], banks[2][0:DP, 0:D]))
            prep.done(nc.vector.tensor_copy(w_in[0:DP, 1, 0:D], banks[3][0:DP, 0:D]))
            prep.settle()
            dve.sem_inc(weights_ready, 1)

            def spread(stat, n=TT * HEADS):
                return stat.unsqueeze(2).to_broadcast([TP, n, HD])

            def variance(own, out, squares, done):
                own.done(nc.vector.tensor_reduce(out[:], heads(squares[:]), AX_X, ALU.add))
                own.settle()
                nc.vector.tensor_scalar(out[:], out[:], 1.0 / HD, TTT_EPS, ALU.mult, ALU.add).then_inc(done, 1)

            def layernorm(f, own):
                dve.wait_ge(h_kept, f.n + 1)
                nc.vector.memset(veps[:], 0.0)
                layernorm_dve(nc, dve, own, H, f.n, stats, mv, veps, veps_done)

            def normalise(f):
                dve.wait_ge(rstd_done, f.n + 1)
                normalise_dve(nc, H, f.n, mv, rstd, xn, xn_done)

            def z_variance(f, own):
                dve.wait_ge(sq_done, f.n * 2 + 2)
                variance(own, gvar, sq, gvar_done)

            def x_hat(m):
                dve.wait_ge(grstd_done, m.n + 1)
                dve.wait_ge(z_kept, m.n + 1)
                for t in range(TT):
                    ins = nc.vector.tensor_tensor(heads(xh[:, t]), heads(zt[:, t, 0]),
                                                  spread(grstd[:, t * HEADS:(t + 1) * HEADS], HEADS), ALU.mult)
                ins.then_inc(xh_done, 1)

            def coefficient(m, own):
                dve.wait_ge(acts_in_done, m.n + 1)
                own.done(nc.vector.tensor_scalar(coef[:], lr[:].rearrange("p t h -> p (t h)"), 1.0, None, ALU.add))
                own.settle()
                own.done(nc.vector.reciprocal(coef[:], coef[:]))
                own.settle()
                own.done(nc.vector.scalar_tensor_tensor(coef[:], coef[:], 1.0 / (HD * TOKENS), grstd[:], ALU.mult, ALU.mult))

            def less_target(m):
                dve.wait_ge(g2x_done, m.n + 1)
                nc.vector.tensor_tensor(g[:], g[:], zt[:, :, 1], ALU.subtract).then_inc(g_done, 1)

            def grad_in(m, own):
                dve.wait_ge(gx_done, m.n + 1)
                own.done(nc.vector.tensor_reduce(sgx[:], heads(gx[:]), AX_X, ALU.add))
                own.settle()
                own.done(nc.vector.scalar_tensor_tensor(heads(gx[:]), heads(xh[:]), 1.0 / HD, spread(sgx[:]), ALU.mult, ALU.mult))
                own.settle()
                own.done(nc.vector.tensor_tensor(g[:], g[:], gx[:], ALU.subtract))
                own.settle()
                nc.vector.tensor_tensor(heads(g[:]), heads(g[:]), spread(coef[:]), ALU.mult).then_inc(grad_in_done, 1)

            def new_w1(m, own):
                dve.wait_ge(grad_done, m.n + 1)
                grad = GB[0:DP + 1, 0:D]
                own.done(nc.vector.tensor_reduce(gsum[:], heads(grad), AX_X, ALU.add))
                own.settle()
                own.done(nc.vector.scalar_tensor_tensor(heads(gc[:]), gsum[:].unsqueeze(2).to_broadcast([DP + 1, HEADS, HD]),
                                                        -1.0 / HD, heads(grad), ALU.mult, ALU.add))
                own.settle()
                own.done(nc.vector.tensor_tensor(gc[:], gc[:], head_mask[:], ALU.mult))
                own.settle()
                nc.vector.tensor_tensor(w_1n[:].rearrange("p c e -> p (c e)"), w_1c[:].rearrange("p c e -> p (c e)"),
                                        gc[:], ALU.subtract).then_inc(w1n_done, 1)

            def zbar_variance(m, own):
                dve.wait_ge(zbar_sq_done, m.n + 1)
                variance(own, zvar, zsq, zvar_done)

            def normalise_zbar(m):
                dve.wait_ge(zrstd_done, m.n + 1)
                nc.vector.tensor_tensor(heads(zb[:]), GB[0:TP, 0:TT * D].rearrange("p (g e) -> p g e", e=HD),
                                        spread(zrstd[:]), ALU.mult).then_inc(zb_done, 1)

            def add_residual(m):
                dve.wait_ge(out_psum, m.n + 1)
                nc.vector.tensor_tensor(H[:, m.n], H[:, m.n], GB[0:TP, 0:TT * D], ALU.add).then_inc(h_added, 1)

            def m_layernorm(n, own):
                dve.wait_ge(h_added, n.n + 1)
                nc.vector.memset(m_veps[:], 0.0)
                layernorm_dve(nc, dve, own, H, n.n, m_stats, m_mv, m_veps, m_veps_done)

            def m_normalise(n):
                dve.wait_ge(m_rstd_done, n.n + 1)
                normalise_dve(nc, H, n.n, m_mv, m_rstd, m_xn, m_xn_done)

            def residuals(n, own):
                dve.wait_ge(m_xn_done, n.n + 1)
                own.done(nc.vector.tensor_tensor(acc[:].rearrange("p t d -> p (t d)"), H[:, n.n],
                                                 m_xn[:].rearrange("p t d -> p (t d)"), ALU.add))

            def read_logits(n):
                dve.wait_ge(logits_psum, n.n + 1)
                nc.vector.tensor_copy(logits[:].rearrange("p t e -> p (t e)"), YB[0:TP, 0:TT * EXPERTS]).then_inc(logits_read, 1)

            def choose(n, own):
                dve.wait_ge(logits_read, n.n + 1)
                own.done(nc.vector.tensor_reduce(top[:], logits[:], AX_X, ALU.max))
                own.settle()
                own.done(nc.vector.tensor_tensor(chosen[:], logits[:], top[:].unsqueeze(2).to_broadcast([TP, TT, EXPERTS]), ALU.is_equal))
                own.settle()
                own.done(nc.vector.tensor_scalar(left[:], chosen[:, :, 0], -1.0, 1.0, ALU.mult, ALU.add))
                for e in range(1, EXPERTS):
                    own.settle()
                    own.done(nc.vector.tensor_tensor(chosen[:, :, e], chosen[:, :, e], left[:], ALU.mult))
                    if e < EXPERTS - 1:
                        own.settle()
                        own.done(nc.vector.tensor_tensor(left[:], left[:], chosen[:, :, e], ALU.subtract))

            def add_expert(n, e, own):
                dve.wait_ge(y_psum, n.n * 4 + (e + 1))
                if e == 0:
                    own.settle()
                else:
                    dve.wait_ge(y_used, n.n * 4 + e)
                for t in range(TT):
                    dst = acc[:, t] if e < EXPERTS - 1 else H[:, n.n, t * D:(t + 1) * D]
                    ins = nc.vector.scalar_tensor_tensor(dst, YB[0:TP, t * D:(t + 1) * D], chosen[:, t, e:e + 1], acc[:, t],
                                                         ALU.mult, ALU.add)
                ins.then_inc(y_used, 1)

            def body(f, m, n):
                if f is not None: early = Steps(dve, early_steps, f.n * EARLY_STEPS)
                if m is not None: late = Steps(dve, late_steps, m.n * LATE_STEPS)
                if n is not None: moe = Steps(dve, moe_steps, n.n * MOE_STEPS)
                if n is not None: m_layernorm(n, moe)
                if m is not None: x_hat(m)
                if n is not None: m_normalise(n)
                if m is not None: coefficient(m, late)
                if m is not None: less_target(m)
                if m is not None: grad_in(m, late)
                if f is not None: layernorm(f, early)
                if n is not None: read_logits(n)
                if f is not None: normalise(f)
                if m is not None: new_w1(m, late)
                if n is not None: choose(n, moe)
                if n is not None: residuals(n, moe)
                if n is not None: add_expert(n, 0, moe)
                if m is not None: zbar_variance(m, late)
                if f is not None: z_variance(f, early)
                if n is not None: add_expert(n, 1, moe)
                if m is not None: normalise_zbar(m)
                if n is not None: add_expert(n, 2, moe)
                if m is not None: add_residual(m)
                if n is not None: add_expert(n, 3, moe)
                assert f is None or early.n == EARLY_STEPS
                assert m is None or late.n == LATE_STEPS
                assert n is None or moe.n == MOE_STEPS

            body(Image(FIRST, 0, 0), None, None)
            body(Image(1, 1, 0), Image(0, 0, 0), None)
            with dve.Fori(0, PAIRS - 1) as i:
                body(Image(i * 2 + 2, 0, i + 1), Image(i * 2 + 1, 1, i), Image(i * 2, 0, i))
                body(Image(i * 2 + 3, 1, i + 1), Image(i * 2 + 2, 0, i + 1), Image(i * 2 + 1, 1, i))
            body(None, Image(IMAGES - 1, 1, PAIRS - 1), Image(IMAGES - 2, 0, PAIRS - 1))
            body(None, None, Image(IMAGES - 1, 1, PAIRS - 1))


GH = 3
GROUPS = HEADS // GH
SLOT = 32
CAUSAL = TOKENS + TP
SLOTS = 1024
ST = SLOTS // 128
QUARTERS = 4
QW = SLOTS // QUARTERS
PHI_EPS = 1e-6


def attention_dispatch_stage(nc, a, H, ident, phi, neg_row_max, slots_dram):
    FRONT_STEPS = 3
    ATT_STEPS = 7
    DIS_STEPS = 15
    with ExitStack() as ctx:
        st = Stage(nc, ctx, "ad")
        sb, sem = st.sb, st.sem
        ps = ctx.enter_context(nc.psum_tensor("ad_psum", [128, 8, 512], F32))
        COLS = (4, 7)
        ROWS, SUMS, TURN = 5, 6, 7

        w_in = sb("w_in", [DP + 1, DC, 3 * D])
        w_raw = sb("w_raw", [DP, DC, 3 * D])
        b_raw = sb("b_raw", [DP + 1, 3 * D])
        scale_col = sb("scale_col", [DP, DC])
        shift_col = sb("shift_col", [DP, DC])
        shift_w = sb("shift_w", [DP, DC, DP + 1])
        w_out = sb("w_out", [DP + 1, DC, D])
        rezero = sb("rezero", [DP + 1, 1])
        sinks = sb("sinks", [TP, HEADS])
        cos = sb("cos", [TP, TT, HD])
        sin = sb("sin", [TP, TT, HD])
        mask_qk_f = sb("mask_qk_f", [TP, TP])
        mask_kq_f = sb("mask_kq_f", [TP, TP])
        sel_f = sb("sel_f", [GH * SLOT, HEADS, TP])
        mask_qk = sb("mask_qk", [TP, TP], BF16)
        mask_kq = sb("mask_kq", [TP, TP], BF16)
        sel = sb("sel", [GH * SLOT, HEADS, TP], BF16)
        mhalf = sb("mhalf", [128, 24])
        ident_b = sb("ident_b", [128, 128], BF16)
        phi_sq = sb("phi_sq", [DP, DC, SLOTS])
        phi_sum = sb("phi_sum", [DP, DC, ST, 2])

        xn = sb("xn", [TP, TT, D])
        xnT = sb("xnT", [DP + 1, DC, TOKENS])
        stats = sb("stats", [TP, TT, 6])
        mv = sb("mv", [TP, TT, 2])
        veps = sb("veps", [TP, TT])
        rstd = sb("rstd", [TP, TT])
        rot_c = sb("rot_c", [TP, TT, 2 * D])
        rot_s = sb("rot_s", [TP, TT, 2 * D])
        qk = sb("qk", [TP, TT, 2 * HEADS, SLOT])
        kT = sb("kT", [GH * SLOT, GROUPS, TOKENS])
        qT = sb("qT", [GH * SLOT, GROUPS, GH, TOKENS])
        v1 = sb("v1", [TP, TT, HEADS, SLOT])
        y_raw = sb("y_raw", [GH * SLOT, GROUPS, TOKENS])
        peak = sb("peak", [TP, TT, HEADS])
        npk_hi = sb("npk_hi", [TP, TT, HEADS], BF16)
        npk_lo = sb("npk_lo", [TP, TT, HEADS], BF16)
        npk = sb("npk", [TP, TT, GH, SLOT], BF16)
        npkT = sb("npkT", [GH * SLOT, TOKENS], BF16)
        sink_w = sb("sink_w", [TP, TT, HEADS])
        weights = [sb(f"weights{g}", [TP, GH, CAUSAL]) for g in range(2)]
        den = sb("den", [TP, TT, HEADS])
        y = sb("y", [TP, TT, D])
        yT = sb("yT", [DP + 1, DC, TOKENS])

        d_xn = sb("d_xn", [TP, TT, D + 1])
        d_xnT = sb("d_xnT", [DP, DC, TOKENS])
        d_stats = sb("d_stats", [TP, TT, 6])
        d_mv = sb("d_mv", [TP, TT, 2])
        d_veps = sb("d_veps", [TP, TT])
        d_rstd = sb("d_rstd", [TP, TT])
        col_peak = sb("col_peak", [128, 2, 2])
        max_q = sb("max_q", [128, QUARTERS, TOKENS])
        max_all = sb("max_all", [128, TOKENS])
        col_weights = [sb(f"col_weights{q}", [128, 2, TOKENS]) for q in range(2)]
        d_weights = [sb(f"d_weights{q}", [TP, TT, QW]) for q in range(2)]
        s_stats = sb("s_stats", [128, 2, 6])
        s_mv = sb("s_mv", [128, 2, 2])
        s_den = sb("s_den", [128, 2])
        s_veps = sb("s_veps", [128, 2])
        s_rstd = sb("s_rstd", [128, 2])
        slot_in = sb("slot_in", [128, ST, D])

        cleared = sem("cleared")
        weights_in = sem("weights_in")
        prep_psum = sem("prep_psum")
        phi_summed = sem("phi_summed")
        phi_rstd = sem("phi_rstd")
        weights_ready = sem("weights_ready")
        veps_done = sem("veps_done")
        rstd_done = sem("rstd_done")
        xn_done = sem("xn_done")
        xnT_psum = sem("xnT_psum")
        xnT_done = sem("xnT_done")
        qkv_psum = sem("qkv_psum")
        v_kept = sem("v_kept")
        qk_done = sem("qk_done")
        qkT_psum = sem("qkT_psum")
        qkT_done = sem("qkT_done")
        scores_psum = sem("scores_psum")
        peaks_read = sem("peaks_read")
        npk_done = sem("npk_done")
        sink_arg = sem("sink_arg")
        npkT_psum = sem("npkT_psum")
        npkT_done = sem("npkT_done")
        sink_done = sem("sink_done")
        shifted_psum = sem("shifted_psum")
        exp_done = sem("exp_done")
        pv_done = sem("pv_done")
        y_raw_done = sem("y_raw_done")
        y_back = sem("y_back")
        y_done = sem("y_done")
        yT_psum = sem("yT_psum")
        yT_done = sem("yT_done")
        out_psum = sem("out_psum")
        h_added = sem("h_added")
        front_steps = sem("front_steps")
        att_steps = sem("att_steps")
        d_veps_done = sem("d_veps_done")
        d_rstd_done = sem("d_rstd_done")
        d_xn_done = sem("d_xn_done")
        d_xnT_psum = sem("d_xnT_psum")
        d_xnT_done = sem("d_xnT_done")
        cols_psum = sem("cols_psum")
        col_peaks_done = sem("col_peaks_done")
        d_exp_done = sem("d_exp_done")
        rows_psum = sem("rows_psum")
        d_weights_done = sem("d_weights_done")
        max_all_done = sem("max_all_done")
        maxT_psum = sem("maxT_psum")
        slots_psum = sem("slots_psum")
        s_veps_done = sem("s_veps_done")
        s_rstd_done = sem("s_rstd_done")
        slots_done = sem("slots_done")
        stored = sem("stored")
        dis_steps = sem("dis_steps")
        LOADS = 16
        block = ctx.enter_context(nc.Block())

        @block.sync
        def _(sp):
            sp.wait_ge(cleared, 1)
            loads = ((w_raw[:], a["attn_w"]), (b_raw[DP:DP + 1], a["attn_b"]), (scale_col[:], a["norm_scale"]),
                     (shift_col[:], a["norm_bias"]), (w_out[0:DP], a["attn_pw"]), (w_out[DP:DP + 1, 0], a["attn_pb"]),
                     (rezero[:], a["rezero"].partition_broadcast(DP + 1).rearrange("p o d -> p (o d)")),
                     (sinks[:], a["sinks"].partition_broadcast(TP).rearrange("p o d -> p (o d)")),
                     (cos[:], a["rope_cos"]), (sin[:], a["rope_sin"]), (mask_qk_f[:], a["mask_qk"]),
                     (mask_kq_f[:], a["mask_kq"]), (sel_f[:], a["head_sel"]), (mhalf[:], a["mhalf"]),
                     (ident[:], a["ident"]), (phi[:], a["phi"]))
            assert len(loads) == LOADS, len(loads)
            for dst, src in loads:
                sp.dma_start(dst, src).then_inc(weights_in, 16)
            with sp.Fori(0, IMAGES) as n:
                sp.wait_ge(slots_done, n * 4 + 4)
                sp.dma_start(slots_dram[:, n], slot_in[:].rearrange("p j d -> p (j d)")).then_inc(stored, 16)
            sp.wait_ge(stored, 16 * IMAGES + 16)

        @block.gpsimd
        def _(pool):
            def power(ready, count, out, x, done):
                pool.wait_ge(ready, count)
                nc.gpsimd.tensor_tensor(out, x, mhalf[0:x.shape[0], 0:x.shape[1]], ALU.pow).then_inc(done, 1)

            pool.wait_ge(weights_in, 16 * LOADS)
            flat = phi_sum[:].rearrange("p c j r -> p (c j r)")
            for part in (flat[:, 0:16], flat[:, 16:32]):
                power(phi_summed, 1, part, part, phi_rstd)

            def root(n):
                power(veps_done, n + 1, rstd[:], veps[:], rstd_done)

            def d_root(n):
                power(d_veps_done, n + 1, d_rstd[:], d_veps[:], d_rstd_done)

            def slot_root(n, q):
                power(s_veps_done, n * 4 + (q + 1), s_rstd[:], s_veps[:], s_rstd_done)

            def body(m, n, f):
                B, C = n is not None, f is not None
                if B: d_root(n)
                if B: slot_root(n, 0)
                if B: slot_root(n, 1)
                if B: slot_root(n, 2)
                if C: root(f)
                if B: slot_root(n, 3)

            body(None, None, 0)
            body(FIRST, None, 1)
            with pool.Fori(0, IMAGES - 2) as n:
                body(n + 1, n, n + 2)
            body(IMAGES - 1, IMAGES - 2, None)
            body(None, IMAGES - 1, None)

        @block.tensor
        def _(pe):
            pe.wait_ge(weights_in, 16 * LOADS)
            pe.wait_ge(prep_psum, 1)
            for part, (lo, hi) in enumerate(((0, 2 * D), (2 * D, 3 * D))):
                for c in range(DC):
                    mm = nc.tensor.matmul(ps[0:DP + 1, part, 0:hi - lo], shift_w[:, c], w_raw[:, c, lo:hi],
                                          start=c == 0, stop=c == 1)
            mm.then_inc(prep_psum, 1)
            pe.wait_ge(weights_ready, 1)

            def turn_x(n):
                pe.wait_ge(xn_done, n + 1)
                if n is not FIRST:
                    pe.wait_ge(y_raw_done, n * 2)
                transposes_pe(nc, xn, ps[:, 3], ident, xnT_psum)

            def qkv(n, t, columns):
                pe.wait_ge(xnT_done, n + 1)
                o = ps[0:TP, 2 * t, 0:2 * D] if columns == 0 else ps[0:TP, 3, t * D:(t + 1) * D]
                lo, hi = ((0, 2 * D), (2 * D, 3 * D))[columns]
                for c in range(DC):
                    K = DP + 1 - c
                    mm = nc.tensor.matmul(o, xnT[0:K, c, t * TP:(t + 1) * TP], w_in[0:K, c, lo:hi], start=c == 0, stop=c == 1)
                mm.then_inc(qkv_psum, 1)

            def turn_qk(n):
                pe.wait_ge(qk_done, n + 1)
                pe.wait_ge(v_kept, n + 1)
                if n is not FIRST:
                    pe.wait_ge(h_added, n)
                for g in range(GROUPS):
                    for kind in range(2):
                        for t in range(TT):
                            h0 = kind * HEADS + g * GH
                            mm = nc.tensor.transpose(ps[0:GH * SLOT, g, kind * TOKENS + t * TP:kind * TOKENS + (t + 1) * TP],
                                                     qk[:, t, h0:h0 + GH].rearrange("p h s -> p (h s)"), ident[0:TP, 0:TP])
                mm.then_inc(qkT_psum, 1)

            def scores(n, g):
                if g == 0:
                    pe.wait_ge(qkT_done, n * 2 + 2)
                for j in range(GH):
                    h = g * GH + j
                    if h >= GH:
                        pe.wait_ge(peaks_read, n * HEADS + (h - GH + 1))
                    for t, o in ((0, ps[0:TP, j, 0:TP]), (1, ps[0:TP, j, TP:CAUSAL])):
                        nc.tensor.matmul(o, qT[:, g, j, t * TP:(t + 1) * TP], kT[:, g, 0:(t + 1) * TP],
                                         start=t == 0, stop=True, skip_group_check=True)
                    for m in (ps[0:TP, j, 0:TP], ps[0:TP, j, TOKENS:CAUSAL]):
                        mm = nc.tensor.matmul(m, ident_b[0:TP, 0:TP], mask_qk[:], start=False, stop=True, skip_group_check=True)
                    mm.then_inc(scores_psum, 1)

            def turn_peaks(n):
                pe.wait_ge(npk_done, n + 1)
                for t in range(TT):
                    mm = nc.tensor.transpose(ps[0:GH * SLOT, 3, 0:TP].bitcast(BF16)[:, t * TP:(t + 1) * TP],
                                             npk[:, t].rearrange("p j s -> p (j s)"), ident_b[0:TP, 0:TP])
                mm.then_inc(npkT_psum, 1)

            def shifted(n, g):
                if g == 0:
                    pe.wait_ge(npkT_done, n + 1)
                for j in range(GH):
                    h = g * GH + j
                    if h >= GH:
                        pe.wait_ge(exp_done, n * HEADS + (h - GH + 1))
                    halves = ((0, ps[0:TP, j, 0:TOKENS]), (1, ps[0:TP, j, TOKENS:CAUSAL]))
                    for t, o in halves:
                        nc.tensor.matmul(o, kT[:, g, t * TP:(t + 1) * TP], qT[:, g, j, t * TP:TOKENS],
                                         start=t == 0, stop=True, skip_group_check=True)
                    for t, o in halves:
                        nc.tensor.matmul(o, sel[:, h], npkT[:, t * TP:TOKENS], start=False, stop=True, skip_group_check=True)
                    for m in (ps[0:TP, j, 0:TP], ps[0:TP, j, TOKENS:CAUSAL]):
                        mm = nc.tensor.matmul(m, ident_b[0:TP, 0:TP], mask_kq[:], start=False, stop=True, skip_group_check=True)
                    mm.then_inc(shifted_psum, 1)

            def values(n, g):
                pe.wait_ge(exp_done, n * HEADS + (g + 1) * GH)
                if g == 2:
                    pe.wait_ge(y_raw_done, n * 2 + 1)
                p = weights[g % 2]
                for j in range(GH):
                    h = g * GH + j
                    o = ps[SLOT * j:SLOT * (j + 1), 3, g % 2 * TOKENS:(g % 2 + 1) * TOKENS]
                    nc.tensor.matmul(o, v1[:, 0, h], p[:, j, 0:TOKENS], start=True, stop=True)
                    mm = nc.tensor.matmul(o[:, TP:], v1[:, 1, h], p[:, j, TOKENS:CAUSAL], start=False, stop=True,
                                          skip_group_check=True)
                mm.then_inc(pv_done, 1)

            def turn_back(n):
                pe.wait_ge(y_raw_done, n * 2 + 2)
                for g in range(GROUPS):
                    for t in range(TT):
                        mm = nc.tensor.transpose(ps[0:TP, t, g * GH * SLOT:(g + 1) * GH * SLOT],
                                                 y_raw[:, g, t * TP:(t + 1) * TP], ident[0:GH * SLOT, 0:GH * SLOT])
                mm.then_inc(y_back, 1)

            def turn_y(n):
                pe.wait_ge(y_done, n + 1)
                transposes_pe(nc, y, ps[:, 0], ident, yT_psum)

            def project(n):
                pe.wait_ge(yT_done, n + 1)
                for t in range(TT):
                    for c in range(DC):
                        K = DP + 1 - c
                        mm = nc.tensor.matmul(ps[0:TP, 1, t * D:(t + 1) * D], yT[0:K, c, t * TP:(t + 1) * TP], w_out[0:K, c],
                                              start=c == 0, stop=c == 1)
                mm.then_inc(out_psum, 1)

            def d_turn_x(n):
                pe.wait_ge(d_xn_done, n + 1)
                transposes_pe(nc, d_xn, ps[:, TURN], ident, d_xnT_psum)

            def logits(n, q):
                if q == 0:
                    pe.wait_ge(d_xnT_done, n + 1)
                if q >= 2:
                    pe.wait_ge(d_exp_done, n * 4 + (q - 1))
                for s in range(2):
                    for c in range(DC):
                        mm = nc.tensor.matmul(ps[0:128, COLS[q % 2], s * TOKENS:(s + 1) * TOKENS],
                                              phi[:, c, (2 * q + s) * 128:(2 * q + s + 1) * 128], d_xnT[:, c],
                                              start=c == 0, stop=c == 1)
                mm.then_inc(cols_psum, 1)

            def turn_weights(n, q):
                pe.wait_ge(d_exp_done, n * 4 + (q + 1))
                if q > 0:
                    pe.wait_ge(d_weights_done, n * 4 + q)
                for t in range(TT):
                    for s in range(2):
                        mm = nc.tensor.transpose(ps[0:TP, ROWS, t * QW + s * 128:t * QW + (s + 1) * 128],
                                                 col_weights[q % 2][:, s, t * TP:(t + 1) * TP], ident[:])
                mm.then_inc(rows_psum, 1)

            def turn_max(n):
                pe.wait_ge(max_all_done, n + 1)
                for t in range(TT):
                    mm = nc.tensor.transpose(ps[0:TP, TURN, t * 128:(t + 1) * 128], max_all[:, t * TP:(t + 1) * TP], ident[:])
                mm.then_inc(maxT_psum, 1)

            def slot_sums(n, q):
                pe.wait_ge(d_weights_done, n * 4 + (q + 1))
                if q > 0:
                    pe.wait_ge(slots_done, n * 4 + q)
                for s in range(2):
                    for t in range(TT):
                        mm = nc.tensor.matmul(ps[0:128, SUMS, s * (D + 1):(s + 1) * (D + 1)],
                                              d_weights[q % 2][:, t, s * 128:(s + 1) * 128], d_xn[:, t], start=t == 0, stop=t == 1)
                mm.then_inc(slots_psum, 1)

            def body(m, n, f):
                A, B, C = m is not None, n is not None, f is not None
                if B: d_turn_x(n)
                if B: logits(n, 0)
                if B: logits(n, 1)
                if A: turn_qk(m)
                if B: turn_weights(n, 0)
                if B: logits(n, 2)
                if A: scores(m, 0)
                if B: slot_sums(n, 0)
                if A: scores(m, 1)
                if B: turn_weights(n, 1)
                if A: scores(m, 2)
                if A: scores(m, 3)
                if B: slot_sums(n, 1)
                if B: logits(n, 3)
                if B: turn_weights(n, 2)
                if A: turn_peaks(m)
                if A: shifted(m, 0)
                if B: slot_sums(n, 2)
                if A: shifted(m, 1)
                if A: values(m, 0)
                if B: turn_weights(n, 3)
                if A: shifted(m, 2)
                if A: values(m, 1)
                if A: shifted(m, 3)
                if A: values(m, 2)
                if A: values(m, 3)
                if B: turn_max(n)
                if C: turn_x(f)
                if A: turn_back(m)
                if B: slot_sums(n, 3)
                if A: turn_y(m)
                if C: qkv(f, 0, 1)
                if A: project(m)
                if C: qkv(f, 1, 0)
                if C: qkv(f, 1, 1)
                if C: qkv(f, 0, 0)

            body(None, None, 0)
            body(FIRST, None, 1)
            with pe.Fori(0, IMAGES - 2) as n:
                body(n + 1, n, n + 2)
            body(IMAGES - 1, IMAGES - 2, None)
            body(None, IMAGES - 1, None)

        @block.scalar
        def _(act):
            def xnT_out(n):
                act.wait_ge(xnT_psum, n + 1)
                nc.scalar.copy(xnT[0:DP].rearrange("p c t -> p (c t)"), ps[0:DP, 3, 0:DC * TOKENS]).then_inc(xnT_done, 1)

            def v_out(n):
                act.wait_ge(qkv_psum, n * 4 + 4)
                for t in range(TT):
                    ins = nc.scalar.copy(v1[:, t, :, 0:HD], ps[0:TP, 3, t * D:(t + 1) * D].rearrange("p (h e) -> p h e", e=HD))
                ins.then_inc(v_kept, 1)

            def qkT_out(n):
                act.wait_ge(qkT_psum, n + 1)
                nc.scalar.copy(kT[:, 0:2], ps[0:GH * SLOT, 0:2, TOKENS:2 * TOKENS])
                for j in range(GH):
                    rows = slice(SLOT * j, SLOT * (j + 1))
                    ins = nc.scalar.copy(qT[rows, 0:2, j], ps[rows, 0:2, 0:TOKENS])
                ins.then_inc(qkT_done, 1)

            def sink_exp(n):
                act.wait_ge(sink_arg, n + 1)
                nc.scalar.activation(sink_w[:], sink_w[:], ACT.Exp).then_inc(sink_done, 1)

            def weights_exp(n, g):
                if g >= 2:
                    act.wait_ge(pv_done, n * 4 + (g - 1))
                for j in range(GH):
                    act.wait_ge(shifted_psum, n * HEADS + (g * GH + j + 1))
                    nc.scalar.activation(weights[g % 2][:, j], ps[0:TP, j, 0:CAUSAL], ACT.Exp).then_inc(exp_done, 1)

            def y_raw_out(n, half):
                act.wait_ge(pv_done, n * 4 + (2 * half + 2))
                nc.scalar.copy(y_raw[:, 2 * half:2 * half + 2].rearrange("p g t -> p (g t)"),
                               ps[0:GH * SLOT, 3, 0:2 * TOKENS]).then_inc(y_raw_done, 1)

            def yT_out(n):
                act.wait_ge(yT_psum, n + 1)
                nc.scalar.copy(yT[0:DP].rearrange("p c t -> p (c t)"), ps[0:DP, 0, 0:DC * TOKENS]).then_inc(yT_done, 1)

            def d_xnT_out(n):
                act.wait_ge(d_xnT_psum, n + 1)
                nc.scalar.copy(d_xnT[:].rearrange("p c t -> p (c t)"), ps[0:DP, TURN, 0:DC * TOKENS]).then_inc(d_xnT_done, 1)

            def d_exp(n, q):
                act.wait_ge(col_peaks_done, n * 4 + (q + 1))
                if q >= 2:
                    act.wait_ge(rows_psum, n * 4 + (q - 1))
                for s in range(2):
                    ins = nc.scalar.activation(col_weights[q % 2][:, s], ps[0:128, COLS[q % 2], s * TOKENS:(s + 1) * TOKENS],
                                               ACT.Exp, bias=col_peak[:, q % 2, s:s + 1])
                ins.then_inc(d_exp_done, 1)

            def d_weights_out(n, q):
                act.wait_ge(rows_psum, n * 4 + (q + 1))
                if q >= 2:
                    act.wait_ge(slots_psum, n * 4 + (q - 1))
                nc.scalar.copy(d_weights[q % 2][:].rearrange("p t s -> p (t s)"), ps[0:TP, ROWS, 0:TT * QW]).then_inc(d_weights_done, 1)

            def body(m, n, f):
                A, B, C = m is not None, n is not None, f is not None
                if B: d_xnT_out(n)
                if A: v_out(m)
                if B: d_exp(n, 0)
                if A: qkT_out(m)
                if B: d_weights_out(n, 0)
                if B: d_exp(n, 1)
                if B: d_exp(n, 2)
                if B: d_weights_out(n, 1)
                if B: d_weights_out(n, 2)
                if B: d_exp(n, 3)
                if A: sink_exp(m)
                if A: weights_exp(m, 0)
                if A: weights_exp(m, 1)
                if B: d_weights_out(n, 3)
                if A: weights_exp(m, 2)
                if A: y_raw_out(m, 0)
                if A: weights_exp(m, 3)
                if A: y_raw_out(m, 1)
                if C: xnT_out(f)
                if A: yT_out(m)

            act.wait_ge(weights_ready, 1)
            body(None, None, 0)
            body(FIRST, None, 1)
            with act.Fori(0, IMAGES - 2) as n:
                body(n + 1, n, n + 2)
            body(IMAGES - 1, IMAGES - 2, None)
            body(None, IMAGES - 1, None)

        @block.vector
        def _(dve):
            nc.vector.memset(shift_w[:], 0.0)
            nc.vector.memset(xnT[DP:DP + 1], 1.0)
            nc.vector.memset(yT[DP:DP + 1], 1.0)
            nc.vector.memset(v1[:, :, :, HD + 1:], 0.0)
            nc.vector.memset(v1[:, :, :, HD:HD + 1], 1.0)
            nc.vector.memset(npk[:], 0.0)
            nc.vector.memset(qk[:], 0.0)
            nc.vector.memset(qT[:], 0.0)
            nc.vector.memset(d_xn[:], 1.0)
            nc.vector.memset(w_in[:], 0.0).then_inc(cleared, 1)
            dve.wait_ge(cleared, 1)
            dve.wait_ge(weights_in, 16 * LOADS)
            nc.vector.tensor_copy(shift_w[:, :, DP], shift_col[:]).then_inc(prep_psum, 1)
            prep = Steps(dve, att_steps, 0)
            for c in range(DC):
                nc.vector.tensor_scalar(w_in[0:DP, c], w_raw[:, c], scale_col[:, c:c + 1], None, ALU.mult)
            nc.vector.tensor_copy(ident_b[:], ident[:])
            nc.vector.tensor_copy(mask_qk[:], mask_qk_f[:])
            nc.vector.tensor_copy(mask_kq[:], mask_kq_f[:])
            nc.vector.tensor_copy(sel[:], sel_f[:])
            nc.vector.tensor_scalar(w_out[:, 0], w_out[:, 0], rezero[:], None, ALU.mult)
            nc.vector.tensor_scalar(w_out[0:DP, 1], w_out[0:DP, 1], rezero[0:DP], None, ALU.mult)
            prep.done(nc.vector.tensor_tensor(phi_sq[:], phi[:], phi[:], ALU.mult))
            prep.settle()
            for c in range(DC):
                prep.done(nc.vector.tensor_reduce(phi_sum[:, c], phi_sq[:, c].rearrange("p (j n r) -> p j r n", j=ST, r=2), AX_X, ALU.add))
            prep.settle()
            nc.vector.tensor_scalar(phi_sum[:], phi_sum[:], PHI_EPS, None, ALU.add).then_inc(phi_summed, 1)
            dve.wait_ge(prep_psum, 2)
            row = w_in[DP:DP + 1, 0]
            prep.done(nc.vector.tensor_tensor(row[:, 0:2 * D], ps[DP:DP + 1, 0, 0:2 * D], b_raw[DP:DP + 1, 0:2 * D], ALU.add))
            prep.done(nc.vector.tensor_tensor(row[:, 2 * D:], ps[DP:DP + 1, 1, 0:D], b_raw[DP:DP + 1, 2 * D:], ALU.add))
            prep.settle()
            prep.done(nc.vector.tensor_scalar(w_in[:, :, 0:D], w_in[:, :, 0:D], HD ** -0.5, None, ALU.mult))
            dve.wait_ge(phi_rstd, 2)
            for c in range(DC):
                v = phi[:, c].rearrange("p (j n r) -> p j n r", j=ST, r=2)
                prep.done(nc.vector.tensor_tensor(v, v, phi_sum[:, c].unsqueeze(2).to_broadcast([DP, ST, SLOTS // ST // 2, 2]), ALU.mult))
            prep.settle()
            dve.sem_inc(weights_ready, 1)
            dve.sem_inc(stored, 16)

            def rotate(n, own):
                dve.wait_ge(qkv_psum, n * 4 + 4)
                for t in range(TT):
                    src = ps[0:TP, 2 * t, 0:2 * D].rearrange("p (h e) -> p h e", e=HD)
                    dc = rot_c[:, t].rearrange("p (h e) -> p h e", e=HD)
                    ds = rot_s[:, t].rearrange("p (h e) -> p h e", e=HD)
                    half = [TP, 2 * HEADS, HD // 2]
                    nc.vector.tensor_tensor(dc, src, cos[:, t].unsqueeze(1).to_broadcast([TP, 2 * HEADS, HD]), ALU.mult)
                    for one, other in ((0, 1), (1, 0)):
                        ins = nc.vector.tensor_tensor(ds[:, :, one::2], src[:, :, other::2],
                                                      sin[:, t, one::2].unsqueeze(1).to_broadcast(half), ALU.mult)
                own.done(ins)
                own.settle()
                for t in range(TT):
                    ins = nc.vector.tensor_tensor(qk[:, t, :, 0:HD], rot_c[:, t].rearrange("p (h e) -> p h e", e=HD),
                                                  rot_s[:, t].rearrange("p (h e) -> p h e", e=HD), ALU.add)
                ins.then_inc(qk_done, 1)

            def peaks(n, g):
                for j in range(GH):
                    h = g * GH + j
                    dve.wait_ge(scores_psum, n * HEADS + (h + 1))
                    nc.vector.tensor_reduce(peak[:, 0, h:h + 1], ps[0:TP, j, 0:TP], AX_X, ALU.max)
                    nc.vector.tensor_reduce(peak[:, 1, h:h + 1], ps[0:TP, j, TP:CAUSAL], AX_X, ALU.max).then_inc(peaks_read, 1)

            def qkT_half(n):
                dve.wait_ge(qkT_psum, n + 1)
                nc.vector.tensor_copy(kT[:, 2:4], ps[0:GH * SLOT, 2:4, TOKENS:2 * TOKENS])
                for j in range(GH):
                    rows = slice(SLOT * j, SLOT * (j + 1))
                    ins = nc.vector.tensor_copy(qT[rows, 2:4, j], ps[rows, 2:4, 0:TOKENS])
                ins.then_inc(qkT_done, 1)

            every_t = sinks[:].unsqueeze(1).to_broadcast([TP, TT, HEADS])

            def peak_parts(n, own):
                dve.wait_ge(peaks_read, n * HEADS + HEADS)
                own.done(nc.vector.tensor_tensor(peak[:], peak[:], every_t, ALU.max))
                own.settle()
                own.done(nc.vector.tensor_scalar(npk_hi[:], peak[:], -1.0, None, ALU.mult))
                own.settle()
                own.done(nc.vector.scalar_tensor_tensor(npk_lo[:], peak[:], -1.0, npk_hi[:], ALU.mult, ALU.subtract))
                own.settle()
                nc.vector.tensor_copy(npk[:, :, :, 0:HEADS], npk_hi[:].unsqueeze(2).to_broadcast([TP, TT, GH, HEADS]))
                nc.vector.tensor_copy(npk[:, :, :, HEADS:2 * HEADS],
                                      npk_lo[:].unsqueeze(2).to_broadcast([TP, TT, GH, HEADS])).then_inc(npk_done, 1)
                own.done(nc.vector.tensor_tensor(sink_w[:], npk_hi[:], npk_lo[:], ALU.add))
                own.settle()
                nc.vector.tensor_tensor(sink_w[:], sink_w[:], every_t, ALU.add).then_inc(sink_arg, 1)

            def peaks_out(n):
                dve.wait_ge(npkT_psum, n + 1)
                nc.vector.tensor_copy(npkT[:], ps[0:GH * SLOT, 3, 0:TP].bitcast(BF16)).then_inc(npkT_done, 1)

            def attended(n, own):
                dve.wait_ge(y_back, n + 1)
                dve.wait_ge(sink_done, n + 1)
                o = ps[0:TP, 0:TT, 0:HEADS * SLOT].rearrange("p t (h s) -> p t h s", s=SLOT)
                own.done(nc.vector.tensor_tensor(den[:], o[:, :, :, HD], sink_w[:], ALU.add))
                own.settle()
                own.done(nc.vector.reciprocal(den[:], den[:]))
                own.settle()
                for t in range(TT):
                    ins = nc.vector.tensor_tensor(y[:, t].rearrange("p (h e) -> p h e", e=HD), o[:, t, :, 0:HD],
                                                  den[:, t].unsqueeze(2).to_broadcast([TP, HEADS, HD]), ALU.mult)
                ins.then_inc(y_done, 1)

            def add_residual(n):
                dve.wait_ge(out_psum, n + 1)
                nc.vector.tensor_tensor(H[:, n], H[:, n], ps[0:TP, 1, 0:TT * D], ALU.add).then_inc(h_added, 1)

            def col_peaks(n, q):
                dve.wait_ge(cols_psum, n * 4 + (q + 1))
                bank = ps[0:128, COLS[q % 2], 0:2 * TOKENS].rearrange("p (s t) -> p s t", s=2)
                nc.vector.tensor_reduce(max_q[:, q], bank.rearrange("p s t -> p t s"), AX_X, ALU.max)
                nc.vector.tensor_reduce(col_peak[:, q % 2], bank, AX_X, ALU.max, negate=True).then_inc(col_peaks_done, 1)

            def tokens_max(n):
                dve.wait_ge(col_peaks_done, n * 4 + 4)
                nc.vector.tensor_reduce(max_all[:], max_q[:].rearrange("p q t -> p t q"), AX_X, ALU.max).then_inc(max_all_done, 1)

            def slot_stats(n, q, own):
                dve.wait_ge(slots_psum, n * 4 + (q + 1))
                raw = ps[0:128, SUMS, 0:2 * (D + 1)].rearrange("p (s d) -> p s d", s=2)
                for s in range(2):
                    nc.vector.bn_stats(s_stats[:, s], raw[:, s, 0:D])
                own.done(nc.vector.tensor_copy(s_den[:], raw[:, :, D]))
                own.settle()
                own.done(nc.vector.tensor_tensor(s_den[:], s_den[:], s_den[:], ALU.mult))
                for s in range(2):
                    ins = nc.vector.bn_aggr(s_mv[:, s], s_stats[:, s])
                own.done(ins)
                own.settle()
                nc.vector.scalar_tensor_tensor(s_veps[:], s_den[:], LN_EPS, s_mv[:, :, 1], ALU.mult, ALU.add).then_inc(s_veps_done, 1)

            def slot_norm(n, q):
                dve.wait_ge(s_rstd_done, n * 4 + (q + 1))
                if q == 0:
                    dve.wait_ge(stored, n * 16 + 16)
                for s in range(2):
                    ins = nc.vector.tensor_scalar(slot_in[:, 2 * q + s], ps[0:128, SUMS, s * (D + 1):s * (D + 1) + D],
                                                  s_mv[:, s, 0:1], s_rstd[:, s:s + 1], ALU.subtract, ALU.mult)
                ins.then_inc(slots_done, 1)

            def layernorm(n, own):
                layernorm_dve(nc, dve, own, H, n, stats, mv, veps, veps_done)

            def normalise(n):
                dve.wait_ge(rstd_done, n + 1)
                normalise_dve(nc, H, n, mv, rstd, xn, xn_done)

            def d_layernorm(n, own):
                dve.wait_ge(h_added, n + 1)
                layernorm_dve(nc, dve, own, H, n, d_stats, d_mv, d_veps, d_veps_done)

            def d_normalise(n):
                dve.wait_ge(d_rstd_done, n + 1)
                normalise_dve(nc, H, n, d_mv, d_rstd, d_xn, d_xn_done)

            def rows_max(n):
                dve.wait_ge(maxT_psum, n + 1)
                nc.vector.tensor_reduce(neg_row_max[:, n], ps[0:TP, TURN, 0:TT * 128].rearrange("p (t s) -> p t s", t=TT),
                                        AX_X, ALU.max, negate=True)

            def body(m, n, f):
                A, B, C = m is not None, n is not None, f is not None
                if A: att = Steps(dve, att_steps, m * ATT_STEPS + prep.n)
                if B: dis = Steps(dve, dis_steps, n * DIS_STEPS)
                if C: front = Steps(dve, front_steps, f * FRONT_STEPS)
                if B: d_layernorm(n, dis)
                if B: d_normalise(n)
                if A: rotate(m, att)
                if B: col_peaks(n, 0)
                if A: qkT_half(m)
                if B: col_peaks(n, 1)
                if A: peaks(m, 0)
                if B: col_peaks(n, 2)
                if B: slot_stats(n, 0, dis)
                if A: peaks(m, 1)
                if B: slot_norm(n, 0)
                if A: peaks(m, 2)
                if A: peaks(m, 3)
                if A: peak_parts(m, att)
                if B: slot_stats(n, 1, dis)
                if A: peaks_out(m)
                if B: slot_norm(n, 1)
                if B: col_peaks(n, 3)
                if B: tokens_max(n)
                if B: slot_stats(n, 2, dis)
                if C: layernorm(f, front)
                if B: slot_norm(n, 2)
                if C: normalise(f)
                if B: rows_max(n)
                if A: attended(m, att)
                if B: slot_stats(n, 3, dis)
                if B: slot_norm(n, 3)
                if A: add_residual(m)
                assert (not A or att.n == ATT_STEPS) and (not B or dis.n == DIS_STEPS) and (not C or front.n == FRONT_STEPS)

            body(None, None, 0)
            body(FIRST, None, 1)
            with dve.Fori(0, IMAGES - 2) as n:
                body(n + 1, n, n + 2)
            body(IMAGES - 1, IMAGES - 2, None)
            body(None, IMAGES - 1, None)


SOFT_EXPERTS = 64
ROWS = 128 * ST
HALF = ROWS // 2
HID = 2 * D
HC = HID // 128


def experts_stage(nc, a, ident, slots_dram, outs_dram):
    PAIRS_E = SOFT_EXPERTS // 2
    with ExitStack() as ctx:
        st = Stage(nc, ctx, "exp")
        sb, sem = st.sb, st.sem
        ps = ctx.enter_context(nc.psum_tensor("exp_psum", [128, 8, 512], F32))
        two = range(2)

        gain = sb("gain", [DP, SOFT_EXPERTS, DC])
        shift = sb("shift", [DP, SOFT_EXPERTS, DC])
        w_1 = [sb(f"w_1{b}", [DP + 1, DC, HID]) for b in two]
        w_2 = [sb(f"w_2{b}", [128, HC, D]) for b in two]
        b_2 = [sb(f"b_2{b}", [128, D]) for b in two]
        x = [sb(f"x{b}", [128, ST, D]) for b in two]
        xT = [[sb(f"xT{b}{h}", [DP + 1, DC, HALF]) for h in two] for b in two]
        hid = [sb(f"hid{h}", [128, HC, HALF]) for h in two]
        y = [sb(f"y{b}", [128, ST, D]) for b in two]

        ident_in = sem("ident_in")
        vectors_in = sem("vectors_in")
        loaded = [sem("loaded0"), sem("loaded1")]
        xT_psum = sem("xT_psum")
        xT_done = sem("xT_done")
        hid_psum = sem("hid_psum")
        hid_done = sem("hid_done")
        y_psum = sem("y_psum")
        y_done = sem("y_done")
        stored = [sem("stored0"), sem("stored1")]
        x_dram = slots_dram.rearrange("(e r) n f -> e (r n) f", r=2)
        y_dram = outs_dram.rearrange("(e r) n f -> e (r n) f", r=2)
        block = ctx.enter_context(nc.Block())

        @block.sync
        def _(sp):
            sp.dma_start(ident[:], a["ident"]).then_inc(ident_in, 16)
            sp.dma_start(gain[:], a["ln_g"]).then_inc(vectors_in, 16)
            sp.dma_start(shift[:], a["ln_b"]).then_inc(vectors_in, 16)

            def load(b, e):
                sp.dma_start(x[b][:].rearrange("p j d -> p (j d)"),
                             x_dram[e]).then_inc(loaded[b], 16)
                sp.dma_start(w_1[b][0:DP], a["soft_w1"][e]).then_inc(loaded[b], 16)
                sp.dma_start(w_1[b][DP:DP + 1, 0], a["soft_b1"][e]).then_inc(loaded[b], 16)
                sp.dma_start(w_2[b][:], a["soft_w2"][e]).then_inc(loaded[b], 16)
                sp.dma_start(b_2[b][:], a["soft_b2"][e].partition_broadcast(128).rearrange("p o d -> p (o d)"))\
                  .then_inc(loaded[b], 16)

            for b in two:
                load(b, b)
            def store(b, i):
                sp.wait_ge(y_done, i * 4 + (2 * b + 3))
                sp.dma_start(y_dram[i * 2 + b], y[b][:].rearrange("p j d -> p (j d)")).then_inc(stored[b], 16)

            with sp.Fori(0, PAIRS_E - 1) as i:
                for b in two:
                    store(b, i)
                    load(b, i * 2 + (b + 2))
            for b in two:
                store(b, PAIRS_E - 1)
                sp.wait_ge(stored[b], 16 * PAIRS_E + 16)

        @block.tensor
        def _(pe):
            def turn(b, h, k):
                if h == 0:
                    pe.wait_ge(loaded[b], (k - 2 * b) * 20 + 80)
                if not (isinstance(k, int) and k == 0):
                    pe.wait_ge(xT_done, k)
                for c in range(DC):
                    for j in range(4):
                        mm = nc.tensor.transpose(ps[0:DP, c, j * 128:(j + 1) * 128], x[b][:, 4 * h + j, c * DP:(c + 1) * DP], ident[:])
                mm.then_inc(xT_psum, 1)

            def hidden(b, h, k):
                pe.wait_ge(xT_done, k + 1)
                for m in range(HC):
                    pe.wait_ge(hid_done, k * HC + (m + 1))
                    for c in range(DC):
                        K = DP + 1 - c
                        mm = nc.tensor.matmul(ps[0:128, 2 + m], w_1[b][0:K, c, m * 128:(m + 1) * 128], xT[b][h][0:K, c],
                                              start=c == 0, stop=c == 1)
                    mm.then_inc(hid_psum, 1)

            def output(b, h, k):
                pe.wait_ge(hid_done, k * HC + 2 * HC)
                pe.wait_ge(y_done, k + 1)
                for j in range(4):
                    for m in range(HC):
                        mm = nc.tensor.matmul(ps[0:128, 5 + j // 2, (j % 2) * D:(j % 2 + 1) * D],
                                              hid[h][:, m, j * 128:(j + 1) * 128], w_2[b][:, m], start=m == 0, stop=m == HC - 1)
                mm.then_inc(y_psum, 1)

            def pair(i, last):
                for b in two:
                    k = i * 4 + 2 * b
                    turn(b, 1, k + 1)
                    hidden(b, 0, k)
                    hidden(b, 1, k + 1)
                    output(b, 0, k)
                    if not (last and b == 1):
                        turn(1 - b, 0, k + 2)
                    output(b, 1, k + 1)

            pe.wait_ge(ident_in, 16)
            turn(0, 0, 0)
            with pe.Fori(0, PAIRS_E - 1) as i:
                pair(i, False)
            pair(PAIRS_E - 1, True)

        @block.scalar
        def _(act):
            act.sem_inc(hid_done, HC)
            with act.Fori(0, PAIRS_E) as i:
                for b in two:
                    for h in two:
                        for m in range(HC):
                            act.wait_ge(hid_psum, i * (4 * HC) + ((2 * b + h) * HC + m + 1))
                            nc.scalar.activation(hid[h][:, m], ps[0:128, 2 + m], ACT.Gelu)\
                              .then_inc(hid_done, 1)

        @block.vector
        def _(dve):
            def take_xT(b, h, e, k):
                dve.wait_ge(xT_psum, k + 1)
                for c in range(DC):
                    ins = nc.vector.tensor_scalar(xT[b][h][0:DP, c], ps[0:DP, c], gain[:, e, c:c + 1], shift[:, e, c:c + 1], ALU.mult, ALU.add)
                ins.then_inc(xT_done, 1)

            def take_y(b, h, i, k):
                dve.wait_ge(y_psum, k + 1)
                if h == 0:
                    dve.wait_ge(stored[b], i * 16 + 16)
                for s in range(2):
                    ins = nc.vector.tensor_tensor(y[b][:, 4 * h + 2 * s:4 * h + 2 * s + 2],
                                                  ps[0:128, 5 + s, 0:2 * D].rearrange("p (j d) -> p j d", j=2),
                                                  b_2[b][:].unsqueeze(1).to_broadcast([128, 2, D]), ALU.add)
                ins.then_inc(y_done, 1)

            def pair(i, last):
                for b in two:
                    k = i * 4 + 2 * b
                    take_xT(b, 1, i * 2 + b, k + 1)
                    take_y(b, 0, i, k)
                    if not (last and b == 1):
                        take_xT(1 - b, 0, i * 2 + (b + 1), k + 2)
                    take_y(b, 1, i, k + 1)

            dve.wait_ge(vectors_in, 32)
            for b in two:
                for h in two:
                    nc.vector.memset(xT[b][h][DP:DP + 1], 1.0)
            dve.sem_inc(y_done, 1)
            dve.sem_inc(stored[0], 16)
            dve.sem_inc(stored[1], 16)
            take_xT(0, 0, 0, 0)
            with dve.Fori(0, PAIRS_E - 1) as i:
                pair(i, False)
            pair(PAIRS_E - 1, True)


def combine_stage(nc, a, H, ident, phi, neg_row_max, outs_dram, out):
    FRONT_STEPS, END_STEPS = 8, 2
    with ExitStack() as ctx:
        st = Stage(nc, ctx, "com")
        sb, sem = st.sb, st.sem
        ps = ctx.enter_context(nc.psum_tensor("com_psum", [128, 8, 512], F32))
        two = range(2)

        mhalf = sb("mhalf", [TP, TT])
        ident_b = sb("ident_b", [TP, TP], BF16)
        ones = sb("ones", [2, 128], BF16)
        xn = [sb(f"xn{b}", [TP, TT, D]) for b in two]
        xnT = [sb(f"xnT{b}", [DP, DC, TOKENS]) for b in two]
        stats = [sb(f"stats{b}", [TP, TT, 6]) for b in two]
        mv = [sb(f"mv{b}", [TP, TT, 2]) for b in two]
        veps = [sb(f"veps{b}", [TP, TT]) for b in two]
        rstd = [sb(f"rstd{b}", [TP, TT]) for b in two]
        parts = [sb(f"parts{b}", [TP, TT, 2], BF16) for b in two]
        row = [sb(f"row{b}", [2, TOKENS], BF16) for b in two]
        weights = [[sb(f"weights{b}{q}", [128, 2, TOKENS]) for q in two] for b in two]
        y = [sb(f"y{b}", [128, ST, D + 1]) for b in two]
        rden = [sb(f"rden{b}", [TP, TT]) for b in two]
        res = [sb(f"res{b}", [TP, TT, D]) for b in two]

        consts_in = sem("consts_in")
        ready = sem("ready")
        y_in = [sem("y_in0"), sem("y_in1")]
        veps_done = sem("veps_done")
        rstd_done = sem("rstd_done")
        xn_done = sem("xn_done")
        parts_done = sem("parts_done")
        xnT_psum = sem("xnT_psum")
        xnT_done = sem("xnT_done")
        row_psum = sem("row_psum")
        row_done = sem("row_done")
        shifted_psum = sem("shifted_psum")
        exp_done = sem("exp_done")
        mixed = sem("mixed")
        res_done = sem("res_done")
        stored = [sem("stored0"), sem("stored1")]
        front_steps = sem("front_steps")
        end_steps = sem("end_steps")
        block = ctx.enter_context(nc.Block())

        @block.sync
        def _(sp):
            sp.dma_start(ident[:], a["ident"]).then_inc(consts_in, 16)
            sp.dma_start(mhalf[:], a["mhalf"][0:TP, 0:TT]).then_inc(consts_in, 16)

            def load(b, n):
                sp.dma_start(y[b][:, :, 0:D], outs_dram[:, n].rearrange("p (j d) -> p j d", j=ST)).then_inc(y_in[b], 16)

            sp.wait_ge(ready, 1)
            for b in two:
                load(b, b)
            def store(b, i):
                sp.wait_ge(res_done, i * 2 + (b + 3))
                sp.dma_start(out[i * 2 + b].rearrange("(t p) d -> p t d", t=TT), res[b][:]).then_inc(stored[b], 16)

            with sp.Fori(0, PAIRS - 1) as i:
                for b in two:
                    sp.wait_ge(mixed, i * 2 + (b + 1))
                    load(b, i * 2 + (b + 2))
                for b in two:
                    store(b, i)
            for b in two:
                store(b, PAIRS - 1)
                sp.wait_ge(stored[b], 16 * PAIRS + 16)

        @block.gpsimd
        def _(pool):
            pool.wait_ge(consts_in, 32)
            with pool.Fori(0, PAIRS) as i:
                for b in two:
                    pool.wait_ge(veps_done, i * 2 + (b + 1))
                    nc.gpsimd.tensor_tensor(rstd[b][:], veps[b][:], mhalf[:], ALU.pow).then_inc(rstd_done, 1)

        @block.tensor
        def _(pe):
            def turn_x(i):
                for b in two:
                    pe.wait_ge(xn_done, i * 2 + (b + 1))
                    transposes_pe(nc, xn[b], ps[:, 4 * b + 3], ident, xnT_psum)

            def turn_parts(i):
                for b in two:
                    pe.wait_ge(xnT_done, i * 2 + (b + 1))
                    pe.wait_ge(parts_done, i * 2 + (b + 1))
                    for t in range(TT):
                        mm = nc.tensor.transpose(ps[0:2, 4 * b + 3, 0:TP].bitcast(BF16)[:, t * TP:(t + 1) * TP], parts[b][:, t], ident_b[:])
                    mm.then_inc(row_psum, 1)

            def logits(i, q):
                for b in two:
                    if q == 0:
                        pe.wait_ge(row_done, i * 2 + (b + 1))
                    for s in range(2):
                        j = 2 * q + s
                        o = ps[0:128, 4 * b + q % 2, s * TOKENS:(s + 1) * TOKENS]
                        for c in range(DC):
                            nc.tensor.matmul(o, phi[:, c, j * 128:(j + 1) * 128], xnT[b][:, c], start=c == 0, stop=False)
                        mm = nc.tensor.matmul(o, ones[:], row[b][:], start=False, stop=True)
                    mm.then_inc(shifted_psum, 1)

            def mix(i, q):
                for b in two:
                    pe.wait_ge(exp_done, i * 8 + (2 * q + b + 1))
                    if q == 0:
                        pe.wait_ge(y_in[b], i * 16 + 16)
                        pe.wait_ge(res_done, i * 2 + (b + 1))
                    for t in range(TT):
                        for s in range(2):
                            j = 2 * q + s
                            mm = nc.tensor.matmul(ps[0:TP, 4 * b + 2, t * (D + 1):(t + 1) * (D + 1)],
                                                  weights[b][q % 2][:, s, t * TP:(t + 1) * TP], y[b][:, j],
                                                  start=j == 0 and t == 0, stop=j == ST - 1, skip_group_check=True)
                    if q == QUARTERS - 1:
                        mm.then_inc(mixed, 1)

            def pair(i, following):
                logits(i, 0)
                logits(i, 1)
                mix(i, 0)
                logits(i, 2)
                mix(i, 1)
                logits(i, 3)
                if following is not None:
                    turn_x(following)
                mix(i, 2)
                if following is not None:
                    turn_parts(following)
                mix(i, 3)

            pe.wait_ge(ready, 1)
            turn_x(0)
            turn_parts(0)
            with pe.Fori(0, PAIRS - 1) as i:
                pair(i, i + 1)
            pair(PAIRS - 1, None)

        @block.scalar
        def _(act):
            def xnT_out(i):
                for b in two:
                    act.wait_ge(xnT_psum, i * 2 + (b + 1))
                    nc.scalar.copy(xnT[b][:].rearrange("p c t -> p (c t)"), ps[0:DP, 4 * b + 3, 0:DC * TOKENS]).then_inc(xnT_done, 1)

            def exps(i):
                for q in range(QUARTERS):
                    for b in two:
                        act.wait_ge(shifted_psum, i * 8 + (2 * q + b + 1))
                        nc.scalar.activation(weights[b][q % 2][:].rearrange("p s t -> p (s t)"),
                                             ps[0:128, 4 * b + q % 2, 0:2 * TOKENS], ACT.Exp).then_inc(exp_done, 1)

            xnT_out(0)
            with act.Fori(0, PAIRS - 1) as i:
                exps(i)
                xnT_out(i + 1)
            exps(PAIRS - 1)

        @block.vector
        def _(dve):
            dve.wait_ge(consts_in, 32)
            nc.vector.memset(ones[:], 1.0)
            nc.vector.tensor_copy(ident_b[:], ident[0:TP, 0:TP])
            nc.vector.memset(y[0][:], 1.0)
            nc.vector.memset(y[1][:], 1.0).then_inc(ready, 1)
            dve.sem_inc(res_done, 2)
            dve.sem_inc(stored[0], 16)
            dve.sem_inc(stored[1], 16)

            def front(i):
                own = Steps(dve, front_steps, i * FRONT_STEPS)
                for b in two:
                    layernorm_dve(nc, dve, own, H, i * 2 + b, stats[b], mv[b], veps[b], veps_done)
                for b in two:
                    own.done(nc.vector.tensor_copy(parts[b][:, :, 0], neg_row_max[:, i * 2 + b]))
                    own.settle()
                    nc.vector.tensor_tensor(parts[b][:, :, 1], neg_row_max[:, i * 2 + b], parts[b][:, :, 0], ALU.subtract)\
                      .then_inc(parts_done, 1)
                for b in two:
                    dve.wait_ge(rstd_done, i * 2 + (b + 1))
                    normalise_dve(nc, H, i * 2 + b, mv[b], rstd[b], xn[b], xn_done)
                assert own.n == FRONT_STEPS, own.n

            def rows_out(i):
                for b in two:
                    dve.wait_ge(row_psum, i * 2 + (b + 1))
                    nc.vector.tensor_copy(row[b][:], ps[0:2, 4 * b + 3, 0:TP].bitcast(BF16)).then_inc(row_done, 1)

            def results(i):
                own = Steps(dve, end_steps, i * END_STEPS)
                for b in two:
                    dve.wait_ge(mixed, i * 2 + (b + 1))
                    acc = ps[0:TP, 4 * b + 2, 0:TT * (D + 1)].rearrange("p (t d) -> p t d", t=TT)
                    own.done(nc.vector.reciprocal(rden[b][:], acc[:, :, D]))
                    own.settle()
                    dve.wait_ge(stored[b], i * 16 + 16)
                    for t in range(TT):
                        ins = nc.vector.scalar_tensor_tensor(res[b][:, t], acc[:, t, 0:D], rden[b][:, t:t + 1],
                                                             H[:, i * 2 + b, t * D:(t + 1) * D], ALU.mult, ALU.add)
                    ins.then_inc(res_done, 1)
                assert own.n == END_STEPS, own.n

            front(0)
            rows_out(0)
            with dve.Fori(0, PAIRS - 1) as i:
                front(i + 1)
                rows_out(i + 1)
                results(i)
            results(PAIRS - 1)


def build(nc, a, out):
    slots_dram = nc.dram_tensor("slots", (128, IMAGES, ST * D), F32, kind="Internal").ap()
    outs_dram = nc.dram_tensor("slot_outs", (128, IMAGES, ST * D), F32, kind="Internal").ap()
    with (
        nc.sbuf_tensor("h", [TP, IMAGES, TT * D], F32) as H,
        nc.sbuf_tensor("ident", [128, 128], F32) as ident,
        nc.sbuf_tensor("phi", [DP, DC, SLOTS], F32) as phi,
        nc.sbuf_tensor("neg_row_max", [TP, IMAGES, TT], F32) as neg_row_max,
    ):
        ttt_moe_stage(nc, a, H, ident)
        attention_dispatch_stage(nc, a, H, ident, phi, neg_row_max, slots_dram)
        experts_stage(nc, a, ident, slots_dram, outs_dram)
        combine_stage(nc, a, H, ident, phi, neg_row_max, outs_dram, out)


def laid_out(np, v):
    f = {k: np.asarray(x) for k, x in v.items()}
    c = np.ascontiguousarray

    def chunks(w):
        return c(w.reshape(DC, DP, *w.shape[1:]).swapaxes(0, 1))

    def row(x):
        return c(x.reshape(1, -1))

    x = f["x"].reshape(IMAGES, GRID, PATCH, GRID, PATCH).transpose(0, 2, 4, 1, 3)
    qkv = f["L0_attn_qkv_weight"].reshape(3, D, D)
    slots = 128 * 8
    phi = f["L1_ffn_phi"].reshape(128, 8, D).transpose(2, 1, 0).reshape(D, slots)
    return {
        "patches": c(x.reshape(IMAGES, 2, 128, TOKENS).transpose(0, 2, 1, 3)),
        "tok_wT": c(f["L0_tok_W"].T.reshape(2, 128, D).transpose(1, 0, 2)),
        "qkv": c(qkv.reshape(3, DC, DP, D).transpose(2, 0, 1, 3)),
        "qkv_T": c(qkv.transpose(0, 2, 1).reshape(3, DC, DP, D).transpose(2, 0, 1, 3)),
        "q_bias": row(f["L0_attn_q_bias"]),
        "q_bias_col": chunks(f["L0_attn_q_bias"]),
        "v_bias": row(f["L0_attn_v_bias"]),
        "lr_wT": chunks(f["L0_attn_ttt_lr_weight"].reshape(HEADS, D).T),
        "lr_bias": row(f["L0_attn_ttt_lr_bias"]),
        "proj_T": chunks(f["L0_attn_proj_weight"].T),
        "proj_bias": row(f["L0_attn_proj_bias"]),
        "ttt_gamma": row(f["L0_attn_ttt_norm_weight"]),
        "ttt_gamma_col": chunks(f["L0_attn_ttt_norm_weight"].reshape(D)),
        "ttt_beta": row(f["L0_attn_ttt_norm_bias"]),
        "ttt_beta_col": chunks(f["L0_attn_ttt_norm_bias"].reshape(D)),
        "W1": f["L0_attn_W1"],
        "b1": c(f["L0_attn_b1"].reshape(1, DC, DP)),
        "router_w": chunks(f["L0_ffn_router_w"]),
        "router_b": row(f["L0_ffn_router_b"]),
        "moe_w1": c(f["L0_ffn_w1"].reshape(4, DC, DP, D).transpose(2, 1, 0, 3)),
        "moe_b1": c(f["L0_ffn_b1"].reshape(1, 4, D)),
        "moe_w2": c(f["L0_ffn_w2"].reshape(4, DC, DP, D).transpose(2, 1, 0, 3)),
        "moe_b2": c(f["L0_ffn_b2"].reshape(1, 4, D)),
        "norm_scale": chunks(f["L1_attn_norm_scale"]),
        "norm_bias": chunks(f["L1_attn_norm_bias"]),
        "attn_w": chunks(f["L1_attn_W_attn"]),
        "attn_b": row(f["L1_attn_b_attn"]),
        "attn_pw": chunks(f["L1_attn_W_proj"]),
        "attn_pb": row(f["L1_attn_b_proj"]),
        "sinks": row(f["L1_attn_sinks"]),
        "rezero": row(f["L1_attn_rezero"]),
        "phi": chunks(phi),
        "ln_g": c(f["L1_ffn_ln_g"].reshape(64, DC, DP).transpose(2, 0, 1)),
        "ln_b": c(f["L1_ffn_ln_b"].reshape(64, DC, DP).transpose(2, 0, 1)),
        "soft_w1": c(f["L1_ffn_w1"].reshape(64, DC, DP, 2 * D).transpose(0, 2, 1, 3)),
        "soft_b1": f["L1_ffn_b1"].reshape(64, 1, 2 * D),
        "soft_w2": c(f["L1_ffn_w2"].reshape(64, 3, 128, D).transpose(0, 2, 1, 3)),
        "soft_b2": f["L1_ffn_b2"].reshape(64, 1, D),
    }


def constants(np):
    r = np.arange(DP + 1)
    head_mask = (r[:, None] // HD == r[None, :DP] // HD) | (r[:, None] == DP)
    ang = np.outer(np.arange(TOKENS), 1.0 / 10000.0 ** (np.arange(0, HD, 2, dtype=np.float32) / HD)).astype(np.float32)
    cos = np.repeat(np.cos(ang), 2, axis=1).reshape(TT, TP, HD).transpose(1, 0, 2)
    sin = np.stack([-np.sin(ang), np.sin(ang)], axis=2).reshape(TT, TP, HD).transpose(1, 0, 2)
    k, q = np.arange(TP)[:, None], np.arange(TP)[None, :]
    rows, heads = np.arange(96)[:, None], np.arange(HEADS)[None, :]
    head_sel = (rows // 32 == heads % 3) & ((rows % 32 == heads) | (rows % 32 == heads + HEADS))
    return {
        "ident": np.eye(128, dtype=np.float32),
        "head_mask": head_mask.astype(np.float32),
        "mhalf": np.full((128, 24), -0.5, np.float32),
        "rope_cos": np.ascontiguousarray(cos.astype(np.float32)),
        "rope_sin": np.ascontiguousarray(sin.astype(np.float32)),
        "head_sel": np.ascontiguousarray(np.repeat(head_sel[:, :, None], TP, axis=2).astype(np.float32)),
        "mask_kq": np.where(k > q, np.float32(-1e30), np.float32(0.0)).astype(np.float32),
        "mask_qk": np.where(q > k, np.float32(-1e30), np.float32(0.0)).astype(np.float32),
    }


def kernel(**inputs):
    import numpy as _np
    import concourse.bacc as _bacc
    from concourse import mybir as _mybir
    from concourse.bass_utils import run_bass_kernel_spmd as _run

    nc = _bacc.Bacc("TRN2", target_bir_lowering=False, num_devices=1)
    data, aps = {}, {}
    for name, array in {**laid_out(_np, inputs), **constants(_np)}.items():
        data[f"in_{name}"] = array
        aps[name] = nc.dram_tensor(f"in_{name}", array.shape, _mybir.dt.from_np(array.dtype), kind="ExternalInput").ap()
    out = nc.dram_tensor("out", (IMAGES, TOKENS, D), F32, kind="ExternalOutput").ap()
    build(nc, aps, out)
    r = _run(nc, [data], core_ids=[0])
    return r.results[0]["out"]
```
